# Optimizing a Trainium2 kernel written in Bass

```python
import numpy as np
import jax
import jax.numpy as jnp

def _softmax(x, axis=-1):
    return jax.nn.softmax(x, axis=axis)

def _gelu(x):
    return jax.nn.gelu(x, approximate=True)

def _silu(x):
    return jax.nn.silu(x)

def _sigmoid(x):
    return jax.nn.sigmoid(x)

def _layernorm(x, axis=-1, eps=1e-05):
    m = jnp.mean(x, axis=axis, keepdims=True)
    v = jnp.var(x, axis=axis, keepdims=True)
    return (x - m) / jnp.sqrt(v + eps)

def _scatter_add(tgt, idx, src, axis=0):
    return tgt.at[idx].add(src)

def _segment_sum(src, seg, n):
    return jax.ops.segment_sum(src, seg, n)
kernel_name = 'mk_audio_tower_d1_tok_audfeat256_r4_620835'

def setup_inputs(seed: int=0):
    np.random.seed(seed)
    _w = jnp.asarray

    def _rec_inputs():
        import jax
        import jax.numpy as jnp
        _rk = jax.random.key(seed)
        x = -7.10856e-05 + 0.999911 * jax.random.normal(jax.random.fold_in(_rk, 1), (128, 64, 750), jnp.float32)
        return x
    x = _rec_inputs()

    def _L0_tok_setup():
        import jax, jax.numpy as jnp
        import numpy as np
        KERNEL_SIZE = 8
        key = jax.random.key(seed)
        k1, k2 = jax.random.split(key)
        B, F, T = (16, 64, 4096)
        x = jax.random.normal(k1, (B, F, T), dtype=jnp.float32)
        w = jax.random.normal(k2, (1, F), dtype=jnp.float32) * 0.05
        b = jnp.zeros((1,), dtype=jnp.float32)
        return {'x': x, 'w': w, 'b': b}
    _L0_tok_all = _L0_tok_setup()
    _L0_tok_in = {k: v for k, v in _L0_tok_all.items() if k in ('w', 'b')}
    del _L0_tok_all

    def _L0_attn_setup():
        import jax, jax.numpy as jnp
        import numpy as np
        from math import sqrt
        DIM = 64
        key = jax.random.key(seed)
        k1, k2, k3, k4 = jax.random.split(key, 4)
        B, T, D, H, R = (2, 1024, DIM, 8, 32)

        def xavier(k, shape, fan_in, fan_out):
            a = sqrt(6.0 / (fan_in + fan_out))
            return jax.random.uniform(k, shape, jnp.float32, -a, a)
        x = jax.random.normal(k1, (B, T, D), jnp.float32)
        Q = xavier(k2, (H, R, D), D, R)
        K = xavier(k3, (H, R, D), D, R)
        VO = xavier(k4, (H, D, D), D, D)
        return {'x': x, 'Q': Q, 'K': K, 'VO': VO}
    _L0_attn_all = _L0_attn_setup()
    _L0_attn_in = {k: v for k, v in _L0_attn_all.items() if k in ('Q', 'K', 'VO')}
    del _L0_attn_all

    def _L0_ffn_setup():
        import jax, jax.numpy as jnp
        import numpy as np
        B, S, H, NH, NE = (4, 256, 64, 4, 4)
        D = H // NH
        EPS = 1e-08

        def layernorm(x, g, b):
            m = jnp.mean(x, axis=-1, keepdims=True)
            v = jnp.mean((x - m) ** 2, axis=-1, keepdims=True)
            return (x - m) / jnp.sqrt(v + EPS) * g + b
        key = jax.random.key(seed)
        ks = jax.random.split(key, 18)
        sc = 0.05
        return {'x': jax.random.normal(ks[0], (B, S, H), jnp.float32), 'hl_w': jax.random.normal(ks[1], (NH, D, H), jnp.float32) * sc, 'hl_b': jax.random.normal(ks[2], (NH, D), jnp.float32) * sc, 'wq': jax.random.normal(ks[3], (NH, NE, D, D), jnp.float32) * sc, 'wk': jax.random.normal(ks[4], (NH, D, D), jnp.float32) * sc, 'wv': jax.random.normal(ks[5], (NH, D, D), jnp.float32) * sc, 'gate_w': jax.random.normal(ks[6], (NH, NE, NE * D), jnp.float32) * sc, 'gate_b': jax.random.normal(ks[7], (NH, NE), jnp.float32) * sc, 'ln_g': jnp.ones((D,), jnp.float32), 'ln_b': jnp.zeros((D,), jnp.float32), 'fc1_w': jax.random.normal(ks[8], (D, D), jnp.float32) * sc, 'fc1_b': jax.random.normal(ks[9], (D,), jnp.float32) * sc, 'fc2_w': jax.random.normal(ks[10], (D, D), jnp.float32) * sc, 'fc2_b': jax.random.normal(ks[11], (D,), jnp.float32) * sc, 'fnorm_g': jnp.ones((D,), jnp.float32), 'fnorm_b': jnp.zeros((D,), jnp.float32), 'fgate_w': jax.random.normal(ks[12], (NH, H), jnp.float32) * sc}
    _L0_ffn_all = _L0_ffn_setup()
    _L0_ffn_in = {k: v for k, v in _L0_ffn_all.items() if k in ('hl_w', 'hl_b', 'wq', 'wk', 'wv', 'gate_w', 'gate_b', 'ln_g', 'ln_b', 'fc1_w', 'fc1_b', 'fc2_w', 'fc2_b', 'fnorm_g', 'fnorm_b', 'fgate_w')}
    del _L0_ffn_all
    return {'x': x, 'L0_tok_w': _L0_tok_in['w'], 'L0_tok_b': _L0_tok_in['b'], 'L0_attn_Q': _L0_attn_in['Q'], 'L0_attn_K': _L0_attn_in['K'], 'L0_attn_VO': _L0_attn_in['VO'], 'L0_ffn_hl_w': _L0_ffn_in['hl_w'], 'L0_ffn_hl_b': _L0_ffn_in['hl_b'], 'L0_ffn_wq': _L0_ffn_in['wq'], 'L0_ffn_wk': _L0_ffn_in['wk'], 'L0_ffn_wv': _L0_ffn_in['wv'], 'L0_ffn_gate_w': _L0_ffn_in['gate_w'], 'L0_ffn_gate_b': _L0_ffn_in['gate_b'], 'L0_ffn_ln_g': _L0_ffn_in['ln_g'], 'L0_ffn_ln_b': _L0_ffn_in['ln_b'], 'L0_ffn_fc1_w': _L0_ffn_in['fc1_w'], 'L0_ffn_fc1_b': _L0_ffn_in['fc1_b'], 'L0_ffn_fc2_w': _L0_ffn_in['fc2_w'], 'L0_ffn_fc2_b': _L0_ffn_in['fc2_b'], 'L0_ffn_fnorm_g': _L0_ffn_in['fnorm_g'], 'L0_ffn_fnorm_b': _L0_ffn_in['fnorm_b'], 'L0_ffn_fgate_w': _L0_ffn_in['fgate_w']}

def reference(x, L0_tok_w, L0_tok_b, L0_attn_Q, L0_attn_K, L0_attn_VO, L0_ffn_hl_w, L0_ffn_hl_b, L0_ffn_wq, L0_ffn_wk, L0_ffn_wv, L0_ffn_gate_w, L0_ffn_gate_b, L0_ffn_ln_g, L0_ffn_ln_b, L0_ffn_fc1_w, L0_ffn_fc1_b, L0_ffn_fc2_w, L0_ffn_fc2_b, L0_ffn_fnorm_g, L0_ffn_fnorm_b, L0_ffn_fgate_w):
    import jax
    import jax.numpy as jnp

    def _L0_tok_ref(x, w, b):
        import jax, jax.numpy as jnp
        import numpy as np
        KERNEL_SIZE = 8
        k = KERNEL_SIZE
        B, F, T = x.shape
        pad = -T % k
        if pad:
            x = jnp.pad(x, ((0, 0), (0, 0), (0, pad)))
            T += pad
        nw = T // k
        xp = x.reshape(B, F, nw, k).transpose(0, 2, 3, 1)
        scores = jnp.einsum('bwkf,of->bwko', xp, w) + b
        weights = jax.nn.softmax(scores, axis=2)
        pooled = jnp.sum(xp * weights, axis=2)
        return pooled

    def _L0_attn_ref(x, Q, K, VO):
        import jax, jax.numpy as jnp
        import numpy as np
        from math import sqrt
        DIM = 64
        d = x.shape[-1]
        q = jnp.einsum('btd,hrd->bhtr', x, Q)
        k = jnp.einsum('bud,hrd->bhur', x, K)
        scores = jnp.einsum('bhtr,bhur->bhtu', q, k) / sqrt(d)
        attn = jax.nn.softmax(scores, axis=-1)
        ctx = jnp.einsum('bhtu,bud->bhtd', attn, x)
        out = jnp.einsum('bhtd,hde->bte', ctx, VO)
        return out

    def _L0_ffn_ref(x, hl_w, hl_b, wq, wk, wv, gate_w, gate_b, ln_g, ln_b, fc1_w, fc1_b, fc2_w, fc2_b, fnorm_g, fnorm_b, fgate_w):
        import jax, jax.numpy as jnp
        import numpy as np
        B, S, H, NH, NE = (4, 256, 64, 4, 4)
        D = H // NH
        EPS = 1e-08

        def layernorm(x, g, b):
            m = jnp.mean(x, axis=-1, keepdims=True)
            v = jnp.mean((x - m) ** 2, axis=-1, keepdims=True)
            return (x - m) / jnp.sqrt(v + EPS) * g + b
        b, s, h = x.shape
        nh, d, _ = wk.shape
        ne = wq.shape[1]
        sx = jnp.einsum('bsh,ndh->bnsd', x, hl_w) + hl_b[None, :, None, :]
        pad = sx == 0
        q = jnp.einsum('bnsd,neod->bneso', sx, wq)
        k = jnp.einsum('bnsd,nod->bnso', sx, wk)
        v = jnp.einsum('bnsd,nod->bnso', sx, wv)
        causal = jnp.where(jnp.tril(jnp.ones((s, s), bool)), 0.0, -jnp.inf).astype(x.dtype)
        scores = jnp.einsum('bnesd,bntd->bnest', q, k) * d ** 0.5 + causal
        att = jax.nn.softmax(scores, axis=-1)
        qkv = jnp.einsum('bnest,bntd->bnesd', att, v)
        qkv = jnp.where(pad[:, :, None], 0.0, qkv)
        out = jnp.transpose(qkv, (0, 1, 3, 2, 4)).reshape(b, nh, s, ne * d)
        gs = jax.nn.softmax(jnp.einsum('bnsf,nef->bnse', out, gate_w) + gate_b[None, :, None, :], axis=-1)
        mixed = jnp.einsum('bnsed,bnse->bnsd', out.reshape(b, nh, s, ne, d), gs)
        resid = sx[jnp.arange(nh), jnp.arange(nh)]
        hn = layernorm(mixed + resid, ln_g, ln_b)
        f_n = jnp.transpose(hn, (0, 2, 1, 3)).reshape(b, s, h)
        fx = f_n.reshape(b, s, nh, d)
        pm = fx == 0
        hx = jnp.where(pm, 0.0, fx @ fc1_w.T + fc1_b)
        hx = jax.nn.relu(hx)
        hx = jnp.where(pm, 0.0, hx @ fc2_w.T + fc2_b)
        hx = layernorm(hx + fx, fnorm_g, fnorm_b)
        fout = hx.reshape(b, s, h)
        fg = jax.nn.softmax(fout @ fgate_w.T, axis=-1)
        return (fout.reshape(b, s, nh, d) * fg[..., None]).reshape(b, s, h)
    h = _L0_tok_ref(x, L0_tok_w, L0_tok_b)
    h = h + _L0_attn_ref(_layernorm(h, axis=-1), L0_attn_Q, L0_attn_K, L0_attn_VO)
    h = h + _L0_ffn_ref(_layernorm(h, axis=-1), L0_ffn_hl_w, L0_ffn_hl_b, L0_ffn_wq, L0_ffn_wk, L0_ffn_wv, L0_ffn_gate_w, L0_ffn_gate_b, L0_ffn_ln_g, L0_ffn_ln_b, L0_ffn_fc1_w, L0_ffn_fc1_b, L0_ffn_fc2_w, L0_ffn_fc2_b, L0_ffn_fnorm_g, L0_ffn_fnorm_b, L0_ffn_fgate_w)
    return h

_drawn_inputs = setup_inputs


def setup_inputs(seed=0):
    import zlib

    import numpy as np

    out = dict(_drawn_inputs(seed))
    spreads = {'L0_ffn_ln_g': (1.0, 0.2),
     'L0_ffn_ln_b': (0.0, 0.1),
     'L0_ffn_fnorm_g': (1.0, 0.2),
     'L0_ffn_fnorm_b': (0.0, 0.1)}
    factors = {'L0_ffn_wq': 8.0,
     'L0_ffn_wk': 8.0,
     'L0_ffn_gate_w': 64.0,
     'L0_ffn_gate_b': 51.862,
     'L0_ffn_fc1_w': 5.94,
     'L0_ffn_fc1_b': 8.0,
     'L0_ffn_fc2_w': 4.222,
     'L0_ffn_fc2_b': 2.848}
    for name, (base, spread) in spreads.items():
        noise = np.random.default_rng([zlib.crc32(name.encode()), seed]).standard_normal(out[name].shape)
        drawn = base * np.exp(spread * noise) if base else spread * noise
        out[name] = jnp.asarray(drawn.astype(out[name].dtype))
    for name, factor in factors.items():
        out[name] = (out[name] * factor).astype(out[name].dtype)
    return out
```

```python
from contextlib import ExitStack

import concourse.bass as bass
from concourse import mybir

F32 = mybir.dt.float32
BF16 = mybir.dt.bfloat16
ALU = mybir.AluOpType
ACT = mybir.ActivationFunctionType
AX = mybir.AxisListType

NBATCH, NFEAT, NTIME = 128, 64, 750
KW = 8
NTOK = -(-NTIME // KW)
TP = 96
HEADS, RANK = 8, 32
NH, NE, HD = 4, 4, 16
QB = 32
WIDTH = [QB, 2 * QB, NTOK]
START = [0, QB, 3 * QB]
SROW = START[2] + NTOK
EPS_LN, EPS_FF = 1e-5, 1e-8
MASKED = -1.0e30
FF_LOADS = 16 * (5 * NH + 4 + NH + 6)


def positive(v):
    return not isinstance(v, int) or v > 0


def exists(m, total):
    return not isinstance(m, int) or 0 <= m < total


def bcast(ap, axis, n):
    ap = ap.unsqueeze(axis)
    shape = list(ap.shape)
    shape[axis] = n
    return ap.broadcast_to(shape)


def audio_tower(nc, x, tok_w, tok_b, attn_q, attn_k, attn_vo, hl_w, hl_b, wq, wk, wv, gate_w, gate_b,
                ln_g, ln_b, fc1_w, fc1_b, fc2_w, fc2_b, fnorm_g, fnorm_b, fgate_w, out):
    with ExitStack() as ctx:
        def sb(name, shape, dt=F32):
            return ctx.enter_context(nc.sbuf_tensor(name, shape, dt))

        def sem(name):
            return ctx.enter_context(nc.semaphore(name))

        psum = ctx.enter_context(nc.psum_tensor("psum", [128, 8, 512], F32))

        ident_w = sb("ident_w", [128, 130])
        ident = ident_w[:, 0:128]
        neg_half = sb("neg_half", [TP, 16])
        tokb = sb("tokb", [TP, 1])
        q_w = sb("q_w", [RANK, HEADS, NFEAT])
        k_w = sb("k_w", [RANK, HEADS, NFEAT])
        g_w = sb("g_w", [128, HEADS * NFEAT])
        vo_w = sb("vo_w", [128, HEADS // 2, NFEAT])

        h = sb("h", [TP, NBATCH, NFEAT])

        zeroed = sem("zeroed")
        zeroed2 = sem("zeroed2")
        zeroed3 = sem("zeroed3")
        zeroed4 = sem("zeroed4")
        pool_own = sem("pool_own")
        consts_ready = sem("consts_ready")
        tok_loaded = sem("tok_loaded")
        attn_loaded = sem("attn_loaded")

        NPAIR = NBATCH // 2
        V1 = 4
        xs = sb("xs", [128, V1, NTOK * KW])
        tok_s = sb("tok_s", [TP, 2, 2 * KW])
        tok_m = sb("tok_m", [TP, 2, 2])
        tok_d = sb("tok_d", [TP, 2, 2 * KW])
        tok_e = sb("tok_e", [TP, 2, 2 * KW])
        tok_l = sb("tok_l", [TP, 2, 2])
        tok_r = sb("tok_r", [TP, 2, 2])
        xw = sb("xw", [TP, 2, KW, 128])
        x_loaded = [sem(f"x_loaded{i}") for i in range(V1)]
        x_turned = sem("x_turned")
        tok_scored = sem("tok_scored")
        tok_maxed = sem("tok_maxed")
        tok_shifted = sem("tok_shifted")
        tok_exped = sem("tok_exped")
        tok_summed = sem("tok_summed")
        tok_inverted = sem("tok_inverted")
        x_weighted = sem("x_weighted")
        x_fold = [sem(f"x_fold{i}") for i in range(3)]
        h_pooled = sem("h_pooled")

        x_pairs = x.rearrange("(p two) f t -> p (two f) t", two=2)

        def turned(v2):
            return psum[0:NTOK, 4 * v2:4 * v2 + 4, :].rearrange("p a (two c) -> p (a two) c", two=2)

        V2 = 8
        NQUAD = NBATCH // 4
        HP = HEADS // 2
        NT = 3
        ln_bn = sb("ln_bn", [TP, 4, 6])
        ln_mv = sb("ln_mv", [TP, 4, 2])
        ln_ve = sb("ln_ve", [TP, 4])
        ln_rs = sb("ln_rs", [TP, 4])
        spot = sb("spot", [1, 1])
        xn = sb("xn", [TP, 2, 4, 2, NFEAT])
        xT = sb("xT", [128, 2, 4, 2, NTOK])
        qs = sb("qs", [128, 2, 4, HP, TP])
        mx = sb("mx", [128, 2, NT, 2])
        pl = sb("pl", [128, 2, NT, 2])
        pr = sb("pr", [128, 2, NT, 2])
        pu = sb("pu", [128, 4, NT, 2, NTOK])
        pT = sb("pT", [NTOK, 2, HP * TP])
        cT = sb("cT", [128, 2, HP, TP])
        ln_stat = sem("ln_stat")
        ln_agg = sem("ln_agg")
        ln_var = sem("ln_var")
        ln_rstd = sem("ln_rstd")
        ln_done = sem("ln_done")
        at_turned = sem("at_turned")
        at_xT = sem("at_xT")
        at_projected = sem("at_projected")
        at_q = [sem(f"at_q{i}") for i in range(2)]
        at_scored = sem("at_scored")
        at_maxed = sem("at_maxed")
        at_shifted = sem("at_shifted")
        at_exped = sem("at_exped")
        at_summed = sem("at_summed")
        at_inverted = sem("at_inverted")
        at_normed = sem("at_normed")
        at_pturned = sem("at_pturned")
        at_pT = sem("at_pT")
        at_mixed = sem("at_mixed")
        at_cT = sem("at_cT")
        at_out = sem("at_out")
        at_added = sem("at_added")
        g_made = sem("g_made")
        g_ready = sem("g_ready")

        at_Q = psum[:, 0, 0:4 * TP].rearrange("p (b t) -> p b t", b=4)

        def at_S(v):
            s = psum[:, 1 + 2 * (v % 2):3 + 2 * (v % 2), :].rearrange("p a (two c) -> p (a two) c", two=2)
            return s[:, 0:NT, 0:2 * NTOK]

        at_P = psum[0:NTOK, 5, 0:NT * 128]
        at_C = psum[:, 6, 0:HP * TP]
        at_O = psum[0:TP, 7, 0:NFEAT]

        NJ = 3
        whl = sb("whl", [HD, NH, NFEAT + 1])
        wq_s = sb("wq_s", [HD, NH, NE, HD])
        wk_s = sb("wk_s", [HD, NH, HD])
        wvT = sb("wvT", [HD, NH, HD])
        m_s = sb("m_s", [HD, NH, NE, HD])
        aq = sb("aq", [NFEAT + 1, NE, NH, 32])
        wsx = sb("wsx", [NFEAT + 1, NH, 32])
        wtok = sb("wtok", [NFEAT + 1, 2, NH, HD])
        gT = sb("gT", [128, 2, NH * NE])
        gbb = sb("gbb", [TP, NH * NE])
        gam = sb("gam", [TP, 2, HD])
        bet = sb("bet", [TP, 2, HD])
        fc1 = sb("fc1", [NFEAT, 128])
        b1 = sb("b1", [NFEAT, 1])
        fc2 = sb("fc2", [NFEAT + 1, NFEAT])
        fgT = sb("fgT", [NFEAT, NH])
        causA = sb("causA", [QB, NE * QB], BF16)
        causB = sb("causB", [QB, NH, QB], BF16)
        xn3 = sb("xn3", [TP, 4, NFEAT])
        x3T = sb("x3T", [NFEAT + 1, 4, TP])
        sxd = sb("sxd", [128, 2, 4, NH, NTOK])
        q3 = sb("q3", [128, 2, 4, NJ, NE, QB])
        va = sb("va", [TP, 2, 4, NH, HD + 1])
        nz = sb("nz", [TP, 2, 4, NH, HD])
        resid = sb("resid", [TP, NH, HD])
        mx3 = sb("mx3", [128, 2, NJ, NH])
        pu3 = sb("pu3", [128, 2, NH, NJ, NTOK])
        pT3 = sb("pT3", [NTOK, NH, NE, NJ, QB])
        r3 = sb("r3", [TP, 2, NH * NE])
        o3 = sb("o3", [TP, 2, 4, NH, NE, HD])
        oT = sb("oT", [128, 2, 4, TP])
        gl = sb("gl", [TP, 2, 64])
        ge = sb("ge", [TP, 2, 64])
        gm = sb("gm", [TP, 2, 16])
        gs = sb("gs", [TP, 2, 16])
        gr = sb("gr", [TP, 2, 16])
        yy = sb("yy", [TP, 2, 256])
        st = sb("st", [TP, 2, 2, 4, 16])
        yc = sb("yc", [TP, 2, 256])
        ysq = sb("ysq", [TP, 2, 256])
        fx = sb("fx", [TP, 2, 256])
        fxT = sb("fxT", [NFEAT, 2, 4 * TP])
        hx = sb("hx", [NFEAT, 2, 4 * TP])
        hxm = sb("hxm", [NFEAT + 1, 2, 4 * TP])
        ft = sb("ft", [TP, 2, 256])
        fo = sb("fo", [TP, 2, 256])
        foT = sb("foT", [NFEAT, 2, 4 * TP])
        fl = sb("fl", [TP, 2, 16])
        fe = sb("fe", [TP, 2, 16])
        fm = sb("fm", [TP, 2, 4])
        fs = sb("fs", [TP, 2, 4])
        fr = sb("fr", [TP, 2, 4])
        ho = sb("ho", [TP, 2, 256])
        names3 = """ff_loaded w_made w_read ln3_stat ln3_agg ln3_var ln3_rstd ln3_done f_turned f_xT f_sx f_diagA f_diagV
            f_tok f_va f_q f_qA f_qV f_resid s_scored s_maxed s_shifted s_exped p_turned p_copied p_mixed c_inv c_normed
            c_guarded r0_turned r0_copied r0_gated g_added g_maxed g_shifted g_exped g_summed g_inv g_gs g_mul g_f1 g_f2
            y_made y_sum y_cent y_sq y_var y_eps y_rstd y_mul y_gam fx_made r1_fxt r1_fxc r1_fc1 r1_hx h_masked r1_fc2 t_made z_made
            z_sum z_cent z_sq z_var z_eps z_rstd z_mul z_gam fo_made r1_fot r1_foc r1_fl fl_maxed fl_shifted fl_exped
            fl_summed fl_inv fl_w fo_mul ho_made causal_set"""
        S = {n: sem(n) for n in names3.split()}
        (ff_loaded, w_made, w_read, ln3_stat, ln3_agg, ln3_var, ln3_rstd, ln3_done, f_turned, f_xT, f_sx, f_diagA, f_diagV,
         f_tok, f_va, f_q, f_qA, f_qV, f_resid, s_scored, s_maxed, s_shifted, s_exped, p_turned, p_copied, p_mixed, c_inv, c_normed,
         c_guarded, r0_turned, r0_copied, r0_gated, g_added, g_maxed, g_shifted, g_exped, g_summed, g_inv, g_gs, g_mul, g_f1, g_f2,
         y_made, y_sum, y_cent, y_sq, y_var, y_eps, y_rstd, y_mul, y_gam, fx_made, r1_fxt, r1_fxc, r1_fc1, r1_hx, h_masked, r1_fc2, t_made, z_made,
         z_sum, z_cent, z_sq, z_var, z_eps, z_rstd, z_mul, z_gam, fo_made, r1_fot, r1_foc, r1_fl, fl_maxed, fl_shifted, fl_exped,
         fl_summed, fl_inv, fl_w, fo_mul, ho_made, causal_set) = S.values()
        out_done = [sem("out_done0"), sem("out_done1")]

        F_ = psum[:, 0, :]
        SJ = [psum[:, 2, NH * WIDTH[1]:NH * (WIDTH[1] + WIDTH[0])].rearrange("p (n u) -> p n u", n=NH),
              psum[:, 2, 0:NH * WIDTH[1]].rearrange("p (n u) -> p n u", n=NH),
              psum[:, 1, 0:NH * WIDTH[2]].rearrange("p (n u) -> p n u", n=NH)]
        C3 = psum[0:TP, 5, 0:NH * NE * (HD + 1)].rearrange("p (a c) -> p a c", c=HD + 1)
        R0, R1 = psum[:, 6, :], psum[:, 7, :]

        def P3(n):
            return psum[0:NTOK, 3 + n % 2, 0:NJ * 128]
        out_stored = sem("out_stored")
        block = ctx.enter_context(nc.Block())

        @block.sync
        def _(sp):
            def load(q, pairs):
                for v in range(V1):
                    if positive(V1 * (q - 1) + v + 1):
                        sp.wait_ge(x_turned, V1 * (q - 1) + v + 1)
                    sp.dma_start(xs[:, v, 0:NTIME], pairs(v)).then_inc(x_loaded[v], 16)

            load(0, lambda v: x_pairs[v])
            with sp.Fori(1, NPAIR // V1) as q:
                load(q, lambda v: x_pairs[bass.ds(q * V1 + v, 1)].rearrange("o q t -> (o q) t"))

            def store(g, g2, quad):
                sp.wait_ge(ho_made, g + 1)
                sp.dma_start(quad.rearrange("b t f -> t b f"),
                             ho[0:NTOK, g2, :].rearrange("t (b f) -> t b f", b=4)).then_inc(out_done[g2], 16)

            with sp.Fori(0, NQUAD // 2) as q:
                for g2 in range(2):
                    store(2 * q + g2, g2, out[bass.ds(8 * q + 4 * g2, 4)])
            for g2 in range(2):
                sp.wait_ge(out_done[g2], 16 * NQUAD // 2)

        @block.gpsimd
        def _(pool):
            pool.memset(ident_w[:, :], 0.0).then_inc(zeroed, 1)
            pool.memset(neg_half[:, :], -0.5).then_inc(zeroed, 1)
            pool.memset(xs[:, :, NTIME:NTOK * KW], 0.0).then_inc(zeroed, 1)
            pool.wait_ge(zeroed, 3)
            pool.dma_start(ident_w[0:NFEAT, 128:129], tok_w.rearrange("o f -> f o")).then_inc(tok_loaded, 16)
            pool.dma_start(ident_w[NFEAT:128, 129:130], tok_w.rearrange("o f -> f o")).then_inc(tok_loaded, 16)
            pool.dma_start(tokb[:, :], tok_b.partition_broadcast(TP)).then_inc(tok_loaded, 16)
            pool.dma_start(q_w[:, :, :], attn_q.rearrange("h r d -> r h d")).then_inc(attn_loaded, 16)
            pool.dma_start(k_w[:, :, :], attn_k.rearrange("h r d -> r h d")).then_inc(attn_loaded, 16)
            for par in range(2):
                pool.dma_start(vo_w[64 * par:64 * par + 64, :, :],
                               attn_vo.rearrange("(hp par) d e -> par d hp e", par=2)[par]).then_inc(attn_loaded, 16)
            pool.affine_select(out=ident, in_=ident, compare_op=ALU.not_equal, fill=1.0,
                               base=0, pattern=[[-1, 128]], channel_multiplier=1).then_inc(pool_own, 1)
            pool.wait_ge(pool_own, 1)
            pool.memset(h[64:TP, :, :], 0.0).then_inc(zeroed2, 1)
            pool.wait_ge(zeroed2, 4)

            pool.wait_ge(zeroed3, 5)
            for n in range(NH):
                rows = slice(HD * n, HD * n + HD)
                pool.dma_start(fc1[rows, rows], fc1_w.rearrange("o i -> i o"), allow_slow_non_contiguous=True).then_inc(ff_loaded, 16)
                pool.dma_start(fc2[rows, rows], fc2_w.rearrange("o i -> i o"), allow_slow_non_contiguous=True).then_inc(ff_loaded, 16)
                pool.dma_start(fc2[NFEAT:NFEAT + 1, rows], fc2_b.rearrange("(o i) -> o i", o=1), allow_slow_non_contiguous=True).then_inc(ff_loaded, 16)
                pool.dma_start(b1[rows, :], fc1_b.rearrange("(i o) -> i o", o=1), allow_slow_non_contiguous=True).then_inc(ff_loaded, 16)
                pool.dma_start(gT[64 * (n % 2):64 * (n % 2) + 64, n // 2, NE * n:NE * n + NE],
                               gate_w[n].rearrange("e f -> f e"), allow_slow_non_contiguous=True).then_inc(ff_loaded, 16)
            pool.dma_start(whl[:, :, 0:NFEAT], hl_w.rearrange("n d h -> d n h"), allow_slow_non_contiguous=True).then_inc(ff_loaded, 16)
            pool.dma_start(whl[:, :, NFEAT], hl_b.rearrange("n d -> d n"), allow_slow_non_contiguous=True).then_inc(ff_loaded, 16)
            pool.dma_start(wq_s[:, :, :, :], wq.rearrange("n e o d -> o n e d"), allow_slow_non_contiguous=True).then_inc(ff_loaded, 16)
            pool.dma_start(wk_s[:, :, :], wk.rearrange("n o d -> o n d"), allow_slow_non_contiguous=True).then_inc(ff_loaded, 16)
            for n in range(NH):
                pool.dma_start(wvT[:, n, :], wv[n].rearrange("o d -> d o"), allow_slow_non_contiguous=True).then_inc(ff_loaded, 16)
            pool.dma_start(gbb[:, :], gate_b.rearrange("n e -> (n e)").partition_broadcast(TP), allow_slow_non_contiguous=True).then_inc(ff_loaded, 16)
            pool.dma_start(gam[:, 0, :], ln_g.partition_broadcast(TP)).then_inc(ff_loaded, 16)
            pool.dma_start(bet[:, 0, :], ln_b.partition_broadcast(TP)).then_inc(ff_loaded, 16)
            pool.dma_start(gam[:, 1, :], fnorm_g.partition_broadcast(TP)).then_inc(ff_loaded, 16)
            pool.dma_start(bet[:, 1, :], fnorm_b.partition_broadcast(TP)).then_inc(ff_loaded, 16)
            pool.dma_start(fgT[:, :], fgate_w.rearrange("n f -> f n"), allow_slow_non_contiguous=True).then_inc(ff_loaded, 16)
            pool.memset(causA[:, :], 0.0).then_inc(causal_set, 1)
            pool.memset(causB[:, :, :], 0.0).then_inc(causal_set, 1)
            pool.wait_ge(causal_set, 2)
            cA = causA[:, :].rearrange("p (e t) -> p e t", e=NE)
            pool.affine_select(out=cA, in_=cA, compare_op=ALU.not_equal, fill=1.0, base=0,
                               pattern=[[0, NE], [-1, QB]], channel_multiplier=1).then_inc(causal_set, 1)
            pool.affine_select(out=causB[:, :, :], in_=causB[:, :, :], compare_op=ALU.is_ge, fill=MASKED, base=0,
                               pattern=[[0, NH], [-1, QB]], channel_multiplier=1).then_inc(causal_set, 1)
            pool.wait_ge(causal_set, 4)

            def fold(q, v):
                p, w = V1 * q + v, xw[0:NTOK, v % 2, :, :]
                pool.wait_ge(x_weighted, p + 1)
                pool.tensor_tensor(w[:, 0:4, :], w[:, 0:4, :], w[:, 4:8, :], ALU.add).then_inc(x_fold[0], 1)
                pool.wait_ge(x_fold[0], p + 1)
                pool.tensor_tensor(w[:, 0:2, :], w[:, 0:2, :], w[:, 2:4, :], ALU.add).then_inc(x_fold[1], 1)
                pool.wait_ge(x_fold[1], p + 1)
                pool.tensor_tensor(w[:, 0:1, :], w[:, 0:1, :], w[:, 1:2, :], ALU.add).then_inc(x_fold[2], 1)

            def tokens(q):
                for v in range(V1):
                    fold(q, v)

            tokens(0)
            with pool.Fori(1, NPAIR // V1) as q:
                tokens(q)

            def ln_power(g):
                pool.wait_ge(ln_var, g + 1)
                if positive(g):
                    pool.wait_ge(ln_done, g)
                pool.tensor_tensor(ln_rs[:, 0:4], ln_ve[:, 0:4], neg_half[:, 0:4], ALU.pow).then_inc(ln_rstd, 1)

            def norm_p(m, v):
                pool.wait_ge(at_inverted, m + 1)
                p = pu[:, v % 4, :, :, :].rearrange("p a b u -> p (a b) u")
                pool.tensor_tensor(p, p, bcast(pr[:, v % 2, :, :].rearrange("p a b -> p (a b)"), 2, NTOK),
                                   ALU.mult).then_inc(at_normed, 1)

            def attention(q):
                for v in range(V2):
                    m, g = V2 * q + v, 2 * q + v // 4
                    if v % 4 == 1 and exists(g + 1, NQUAD):
                        ln_power(g + 1)
                    if exists(m - 1, NBATCH):
                        norm_p(m - 1, (v - 1) % V2)

            ln_power(0)
            attention(0)
            with pool.Fori(1, NBATCH // V2 - 1) as q:
                attention(q)
            attention(NBATCH // V2 - 1)
            attention(NBATCH // V2)

            def power3(g):
                pool.wait_ge(ln3_var, g + 1)
                pool.tensor_tensor(ln_rs[:, 0:4], ln_ve[:, 0:4], neg_half[:, 0:4], ALU.pow).then_inc(ln3_rstd, 1)

            def guard(m, v, g):
                pool.wait_ge(c_normed, m + 1)
                pool.wait_ge(f_va, g + 1)
                o = o3[:, v // 4, v % 4, :, :, :]
                pool.tensor_tensor(o, o, bcast(nz[:, v // 4, v % 4, :, :], 2, NE), ALU.mult).then_inc(c_guarded, 1)

            def gates(g, g2):
                pool.wait_ge(g_inv, g + 1)
                e = ge[:, g2, :].rearrange("p (a e) -> p a e", e=NE)
                pool.tensor_tensor(e, e, bcast(gr[:, g2, :], 2, NE), ALU.mult).then_inc(g_gs, 1)
                pool.wait_ge(g_gs, g + 1)
                o = o3[:, g2, :, :, :, :].rearrange("p b n e d -> p (b n e) d")
                pool.tensor_tensor(o, o, bcast(ge[:, g2, :], 2, HD), ALU.mult).then_inc(g_mul, 1)
                pool.wait_ge(g_mul, g + 1)
                o = o3[:, g2, :, :, :, :].rearrange("p b n e d -> p (b n) e d")
                pool.tensor_tensor(o[:, :, 0:2, :], o[:, :, 0:2, :], o[:, :, 2:4, :], ALU.add).then_inc(g_f1, 1)
                pool.wait_ge(g_f1, g + 1)
                y = yy[:, g2, :].rearrange("p (a d) -> p a d", d=HD)
                pool.tensor_tensor(y, o[:, :, 0, :], o[:, :, 1, :], ALU.add).then_inc(g_f2, 1)
                pool.wait_ge(g_f2, g + 1)
                y = yy[:, g2, :].rearrange("p (b c) -> p b c", b=4)
                pool.tensor_tensor(y, y, bcast(resid[:, :, :].rearrange("p n d -> p (n d)"), 1, 4), ALU.add).then_inc(y_made, 1)

            def norm_square(g, g2, cent, sq):
                pool.wait_ge(cent, g + 1)
                pool.tensor_tensor(ysq[:, g2, :], yc[:, g2, :], yc[:, g2, :], ALU.mult).then_inc(sq, 1)

            def norm_power(g, g2, k, eps, rstd):
                pool.wait_ge(eps, g + 1)
                pool.tensor_tensor(st[:, g2, k, 3, :], st[:, g2, k, 2, :], neg_half[:, :], ALU.pow).then_inc(rstd, 1)

            def norm_affine(g, g2, k, mul, mid, done, dst):
                pool.wait_ge(mul, g + 1)
                y = yc[:, g2, :].rearrange("p (a d) -> p a d", d=HD)
                pool.tensor_tensor(y, y, bcast(gam[:, k, :], 1, 16), ALU.mult).then_inc(mid, 1)
                pool.wait_ge(mid, g + 1)
                pool.tensor_tensor(dst[:, g2, :].rearrange("p (a d) -> p a d", d=HD), y, bcast(bet[:, k, :], 1, 16),
                                   ALU.add).then_inc(done, 1)

            def residual(g, g2):
                pool.wait_ge(t_made, g + 1)
                pool.tensor_tensor(ft[:, g2, :], ft[:, g2, :], fx[:, g2, :], ALU.add).then_inc(z_made, 1)

            def finish(g, g2, half):
                pool.wait_ge(fl_inv, g + 1)
                e = fe[:, g2, :].rearrange("p (b n) -> p b n", b=4)
                pool.tensor_tensor(e, e, bcast(fr[:, g2, :], 2, NH), ALU.mult).then_inc(fl_w, 1)
                pool.wait_ge(fl_w, g + 1)
                o = fo[:, g2, :].rearrange("p (a d) -> p a d", d=HD)
                pool.tensor_tensor(o, o, bcast(fe[:, g2, :], 2, HD), ALU.mult).then_inc(fo_mul, 1)
                pool.wait_ge(fo_mul, g + 1)
                if positive(half):
                    pool.wait_ge(out_done[g2], 16 * half)
                pool.tensor_tensor(ho[:, g2, :].rearrange("p (b f) -> p b f", b=4), fo[:, g2, :].rearrange("p (b f) -> p b f", b=4),
                                   h[:, bass.ds(4 * g, 4), :], ALU.add).then_inc(ho_made, 1)

            def experts(q):
                for v in range(V2):
                    m, g = V2 * q + v, 2 * q + v // 4
                    if v % 4 == 0 and exists(g + 1, NQUAD):
                        power3(g + 1)
                    if exists(m - 2, NBATCH):
                        guard(m - 2, (v - 2) % V2, 2 * q + (v - 2) // 4)
                    for s in (13, 12, 11, 10, 9, 8):
                        G, g2 = 2 * q + (v - s) // 4, (v - s) // 4 % 2
                        if (v - s) % 4 or not exists(G, NQUAD):
                            continue
                        if s == 8:
                            gates(G, g2)
                        if s == 9:
                            norm_square(G, g2, y_cent, y_sq)
                            norm_power(G, g2, 0, y_eps, y_rstd)
                            norm_affine(G, g2, 0, y_mul, y_gam, fx_made, fx)
                        if s == 11:
                            residual(G, g2)
                            norm_square(G, g2, z_cent, z_sq)
                            norm_power(G, g2, 1, z_eps, z_rstd)
                            norm_affine(G, g2, 1, z_mul, z_gam, fo_made, fo)
                        if s == 13:
                            finish(G, g2, q + ((v - s) // 4 - g2) // 2)

            power3(0)
            experts(0)
            experts(1)
            with pool.Fori(2, NBATCH // V2 - 1) as q:
                experts(q)
            for q in range(NBATCH // V2 - 1, NBATCH // V2 + 2):
                experts(q)

        @block.tensor
        def _(pe):
            def turn(q, v):
                p = V1 * q + v
                pe.wait_ge(x_loaded[v], 16 * q + 16)
                if positive(p - 1):
                    pe.wait_ge(x_weighted, p - 1)
                for k in range(KW):
                    mm = pe.matmul(turned(v % 2)[:, k, 0:130], xs[:, v, k:NTOK * KW:KW], ident_w[:, :],
                                   start=True, stop=True)
                mm.then_inc(x_turned, 1)

            def tokens(q):
                for v in range(V1):
                    turn(q, v)

            pe.wait_ge(pool_own, 1)
            pe.wait_ge(tok_loaded, 16 * 3)
            tokens(0)
            with pe.Fori(1, NPAIR // V1) as q:
                tokens(q)

            pe.wait_ge(x_weighted, NPAIR)
            pe.wait_ge(attn_loaded, 16 * 4)
            pe.wait_ge(zeroed2, 4)
            for hd in range(HEADS):
                mm = pe.matmul(psum[0:NFEAT, 0, NFEAT * hd:NFEAT * (hd + 1)], q_w[:, hd, :], k_w[:, hd, :],
                               start=True, stop=True)
            mm.then_inc(g_made, 1)
            pe.wait_ge(g_ready, 1)

            def turn_x(g, g2):
                pe.wait_ge(ln_done, g + 1)
                if positive(2 * g):
                    pe.wait_ge(at_q[1], 2 * g)
                for b in range(4):
                    mm = pe.transpose(at_Q[:, b, :], xn[:, g2, b, :, :].rearrange("p a f -> p (a f)"), ident[0:TP, 0:TP])
                mm.then_inc(at_turned, 1)

            def project(g, g2, hp):
                if hp == 0:
                    pe.wait_ge(at_xT, g + 1)
                else:
                    pe.wait_ge(at_q[(hp - 1) % 2], 2 * g + (hp - 1) // 2 + 1)
                pe.matmul(at_Q[:, :, 0:NTOK], g_w[:, 128 * hp:128 * (hp + 1)], xT[:, g2, :, 0, :],
                          start=True, stop=True).then_inc(at_projected, 1)

            def score(m, g, v):
                b, g2 = v % 4, v // 4
                if b == 0:
                    pe.wait_ge(at_q[0], 2 * g + 2)
                    pe.wait_ge(at_q[1], 2 * g + 2)
                if positive(m - 1):
                    pe.wait_ge(at_shifted, m - 1)
                q = qs[:, g2, b, :, :].rearrange("p a t -> p (a t)")
                for t in range(NT):
                    mm = pe.matmul(at_S(v)[:, t, :], q[:, 128 * t:128 * (t + 1)],
                                   xT[:, g2, b, :, :].rearrange("p a u -> p (a u)"), start=True, stop=True)
                mm.then_inc(at_scored, 1)

            def turn_p(m, v, par):
                pe.wait_ge(at_normed, m + 1)
                if positive(2 * m + par):
                    pe.wait_ge(at_pT, 2 * m + par)
                for t in range(NT):
                    mm = pe.transpose(at_P[:, 128 * t:128 * (t + 1)], pu[:, v % 4, t, par, :], ident)
                mm.then_inc(at_pturned, 1)

            def mix(m, v, par):
                pe.wait_ge(at_pT, 2 * m + par + 1)
                if par == 0 and positive(m):
                    pe.wait_ge(at_cT, m)
                pe.matmul(at_C[64 * par:64 * par + 64, :], xn[0:NTOK, v // 4, v % 4, 0, :], pT[:, par, :],
                          start=True, stop=True).then_inc(at_mixed, 1)

            def give_out(m, v):
                pe.wait_ge(at_cT, m + 1)
                if positive(m):
                    pe.wait_ge(at_added, m)
                for hp in range(HP):
                    mm = pe.matmul(at_O, cT[:, v % 2, hp, :], vo_w[:, hp, :], start=(hp == 0), stop=(hp == HP - 1))
                mm.then_inc(at_out, 1)

            def attention(q):
                for v in range(V2):
                    m, g, g2 = V2 * q + v, 2 * q + v // 4, (v // 4 + 1) % 2
                    more = exists(g + 1, NQUAD)
                    v2, v3 = (v - 2) % V2, (v - 3) % V2
                    if exists(m - 2, NBATCH):
                        turn_p(m - 2, v2, 0)
                    if exists(m, NBATCH):
                        score(m, g, v)
                    if v % 4 == 3 and more:
                        project(g + 1, g2, 0)
                    if exists(m - 2, NBATCH):
                        turn_p(m - 2, v2, 1)
                    if exists(m - 3, NBATCH):
                        give_out(m - 3, v3)
                    if v % 4 == 3 and more:
                        project(g + 1, g2, 1)
                    if exists(m - 2, NBATCH):
                        mix(m - 2, v2, 0)
                    if v % 4 == 2 and more:
                        turn_x(g + 1, g2)
                    if v % 4 == 3 and more:
                        project(g + 1, g2, 2)
                    if exists(m - 2, NBATCH):
                        mix(m - 2, v2, 1)
                    if v % 4 == 3 and more:
                        project(g + 1, g2, 3)

            turn_x(0, 0)
            for hp in range(HP):
                project(0, 0, hp)
            attention(0)
            with pe.Fori(1, NBATCH // V2 - 1) as q:
                attention(q)
            attention(NBATCH // V2 - 1)
            attention(NBATCH // V2)

            pe.wait_ge(at_added, NBATCH)
            pe.wait_ge(ff_loaded, FF_LOADS)
            pe.wait_ge(causal_set, 4)
            for n in range(NH):
                for e in range(NE):
                    c = HD * (NE * n + e)
                    mm = pe.matmul(psum[0:HD, 0, c:c + HD], wq_s[:, n, e, :], wk_s[:, n, :], start=True, stop=True)
            mm.then_inc(w_made, 1)
            pe.wait_ge(w_read, 1)
            for n in range(NH):
                pe.matmul(psum[0:NFEAT + 1, 0, 64 * n:64 * n + 64], whl[:, n, :], m_s[:, n, :, :].rearrange("p e d -> p (e d)"),
                          start=True, stop=True)
                pe.matmul(psum[0:NFEAT + 1, 1, HD * n:HD * n + HD], whl[:, n, :], wvT[:, n, :], start=True, stop=True)
                mm = pe.matmul(psum[0:NFEAT + 1, 1, 64 + HD * n:64 + HD * n + HD], whl[:, n, :], ident[0:HD, 0:HD],
                               start=True, stop=True)
            mm.then_inc(w_made, 1)
            pe.wait_ge(w_read, 4)

            def front_turn(g, g2):
                pe.wait_ge(ln3_done, g + 1)
                pe.transpose(F_[:, 0:TP], xn3[:, 0:2, :].rearrange("p b f -> p (b f)"), ident[0:TP, 0:TP])
                for b in range(1, 4):
                    mm = pe.transpose(F_[0:NFEAT, TP * b:TP * b + TP], xn3[:, b, :], ident[0:TP, 0:TP])
                mm.then_inc(f_turned, 1)

            def front_sx(g, g2):
                pe.wait_ge(f_xT, g + 1)
                pe.matmul(F_[:, 0:4 * TP], wsx[:, :, :].rearrange("p n d -> p (n d)"),
                          x3T[:, :, :].rearrange("p b t -> p (b t)"), start=True, stop=True).then_inc(f_sx, 1)

            def front_tok(g, g2):
                pe.wait_ge(f_diagA, g + 1)
                pe.wait_ge(f_diagV, g + 1)
                for b in range(4):
                    mm = pe.matmul(F_[0:TP, 128 * b:128 * b + 128], x3T[:, b, :], wtok[:, :, :, :].rearrange("p a n d -> p (a n d)"),
                                   start=True, stop=True)
                mm.then_inc(f_tok, 1)

            def front_q(g, g2, e):
                if e == 0:
                    pe.wait_ge(f_va, g + 1)
                elif e % 2:
                    pe.wait_ge(f_qA, 2 * g + e // 2 + 1)
                else:
                    pe.wait_ge(f_qV, 2 * g + e // 2)
                pe.matmul(F_[:, 0:4 * TP], aq[:, e, :, :].rearrange("p n d -> p (n d)"),
                          x3T[:, :, :].rearrange("p b t -> p (b t)"), start=True, stop=True).then_inc(f_q, 1)

            def score3(m, g, v):
                b, g2 = v % 4, v // 4
                if b == 0:
                    pe.wait_ge(f_qA, 2 * g + 2)
                    pe.wait_ge(f_qV, 2 * g + 2)
                if positive(m):
                    pe.wait_ge(s_shifted, m)
                for j, start in ((2, True), (1, True), (0, False)):
                    pe.matmul(SJ[j], q3[:, g2, b, j, :, :].rearrange("p e t -> p (e t)"), sxd[:, g2, b, :, 0:WIDTH[j]],
                              start=start, stop=False, skip_group_check=True)
                for j in range(NJ):
                    w = WIDTH[j] - QB * j
                    mm = pe.matmul(SJ[j][:, :, QB * j:WIDTH[j]], causA[:, :], causB[:, :, 0:w],
                                   start=False, stop=True, skip_group_check=True)
                mm.then_inc(s_scored, 1)

            def turn_p3(m, v, n):
                if n == 0:
                    pe.wait_ge(s_exped, m + 1)
                if positive(4 * m + n - 1):
                    pe.wait_ge(p_copied, 4 * m + n - 1)
                for j in range(NJ):
                    mm = pe.transpose(P3(n)[:, 128 * j:128 * j + 128], pu3[:, v % 2, n, j, :], ident)
                mm.then_inc(p_turned, 1)

            def mix3(m, v, n):
                pe.wait_ge(p_copied, 4 * m + n + 1)
                if n == 0 and positive(m):
                    pe.wait_ge(c_normed, m)
                for e in range(NE):
                    mm = pe.matmul(C3[:, NE * n + e, :], pT3[:, n, e, :, :].rearrange("p j t -> p (j t)"),
                                   va[0:NTOK, v // 4, v % 4, n, :], start=True, stop=True)
                mm.then_inc(p_mixed, 1)

            def gate_turn(g, g2, half):
                if half == 0:
                    pe.wait_ge(c_guarded, 4 * g + 4)
                    if positive(g):
                        pe.wait_ge(g_added, g)
                else:
                    pe.wait_ge(r0_copied, 2 * g + 1)
                for b in range(2):
                    o = o3[:, g2, 2 * half + b, :, :, :].rearrange("p n e d -> p (n e d)")
                    for hp in range(2):
                        mm = pe.transpose(R0[:, TP * (2 * b + hp):TP * (2 * b + hp + 1)], o[:, 128 * hp:128 * hp + 128],
                                          ident[0:TP, 0:TP])
                mm.then_inc(r0_turned, 1)

            def gate_logits(g, g2):
                pe.wait_ge(r0_copied, 2 * g + 2)
                for b in range(4):
                    for hp in range(2):
                        mm = pe.matmul(R0[0:TP, 16 * b:16 * b + 16], oT[:, b // 2, 2 * (b % 2) + hp, :], gT[:, hp, :],
                                       start=(hp == 0), stop=(hp == 1))
                mm.then_inc(r0_gated, 1)

            def turn_rest(g, g2, src, ready, done):
                pe.wait_ge(ready, g + 1)
                pe.transpose(R1[:, 0:TP], src[:, g2, 0:128], ident[0:TP, 0:TP])
                for b in range(1, 4):
                    mm = pe.transpose(R1[0:NFEAT, TP * b:TP * b + TP], src[:, g2, 64 * b:64 * b + 64], ident[0:TP, 0:TP])
                mm.then_inc(done, 1)

            def layer1(g, g2):
                pe.wait_ge(r1_fxc, g + 1)
                pe.matmul(R1[:, 0:4 * TP], fc1[:, :], fxT[:, g2, :], start=True, stop=True).then_inc(r1_fc1, 1)

            def layer2(g, g2):
                pe.wait_ge(h_masked, g + 1)
                for b in range(4):
                    mm = pe.matmul(R1[0:TP, 64 * b:64 * b + 64], hxm[:, g2, TP * b:TP * b + TP], fc2[:, :],
                                   start=True, stop=True)
                mm.then_inc(r1_fc2, 1)

            def head_logits(g, g2):
                pe.wait_ge(r1_foc, g + 1)
                for b in range(4):
                    mm = pe.matmul(R1[0:TP, 4 * b:4 * b + 4], foT[:, g2, TP * b:TP * b + TP], fgT[:, :],
                                   start=True, stop=True)
                mm.then_inc(r1_fl, 1)

            def experts(q):
                for v in range(V2):
                    m, g, f2 = V2 * q + v, 2 * q + v // 4, (v // 4 + 1) % 2
                    more = exists(g + 1, NQUAD)

                    def rest(s):
                        G, g2 = 2 * q + (v - s) // 4, (v - s) // 4 % 2
                        if (v - s) % 4 or not exists(G, NQUAD):
                            return
                        if s == 6:
                            gate_turn(G, g2, 0)
                            gate_turn(G, g2, 1)
                        if s == 7:
                            gate_logits(G, g2)
                        if s == 10:
                            if positive(G):
                                pe.wait_ge(fl_shifted, G)
                            turn_rest(G, g2, fx, fx_made, r1_fxt)
                        if s == 10.5:
                            layer1(G, g2)
                        if s == 11:
                            layer2(G, g2)
                        if s == 12:
                            turn_rest(G, g2, fo, fo_made, r1_fot)

                    if exists(m, NBATCH):
                        score3(m, g, v)
                    rest(10)
                    rest(12)
                    if exists(m - 1, NBATCH):
                        turn_p3(m - 1, (v - 1) % V2, 0)
                        turn_p3(m - 1, (v - 1) % V2, 1)
                    if v % 4 == 1 and more:
                        front_turn(g + 1, f2)
                    if v % 4 == 2 and more:
                        front_sx(g + 1, f2)
                    if v % 4 == 3 and more:
                        front_q(g + 1, f2, 1)
                    rest(11)
                    rest(6)
                    rest(7)
                    if exists(m - 1, NBATCH):
                        mix3(m - 1, (v - 1) % V2, 0)
                        turn_p3(m - 1, (v - 1) % V2, 2)
                    if v % 4 == 2 and more:
                        front_tok(g + 1, f2)
                    if v % 4 == 3 and more:
                        front_q(g + 1, f2, 2)
                    if exists(m - 1, NBATCH):
                        mix3(m - 1, (v - 1) % V2, 1)
                        turn_p3(m - 1, (v - 1) % V2, 3)
                    G10, G12 = 2 * q + (v - 10) // 4, 2 * q + (v - 12) // 4
                    if v % 4 == 2 and exists(G10, NQUAD):
                        layer1(G10, (v - 10) // 4 % 2)
                    if v % 4 == 0 and exists(G12, NQUAD):
                        head_logits(G12, (v - 12) // 4 % 2)
                    if v % 4 == 2 and more:
                        front_q(g + 1, f2, 0)
                    if exists(m - 1, NBATCH):
                        mix3(m - 1, (v - 1) % V2, 2)
                        mix3(m - 1, (v - 1) % V2, 3)
                    if v % 4 == 3 and more:
                        front_q(g + 1, f2, 3)

            front_turn(0, 0)
            front_sx(0, 0)
            front_tok(0, 0)
            for e in range(NE):
                front_q(0, 0, e)
            experts(0)
            experts(1)
            with pe.Fori(2, NBATCH // V2 - 1) as q:
                experts(q)
            for q in range(NBATCH // V2 - 1, NBATCH // V2 + 2):
                experts(q)

        @block.scalar
        def _(act):
            def exp_tok(q, v):
                p = V1 * q + v
                act.wait_ge(tok_shifted, p + 1)
                act.activation(tok_e[0:NTOK, v % 2, :], tok_d[0:NTOK, v % 2, :], ACT.Exp).then_inc(tok_exped, 1)

            def store_h(q, v):
                p = V1 * q + v
                act.wait_ge(x_fold[2], p + 1)
                act.wait_ge(tok_inverted, p + 1)
                for b in range(2):
                    ins = act.activation(h[0:NTOK, bass.ds(2 * V1 * q + (2 * v + b), 1), :].rearrange("p o f -> p (o f)"),
                                         xw[0:NTOK, v % 2, 0, NFEAT * b:NFEAT * (b + 1)], ACT.Copy,
                                         scale=tok_r[0:NTOK, v % 2, b:b + 1])
                ins.then_inc(h_pooled, 1)

            def tokens(q):
                for v in range(V1):
                    exp_tok(q, v)
                    if exists(V1 * q + v - 2, NPAIR):
                        store_h(q if v > 1 else q - 1, (v - 2) % V1)

            tokens(0)
            with act.Fori(1, NPAIR // V1) as q:
                tokens(q)
            store_h(NPAIR // V1 - 1, V1 - 2)
            store_h(NPAIR // V1 - 1, V1 - 1)

            act.wait_ge(g_made, 1)
            act.activation(g_w[0:NFEAT, :], psum[0:NFEAT, 0, :], ACT.Copy, scale=float(NFEAT) ** -0.5).then_inc(g_ready, 1)

            def copy_xT(g, g2):
                act.wait_ge(at_turned, g + 1)
                for par in range(2):
                    rows = slice(64 * par, 64 * par + 64)
                    ins = act.activation(xT[rows, g2, :, par, :], at_Q[rows, :, 0:NTOK], ACT.Copy)
                ins.then_inc(at_xT, 1)

            def copy_q(g, g2, hp):
                act.wait_ge(at_projected, 4 * g + hp + 1)
                act.activation(qs[:, g2, :, hp, 0:NTOK], at_Q[:, :, 0:NTOK], ACT.Copy).then_inc(at_q[0], 1)

            def exp_s(m, v):
                act.wait_ge(at_shifted, m + 1)
                p = pu[:, v % 4, :, :, :].rearrange("p a b u -> p (a b u)")
                act.activation(p, p, ACT.Exp).then_inc(at_exped, 1)

            def copy_pT(m, par):
                act.wait_ge(at_pturned, 2 * m + par + 1)
                if positive(2 * m + par - 1):
                    act.wait_ge(at_mixed, 2 * m + par - 1)
                act.activation(pT[:, par, :], at_P, ACT.Copy).then_inc(at_pT, 1)

            def copy_cT(m, v):
                act.wait_ge(at_mixed, 2 * m + 2)
                if positive(m - 1):
                    act.wait_ge(at_out, m - 1)
                act.activation(cT[:, v % 2, :, :].rearrange("p a t -> p (a t)"), at_C, ACT.Copy).then_inc(at_cT, 1)

            def attention(q):
                for v in range(V2):
                    m, g, g2 = V2 * q + v, 2 * q + v // 4, (v // 4 + 1) % 2
                    more = exists(g + 1, NQUAD)
                    if exists(m - 2, NBATCH):
                        copy_pT(m - 2, 0)
                    if v % 4 == 3 and more:
                        copy_q(g + 1, g2, 0)
                    if exists(m - 2, NBATCH):
                        copy_pT(m - 2, 1)
                    if exists(m, NBATCH):
                        exp_s(m, v)
                    if v % 4 == 2 and more:
                        copy_xT(g + 1, g2)
                    if v % 4 == 3 and more:
                        copy_q(g + 1, g2, 2)
                    if exists(m - 2, NBATCH):
                        copy_cT(m - 2, (v - 2) % V2)

            copy_xT(0, 0)
            copy_q(0, 0, 0)
            copy_q(0, 0, 2)
            attention(0)
            with act.Fori(1, NBATCH // V2 - 1) as q:
                attention(q)
            attention(NBATCH // V2 - 1)
            attention(NBATCH // V2)

            act.wait_ge(w_made, 1)
            act.activation(m_s[:, :, :, :].rearrange("p n e d -> p (n e d)"), psum[0:HD, 0, 0:256], ACT.Copy,
                           scale=float(HD) ** 0.5).then_inc(w_read, 1)
            act.wait_ge(w_made, 2)
            act.activation(aq[:, :, :, 0:HD].rearrange("p e n d -> p n e d"),
                           psum[0:NFEAT + 1, 0, 0:256].rearrange("p (n e d) -> p n e d", n=NH, e=NE), ACT.Copy).then_inc(w_read, 1)
            act.activation(wtok[:, :, :, :].rearrange("p a n d -> p (a n d)"), psum[0:NFEAT + 1, 1, 0:128], ACT.Copy).then_inc(w_read, 1)
            act.activation(wsx[:, :, 0:HD], psum[0:NFEAT + 1, 1, 64:128].rearrange("p (n d) -> p n d", n=NH), ACT.Copy).then_inc(w_read, 1)

            def front_xT(g):
                act.wait_ge(f_turned, g + 1)
                act.activation(x3T[0:NFEAT, :, :].rearrange("p b t -> p (b t)"), F_[0:NFEAT, 0:4 * TP], ACT.Copy).then_inc(f_xT, 1)

            def front_diag(g, g2):
                act.wait_ge(f_sx, g + 1)
                for n in (0, 1):
                    rows = slice(32 * n, 32 * n + 32)
                    ins = act.activation(sxd[rows, g2, :, n, :], F_[rows, 0:4 * TP].rearrange("p (b t) -> p b t", b=4)[:, :, 0:NTOK],
                                         ACT.Copy)
                ins.then_inc(f_diagA, 1)

            def front_q(g, g2, e):
                act.wait_ge(f_q, 4 * g + e + 1)
                act.activation(q3[:, g2, :, :, e, :], F_[:, 0:4 * TP].rearrange("p (b j t) -> p b j t", b=4, j=NJ),
                               ACT.Copy).then_inc(f_qA, 1)

            def exp3(m, v):
                act.wait_ge(s_shifted, m + 1)
                for j in range(NJ):
                    p = pu3[:, v % 2, :, j, 0:WIDTH[j]]
                    ins = act.activation(p, p, ACT.Exp)
                ins.then_inc(s_exped, 1)

            def copy_p3(m, n):
                act.wait_ge(p_turned, 4 * m + n + 1)
                if positive(4 * m + n - 3):
                    act.wait_ge(p_mixed, 4 * m + n - 3)
                act.activation(pT3[:, n, :, :, :].rearrange("p e j t -> p j e t"), P3(n).rearrange("p (j e t) -> p j e t", j=NJ, e=NE),
                               ACT.Copy).then_inc(p_copied, 1)

            def experts(q):
                for v in range(V2):
                    m, g, f2 = V2 * q + v, 2 * q + v // 4, (v // 4 + 1) % 2
                    more = exists(g + 1, NQUAD)

                    def rest(s):
                        G, g2 = 2 * q + (v - s) // 4, (v - s) // 4 % 2
                        if (v - s) % 4 or not exists(G, NQUAD):
                            return
                        if s == 6:
                            for half in range(2):
                                act.wait_ge(r0_turned, 2 * G + half + 1)
                                act.activation(oT[:, half, :, :].rearrange("p a t -> p (a t)"), R0[:, 0:4 * TP],
                                               ACT.Copy).then_inc(r0_copied, 1)
                        if s == 7:
                            act.wait_ge(g_shifted, G + 1)
                            act.activation(ge[:, g2, :], gl[:, g2, :], ACT.Exp).then_inc(g_exped, 1)
                        if s == 10:
                            act.wait_ge(r1_fxt, G + 1)
                            act.activation(fxT[:, g2, :], R1[0:NFEAT, 0:4 * TP], ACT.Copy).then_inc(r1_fxc, 1)
                        if s == 12:
                            act.wait_ge(r1_fot, G + 1)
                            act.activation(foT[:, g2, :], R1[0:NFEAT, 0:4 * TP], ACT.Copy).then_inc(r1_foc, 1)

                    rest(10)
                    rest(12)
                    if exists(m - 1, NBATCH):
                        copy_p3(m - 1, 0)
                        copy_p3(m - 1, 1)
                    if v % 4 == 1 and more:
                        front_xT(g + 1)
                    if v % 4 == 2 and more:
                        front_diag(g + 1, f2)
                    rest(6)
                    if exists(m - 1, NBATCH):
                        copy_p3(m - 1, 2)
                    if v % 4 == 3 and more:
                        front_q(g + 1, f2, 2)
                    if exists(m - 1, NBATCH):
                        copy_p3(m - 1, 3)
                    rest(7)
                    G10, G12 = 2 * q + (v - 10) // 4, 2 * q + (v - 12) // 4
                    if v % 4 == 2 and exists(G10, NQUAD):
                        g2 = (v - 10) // 4 % 2
                        act.wait_ge(r1_fc1, G10 + 1)
                        act.activation(hx[:, g2, :], R1[0:NFEAT, 0:4 * TP], ACT.Relu, bias=b1[:, :]).then_inc(r1_hx, 1)
                    if v % 4 == 2 and more:
                        front_q(g + 1, f2, 0)
                    if exists(m, NBATCH):
                        exp3(m, v)
                    if v % 4 == 0 and exists(G12, NQUAD):
                        g2 = (v - 12) // 4 % 2
                        act.wait_ge(fl_shifted, G12 + 1)
                        act.activation(fe[:, g2, :], fl[:, g2, :], ACT.Exp).then_inc(fl_exped, 1)

            front_xT(0)
            front_diag(0, 0)
            front_q(0, 0, 0)
            front_q(0, 0, 2)
            experts(0)
            experts(1)
            with act.Fori(2, NBATCH // V2 - 1) as q:
                experts(q)
            for q in range(NBATCH // V2 - 1, NBATCH // V2 + 2):
                experts(q)

        @block.vector
        def _(dve):
            def shift_tok(q, v):
                p, v2 = V1 * q + v, v % 2
                dve.wait_ge(x_turned, p + 1)
                s = tok_s[0:NTOK, v2, :].rearrange("p (k b) -> p k b", b=2)
                dve.tensor_scalar(s, turned(v2)[:, :, 128:130], tokb[0:NTOK, :], None, ALU.add).then_inc(tok_scored, 1)
                dve.wait_ge(tok_scored, p + 1)
                dve.tensor_reduce(tok_m[0:NTOK, v2, :], s.rearrange("p k b -> p b k"), AX.X, ALU.max).then_inc(tok_maxed, 1)
                dve.wait_ge(tok_maxed, p + 1)
                dve.tensor_tensor(tok_d[0:NTOK, v2, :].rearrange("p (k b) -> p k b", b=2), s,
                                  bcast(tok_m[0:NTOK, v2, :], 1, KW), ALU.subtract).then_inc(tok_shifted, 1)

            def weigh(q, v):
                p, v2 = V1 * q + v, v % 2
                dve.wait_ge(tok_exped, p + 1)
                e = tok_e[0:NTOK, v2, :]
                dve.tensor_reduce(tok_l[0:NTOK, v2, :], e.rearrange("p (k b) -> p b k", b=2), AX.X,
                                  ALU.add).then_inc(tok_summed, 1)
                if positive(p - 1):
                    dve.wait_ge(h_pooled, p - 1)
                dve.tensor_tensor(xw[0:NTOK, v2, :, :].rearrange("p k (b f) -> p k b f", b=2),
                                  turned(v2)[:, :, 0:128].rearrange("p k (b f) -> p k b f", b=2),
                                  bcast(e.rearrange("p (k b) -> p k b", b=2), 3, NFEAT), ALU.mult).then_inc(x_weighted, 1)
                dve.wait_ge(tok_summed, p + 1)
                dve.reciprocal(tok_r[0:NTOK, v2, :], tok_l[0:NTOK, v2, :]).then_inc(tok_inverted, 1)

            def tokens(q):
                for v in range(V1):
                    shift_tok(q, v)
                    if exists(V1 * q + v - 1, NPAIR):
                        weigh(q if v else q - 1, (v - 1) % V1)

            dve.memset(xT[:, :, :, :, :], 0.0).then_inc(zeroed2, 1)
            dve.memset(qs[:, :, :, :, NTOK:TP], 0.0).then_inc(zeroed2, 1)
            dve.memset(g_w[64:128, :], 0.0).then_inc(zeroed2, 1)
            dve.memset(gT[:, :, :], 0.0).then_inc(zeroed3, 1)
            dve.memset(fc1[:, :], 0.0).then_inc(zeroed3, 1)
            dve.memset(fc2[:, :], 0.0).then_inc(zeroed3, 1)
            dve.memset(aq[:, :, :, :], 0.0).then_inc(zeroed3, 1)
            dve.memset(wsx[:, :, :], 0.0).then_inc(zeroed3, 1)
            dve.memset(sxd[:, :, :, :, :], 0.0).then_inc(zeroed4, 1)
            dve.memset(pu3[:, :, :, :, :], 0.0).then_inc(zeroed4, 1)
            dve.memset(va[:, :, :, :, HD:HD + 1], 1.0).then_inc(zeroed4, 1)
            dve.memset(x3T[NFEAT:NFEAT + 1, :, :], 1.0).then_inc(zeroed4, 1)
            dve.memset(hxm[NFEAT:NFEAT + 1, :, :], 1.0).then_inc(zeroed4, 1)
            dve.wait_ge(tok_loaded, 16 * 3)
            tokens(0)
            with dve.Fori(1, NPAIR // V1) as q:
                tokens(q)
            weigh(NPAIR // V1 - 1, V1 - 1)

            dve.wait_ge(h_pooled, NPAIR)
            dve.wait_ge(zeroed2, 4)

            def ln_stats(g, part):
                if part == 0:
                    for b in range(4):
                        ins = dve.bn_stats(ln_bn[:, b, :], h[:, bass.ds(4 * g + b, 1), :].rearrange("p o f -> p (o f)"))
                    ins.then_inc(ln_stat, 1)
                else:
                    dve.wait_ge(ln_stat, g + 1)
                    dve.memset(spot[:, :], 0.0)
                    for b in range(4):
                        ins = dve.bn_aggr(ln_mv[:, b, :], ln_bn[:, b, :])
                    ins.then_inc(ln_agg, 1)
                    dve.wait_ge(ln_agg, g + 1)
                    dve.tensor_scalar(ln_ve[:, 0:4], ln_mv[:, 0:4, 1], EPS_LN, None, ALU.add).then_inc(ln_var, 1)

            def ln_apply(g, g2):
                dve.wait_ge(ln_rstd, g + 1)
                if positive(8 * (g - 1)):
                    dve.wait_ge(at_mixed, 8 * (g - 1))
                for b in range(4):
                    ins = dve.tensor_scalar(xn[:, g2, b, :, :], h[:, bass.ds(4 * g + b, 1), :].broadcast_to([TP, 2, NFEAT]),
                                            ln_mv[:, b, 0:1], ln_rs[:, b:b + 1], ALU.subtract, ALU.mult)
                ins.then_inc(ln_done, 1)

            def copy_q(g, g2, hp):
                dve.wait_ge(at_projected, 4 * g + hp + 1)
                dve.tensor_copy(qs[:, g2, :, hp, 0:NTOK], at_Q[:, :, 0:NTOK]).then_inc(at_q[1], 1)

            def shift(m, v):
                s = at_S(v).rearrange("p a (b u) -> p a b u", b=2)
                dve.wait_ge(at_scored, m + 1)
                dve.tensor_reduce(mx[:, v % 2, :, :], s, AX.X, ALU.max).then_inc(at_maxed, 1)
                dve.wait_ge(at_maxed, m + 1)
                if positive(2 * (m - 4) + 2):
                    dve.wait_ge(at_pturned, 2 * (m - 4) + 2)
                dve.tensor_tensor(pu[:, v % 4, :, :, :], s, bcast(mx[:, v % 2, :, :], 3, NTOK), ALU.subtract)\
                   .then_inc(at_shifted, 1)

            def sums(m, v):
                dve.wait_ge(at_exped, m + 1)
                dve.tensor_reduce(pl[:, v % 2, :, :], pu[:, v % 4, :, :, :], AX.X, ALU.add).then_inc(at_summed, 1)
                dve.wait_ge(at_summed, m + 1)
                if positive(m - 1):
                    dve.wait_ge(at_normed, m - 1)
                dve.reciprocal(pr[:, v % 2, :, :], pl[:, v % 2, :, :]).then_inc(at_inverted, 1)

            def add_out(m):
                dve.wait_ge(at_out, m + 1)
                hm = h[:, bass.ds(m, 1), :].rearrange("p o f -> p (o f)")
                dve.tensor_tensor(hm, at_O, hm, ALU.add).then_inc(at_added, 1)

            def attention(q):
                for v in range(V2):
                    m, g, g2 = V2 * q + v, 2 * q + v // 4, (v // 4 + 1) % 2
                    more = exists(g + 1, NQUAD)
                    if exists(m - 1, NBATCH):
                        sums(m - 1, (v - 1) % V2)
                    if exists(m, NBATCH):
                        shift(m, v)
                    if v % 4 < 2 and more:
                        ln_stats(g + 1, v % 4)
                    if v % 4 == 2 and more:
                        ln_apply(g + 1, g2)
                    if v % 4 == 3 and more:
                        copy_q(g + 1, g2, 1)
                    if exists(m - 3, NBATCH):
                        add_out(m - 3)
                    if v % 4 == 3 and more:
                        copy_q(g + 1, g2, 3)

            ln_stats(0, 0)
            ln_stats(0, 1)
            ln_apply(0, 0)
            copy_q(0, 0, 1)
            copy_q(0, 0, 3)
            attention(0)
            with dve.Fori(1, NBATCH // V2 - 1) as q:
                attention(q)
            attention(NBATCH // V2 - 1)
            attention(NBATCH // V2)

            dve.wait_ge(ff_loaded, FF_LOADS)

            def stats3(g):
                for b in range(4):
                    ins = dve.bn_stats(ln_bn[:, b, :], h[:, bass.ds(4 * g + b, 1), :].rearrange("p o f -> p (o f)"))
                ins.then_inc(ln3_stat, 1)
                dve.wait_ge(ln3_stat, g + 1)
                dve.memset(spot[:, :], 0.0)
                for b in range(4):
                    ins = dve.bn_aggr(ln_mv[:, b, :], ln_bn[:, b, :])
                ins.then_inc(ln3_agg, 1)
                dve.wait_ge(ln3_agg, g + 1)
                dve.tensor_scalar(ln_ve[:, 0:4], ln_mv[:, 0:4, 1], EPS_LN, None, ALU.add).then_inc(ln3_var, 1)

            def apply3(g):
                dve.wait_ge(ln3_rstd, g + 1)
                if positive(g):
                    dve.wait_ge(f_turned, g)
                for b in range(4):
                    ins = dve.tensor_scalar(xn3[:, b, :], h[:, bass.ds(4 * g + b, 1), :].rearrange("p o f -> p (o f)"),
                                            ln_mv[:, b, 0:1], ln_rs[:, b:b + 1], ALU.subtract, ALU.mult)
                ins.then_inc(ln3_done, 1)

            def front_diag(g, g2):
                dve.wait_ge(f_sx, g + 1)
                dve.wait_ge(f_diagA, g + 1)
                for n in (2, 3):
                    rows = slice(32 * n, 32 * n + 32)
                    ins = dve.tensor_copy(sxd[rows, g2, :, n, :], F_[rows, 0:4 * TP].rearrange("p (b t) -> p b t", b=4)[:, :, 0:NTOK])
                ins.then_inc(f_diagV, 1)

            def front_va(g, g2):
                dve.wait_ge(f_tok, g + 1)
                if positive(16 * (g - 1)):
                    dve.wait_ge(p_mixed, 16 * (g - 1))
                    dve.wait_ge(c_guarded, 4 * (g - 1))
                f = F_[0:TP, :].rearrange("p (b a n d) -> p b a n d", b=4, a=2, n=NH)
                for b in range(4):
                    dve.tensor_copy(va[:, g2, b, :, 0:HD], f[:, b, 0, :, :])
                if isinstance(g, int) and g == 0:
                    for n in range(NH):
                        ins = dve.tensor_copy(resid[:, n, :], f[:, n, 1, n, :])
                    ins.then_inc(f_resid, 1)
                dve.tensor_scalar(nz[:, g2, :, :, :].rearrange("p b n d -> p b (n d)"),
                                  F_[0:TP, :].rearrange("p (b c) -> p b c", b=4)[:, :, 64:128], 0.0, None,
                                  ALU.not_equal).then_inc(f_va, 1)

            def front_q(g, g2, e):
                dve.wait_ge(f_q, 4 * g + e + 1)
                dve.tensor_copy(q3[:, g2, :, :, e, :], F_[:, 0:4 * TP].rearrange("p (b j t) -> p b j t", b=4, j=NJ)).then_inc(f_qV, 1)

            def shift3(m, v):
                dve.wait_ge(s_scored, m + 1)
                for j in range(NJ):
                    ins = dve.tensor_reduce(mx3[:, v % 2, j, :], SJ[j], AX.X, ALU.max)
                ins.then_inc(s_maxed, 1)
                dve.wait_ge(s_maxed, m + 1)
                if positive(4 * (m - 1)):
                    dve.wait_ge(p_turned, 4 * (m - 1))
                for j in range(NJ):
                    ins = dve.tensor_tensor(pu3[:, v % 2, :, j, 0:WIDTH[j]], SJ[j], bcast(mx3[:, v % 2, j, :], 2, WIDTH[j]),
                                            ALU.subtract)
                ins.then_inc(s_shifted, 1)

            def norm3(m, v, g):
                dve.wait_ge(p_mixed, 4 * m + 4)
                dve.reciprocal(r3[:, v % 2, :], C3[:, :, HD]).then_inc(c_inv, 1)
                dve.wait_ge(c_inv, m + 1)
                if positive(g - 1):
                    dve.wait_ge(y_made, g - 1)
                dve.tensor_tensor(o3[:, v // 4, v % 4, :, :, :].rearrange("p n e d -> p (n e) d"), C3[:, :, 0:HD],
                                  bcast(r3[:, v % 2, :], 2, HD), ALU.mult).then_inc(c_normed, 1)

            def centre(g, g2, k, src, made, summed, cent):
                dve.wait_ge(made, g + 1)
                y = src[:, g2, :].rearrange("p (a d) -> p a d", d=HD)
                dve.tensor_reduce(st[:, g2, k, 0, :], y, AX.X, ALU.add).then_inc(summed, 1)
                dve.wait_ge(summed, g + 1)
                dve.scalar_tensor_tensor(out=yc[:, g2, :].rearrange("p (a d) -> p a d", d=HD), in0=bcast(st[:, g2, k, 0, :], 2, HD),
                                         scalar=-1.0 / HD, in1=y, op0=ALU.mult, op1=ALU.add).then_inc(cent, 1)

            def variance(g, g2, k, sq, var, eps):
                dve.wait_ge(sq, g + 1)
                dve.tensor_reduce(st[:, g2, k, 1, :], ysq[:, g2, :].rearrange("p (a d) -> p a d", d=HD), AX.X, ALU.add).then_inc(var, 1)
                dve.wait_ge(var, g + 1)
                dve.tensor_scalar(st[:, g2, k, 2, :], st[:, g2, k, 1, :], 1.0 / HD, EPS_FF, ALU.mult, ALU.add).then_inc(eps, 1)

            def scale(g, g2, k, rstd, mul):
                dve.wait_ge(rstd, g + 1)
                y = yc[:, g2, :].rearrange("p (a d) -> p a d", d=HD)
                dve.tensor_tensor(y, y, bcast(st[:, g2, k, 3, :], 2, HD), ALU.mult).then_inc(mul, 1)

            def gate_shift(g, g2):
                dve.wait_ge(r0_gated, g + 1)
                l = gl[:, g2, :].rearrange("p (b c) -> p b c", b=4)
                dve.tensor_tensor(l, R0[0:TP, 0:64].rearrange("p (b c) -> p b c", b=4), bcast(gbb[:, :], 1, 4), ALU.add).then_inc(g_added, 1)
                dve.wait_ge(g_added, g + 1)
                l = gl[:, g2, :].rearrange("p (a e) -> p a e", e=NE)
                dve.tensor_reduce(gm[:, g2, :], l, AX.X, ALU.max).then_inc(g_maxed, 1)
                dve.wait_ge(g_maxed, g + 1)
                dve.tensor_tensor(l, l, bcast(gm[:, g2, :], 2, NE), ALU.subtract).then_inc(g_shifted, 1)

            def gate_sum(g, g2):
                dve.wait_ge(g_exped, g + 1)
                dve.tensor_reduce(gs[:, g2, :], ge[:, g2, :].rearrange("p (a e) -> p a e", e=NE), AX.X, ALU.add).then_inc(g_summed, 1)
                dve.wait_ge(g_summed, g + 1)
                dve.reciprocal(gr[:, g2, :], gs[:, g2, :]).then_inc(g_inv, 1)

            def mask_hidden(g, g2):
                dve.wait_ge(r1_hx, g + 1)
                dve.scalar_tensor_tensor(out=hxm[0:NFEAT, g2, :], in0=fxT[:, g2, :], scalar=0.0, in1=hx[:, g2, :],
                                         op0=ALU.not_equal, op1=ALU.mult).then_inc(h_masked, 1)

            def mask_second(g, g2):
                dve.wait_ge(r1_fc2, g + 1)
                dve.scalar_tensor_tensor(out=ft[:, g2, :], in0=fx[:, g2, :], scalar=0.0, in1=R1[0:TP, 0:256],
                                         op0=ALU.not_equal, op1=ALU.mult).then_inc(t_made, 1)

            def head_shift(g, g2):
                dve.wait_ge(r1_fl, g + 1)
                l = R1[0:TP, 0:16].rearrange("p (b n) -> p b n", b=4)
                dve.tensor_reduce(fm[:, g2, :], l, AX.X, ALU.max).then_inc(fl_maxed, 1)
                dve.wait_ge(fl_maxed, g + 1)
                dve.tensor_tensor(fl[:, g2, :].rearrange("p (b n) -> p b n", b=4), l, bcast(fm[:, g2, :], 2, NH),
                                  ALU.subtract).then_inc(fl_shifted, 1)

            def head_sum(g, g2):
                dve.wait_ge(fl_exped, g + 1)
                dve.tensor_reduce(fs[:, g2, :], fe[:, g2, :].rearrange("p (b n) -> p b n", b=4), AX.X, ALU.add).then_inc(fl_summed, 1)
                dve.wait_ge(fl_summed, g + 1)
                dve.reciprocal(fr[:, g2, :], fs[:, g2, :]).then_inc(fl_inv, 1)

            def experts(q):
                for v in range(V2):
                    m, g, f2 = V2 * q + v, 2 * q + v // 4, (v // 4 + 1) % 2
                    more = exists(g + 1, NQUAD)

                    def rest(s, part=0):
                        G, g2 = 2 * q + (v - s) // 4, (v - s) // 4 % 2
                        if (v - s) % 4 or not exists(G, NQUAD):
                            return
                        if s == 7:
                            gate_shift(G, g2)
                        if s == 8:
                            gate_sum(G, g2)
                        if s == 9 and part == 0:
                            centre(G, g2, 0, yy, y_made, y_sum, y_cent)
                        if s == 9 and part == 1:
                            variance(G, g2, 0, y_sq, y_var, y_eps)
                        if s == 9 and part == 2:
                            scale(G, g2, 0, y_rstd, y_mul)
                        if s == 10:
                            mask_hidden(G, g2)
                        if s == 11 and part == 0:
                            mask_second(G, g2)
                        if s == 11 and part == 1:
                            centre(G, g2, 1, ft, z_made, z_sum, z_cent)
                        if s == 11 and part == 2:
                            variance(G, g2, 1, z_sq, z_var, z_eps)
                        if s == 11 and part == 3:
                            scale(G, g2, 1, z_rstd, z_mul)
                        if s == 12:
                            head_shift(G, g2)
                        if s == 13:
                            head_sum(G, g2)

                    rest(13)
                    rest(8)
                    rest(9, 0)
                    if v % 4 == 0 and more:
                        stats3(g + 1)
                    if exists(m - 2, NBATCH):
                        NG = 2 * q + (v - 2) // 4
                        norm3(m - 2, (v - 2) % V2, NG)
                    rest(9, 1)
                    if exists(m, NBATCH):
                        shift3(m, v)
                    rest(9, 2)
                    if v % 4 == 1 and more:
                        apply3(g + 1)
                    if v % 4 == 2 and more:
                        front_diag(g + 1, f2)
                    rest(11, 0)
                    if v % 4 == 3 and more:
                        front_q(g + 1, f2, 1)
                    if v % 4 == 2 and more:
                        front_va(g + 1, f2)
                    rest(11, 1)
                    rest(7)
                    rest(11, 2)
                    rest(10)
                    rest(12)
                    rest(11, 3)
                    if v % 4 == 3 and more:
                        front_q(g + 1, f2, 3)

            dve.wait_ge(at_added, NBATCH)
            stats3(0)
            apply3(0)
            front_diag(0, 0)
            front_va(0, 0)
            front_q(0, 0, 1)
            front_q(0, 0, 3)
            experts(0)
            experts(1)
            with dve.Fori(2, NBATCH // V2 - 1) as q:
                experts(q)
            for q in range(NBATCH // V2 - 1, NBATCH // V2 + 2):
                experts(q)


_INS = ["x", "L0_tok_w", "L0_tok_b", "L0_attn_Q", "L0_attn_K", "L0_attn_VO", "L0_ffn_hl_w", "L0_ffn_hl_b",
        "L0_ffn_wq", "L0_ffn_wk", "L0_ffn_wv", "L0_ffn_gate_w", "L0_ffn_gate_b", "L0_ffn_ln_g", "L0_ffn_ln_b",
        "L0_ffn_fc1_w", "L0_ffn_fc1_b", "L0_ffn_fc2_w", "L0_ffn_fc2_b", "L0_ffn_fnorm_g", "L0_ffn_fnorm_b",
        "L0_ffn_fgate_w"]


def kernel(**inputs):
    import numpy as np
    import concourse.bacc as bacc
    from concourse.bass_utils import run_bass_kernel_spmd

    nc = bacc.Bacc("TRN2", target_bir_lowering=False, num_devices=1)
    arrays, args = {}, []
    for name in _INS:
        a = np.ascontiguousarray(inputs[name])
        arrays[f"in_{name}"] = a
        args.append(nc.dram_tensor(f"in_{name}", a.shape, mybir.dt.from_np(a.dtype), kind="ExternalInput").ap())
    args.append(nc.dram_tensor("out_h", (NBATCH, NTOK, NFEAT), F32, kind="ExternalOutput").ap())
    audio_tower(nc, *args)
    result = run_bass_kernel_spmd(nc, [arrays], core_ids=[0])
    return result.results[0]["out_h"]
```

```python
from contextlib import ExitStack

import concourse.bass as bass
from concourse import mybir

F32 = mybir.dt.float32
BF16 = mybir.dt.bfloat16
ALU = mybir.AluOpType
ACT = mybir.ActivationFunctionType
AX = mybir.AxisListType

NBATCH, NFEAT, NTIME = 128, 64, 750
KW = 8
NTOK = -(-NTIME // KW)
TP = 96
HEADS, RANK = 8, 32
NH, NE, HD = 4, 4, 16
QB = 32
WIDTH = [QB, 2 * QB, NTOK]
START = [0, QB, 3 * QB]
SROW = START[2] + NTOK
EPS_LN, EPS_FF = 1e-5, 1e-8
MASKED = -1.0e30
FF_LOADS = 16 * (5 * NH + 4 + NH + 6)


def positive(v):
    return not isinstance(v, int) or v > 0


def exists(m, total):
    return not isinstance(m, int) or 0 <= m < total


def bcast(ap, axis, n):
    ap = ap.unsqueeze(axis)
    shape = list(ap.shape)
    shape[axis] = n
    return ap.broadcast_to(shape)


def audio_tower(nc, x, tok_w, tok_b, attn_q, attn_k, attn_vo, hl_w, hl_b, wq, wk, wv, gate_w, gate_b,
                ln_g, ln_b, fc1_w, fc1_b, fc2_w, fc2_b, fnorm_g, fnorm_b, fgate_w, out):
    with ExitStack() as ctx:
        def sb(name, shape, dt=F32):
            return ctx.enter_context(nc.sbuf_tensor(name, shape, dt))

        def sem(name):
            return ctx.enter_context(nc.semaphore(name))

        psum = ctx.enter_context(nc.psum_tensor("psum", [128, 8, 512], F32))

        ident_w = sb("ident_w", [128, 130])
        ident = ident_w[:, 0:128]
        neg_half = sb("neg_half", [TP, 16])
        tokb = sb("tokb", [TP, 1])
        q_w = sb("q_w", [RANK, HEADS, NFEAT])
        k_w = sb("k_w", [RANK, HEADS, NFEAT])
        g_w = sb("g_w", [128, HEADS * NFEAT])
        vo_w = sb("vo_w", [128, HEADS // 2, NFEAT])

        h = sb("h", [TP, NBATCH, NFEAT])

        zeroed = sem("zeroed")
        zeroed2 = sem("zeroed2")
        zeroed3 = sem("zeroed3")
        zeroed4 = sem("zeroed4")
        pool_own = sem("pool_own")
        consts_ready = sem("consts_ready")
        tok_loaded = sem("tok_loaded")
        attn_loaded = sem("attn_loaded")

        NPAIR = NBATCH // 2
        V1 = 4
        xs = sb("xs", [128, V1, NTOK * KW])
        tok_s = sb("tok_s", [TP, 2, 2 * KW])
        tok_m = sb("tok_m", [TP, 2, 2])
        tok_d = sb("tok_d", [TP, 2, 2 * KW])
        tok_e = sb("tok_e", [TP, 2, 2 * KW])
        tok_l = sb("tok_l", [TP, 2, 2])
        tok_r = sb("tok_r", [TP, 2, 2])
        xw = sb("xw", [TP, 2, KW, 128])
        x_sum = sb("x_sum", [TP, 2, 128])
        x_loaded = [sem(f"x_loaded{i}") for i in range(V1)]
        x_turned = sem("x_turned")
        tok_scored = sem("tok_scored")
        tok_maxed = sem("tok_maxed")
        tok_shifted = sem("tok_shifted")
        tok_exped = sem("tok_exped")
        tok_summed = sem("tok_summed")
        tok_inverted = sem("tok_inverted")
        x_weighted = sem("x_weighted")
        x_fold = sem("x_fold")
        x_summed = sem("x_summed")
        h_pooled = sem("h_pooled")

        x_pairs = x.rearrange("(p two) f t -> p (two f) t", two=2)

        def turned(v2):
            return psum[0:NTOK, 4 * v2:4 * v2 + 4, :].rearrange("p a (two c) -> p (a two) c", two=2)

        V2 = 8
        NQUAD = NBATCH // 4
        HP = HEADS // 2
        NT = 3
        ln_bn = sb("ln_bn", [TP, 4, 6])
        ln_mv = sb("ln_mv", [TP, 4, 2])
        ln_ve = sb("ln_ve", [TP, 4])
        ln_rs = sb("ln_rs", [TP, 4])
        spot = sb("spot", [1, 1])
        xn = sb("xn", [TP, 2, 4, 2, NFEAT])
        xT = sb("xT", [128, 2, 4, 2, NTOK])
        qs = sb("qs", [128, 2, 4, HP, TP])
        mx = sb("mx", [128, 2, NT, 2])
        pl = sb("pl", [128, 2, NT, 2])
        pr = sb("pr", [128, 2, NT, 2])
        pu = sb("pu", [128, 4, NT, 2, NTOK])
        pT = sb("pT", [NTOK, 2, HP * TP])
        cT = sb("cT", [128, 2, HP, TP])
        ln_stat = sem("ln_stat")
        ln_agg = sem("ln_agg")
        ln_var = sem("ln_var")
        ln_rstd = sem("ln_rstd")
        ln_done = sem("ln_done")
        at_turned = sem("at_turned")
        at_xT = sem("at_xT")
        at_projected = sem("at_projected")
        at_q = sem("at_q")
        at_scored = sem("at_scored")
        at_maxed = sem("at_maxed")
        at_shifted = sem("at_shifted")
        at_exped = sem("at_exped")
        at_summed = sem("at_summed")
        at_inverted = sem("at_inverted")
        at_normed = sem("at_normed")
        at_pturned = sem("at_pturned")
        at_pT = sem("at_pT")
        at_mixed = sem("at_mixed")
        at_cT = sem("at_cT")
        at_out = sem("at_out")
        at_added = sem("at_added")
        g_made = sem("g_made")
        g_ready = sem("g_ready")

        at_Q = psum[:, 0, 0:4 * TP].rearrange("p (b t) -> p b t", b=4)

        def at_S(v):
            s = psum[:, 1 + 2 * (v % 2):3 + 2 * (v % 2), :].rearrange("p a (two c) -> p (a two) c", two=2)
            return s[:, 0:NT, 0:2 * NTOK]

        at_P = psum[0:NTOK, 5, 0:NT * 128]
        at_C = psum[:, 6, 0:HP * TP]
        at_O = psum[0:TP, 7, 0:NFEAT]

        NJ = 3
        whl = sb("whl", [HD, NH, NFEAT + 1])
        wq_s = sb("wq_s", [HD, NH, NE, HD])
        wk_s = sb("wk_s", [HD, NH, HD])
        wvT = sb("wvT", [HD, NH, HD])
        m_s = sb("m_s", [HD, NH, NE, HD])
        aq = sb("aq", [NFEAT + 1, NE, NH, 32])
        wsx = sb("wsx", [NFEAT + 1, NH, 32])
        wtok = sb("wtok", [NFEAT + 1, 2, NH, HD])
        gT = sb("gT", [128, 2, NH * NE])
        gbb = sb("gbb", [TP, NH * NE])
        gam = sb("gam", [TP, 2, HD])
        bet = sb("bet", [TP, 2, HD])
        fc1 = sb("fc1", [NFEAT, 128])
        b1 = sb("b1", [NFEAT, 1])
        fc2 = sb("fc2", [NFEAT + 1, NFEAT])
        fgT = sb("fgT", [NFEAT, NH])
        causA = sb("causA", [QB, NE * QB], BF16)
        causB = sb("causB", [QB, NH, QB], BF16)
        xn3 = sb("xn3", [TP, 4, NFEAT])
        x3T = sb("x3T", [NFEAT + 1, 4, TP])
        sxd = sb("sxd", [128, 2, 4, NH, NTOK])
        q3 = sb("q3", [128, 2, 4, NJ, NE, QB])
        va = sb("va", [TP, 2, 4, NH, HD + 1])
        nz = sb("nz", [TP, 2, 4, NH, HD])
        resid = sb("resid", [TP, NH, HD])
        mx3 = sb("mx3", [128, 2, NJ, NH])
        pu3 = sb("pu3", [128, 2, NH, NJ, NTOK])
        pT3 = sb("pT3", [NTOK, NH, NE, NJ, QB])
        r3 = sb("r3", [TP, 2, NH * NE])
        o3 = sb("o3", [TP, 2, 4, NH, NE, HD])
        oT = sb("oT", [128, 2, 4, TP])
        gl = sb("gl", [TP, 2, 64])
        ge = sb("ge", [TP, 2, 64])
        gm = sb("gm", [TP, 2, 16])
        gs = sb("gs", [TP, 2, 16])
        gr = sb("gr", [TP, 2, 16])
        yy = sb("yy", [TP, 2, 256])
        st = sb("st", [TP, 2, 2, 4, 16])
        yc = sb("yc", [TP, 2, 2, 256])
        ysq = sb("ysq", [TP, 2, 2, 256])
        fx = sb("fx", [TP, 2, 256])
        fxT = sb("fxT", [NFEAT, 2, 4 * TP])
        hx = sb("hx", [NFEAT, 2, 4 * TP])
        hxm = sb("hxm", [NFEAT + 1, 2, 4 * TP])
        ft = sb("ft", [TP, 2, 256])
        fo = sb("fo", [TP, 2, 256])
        foT = sb("foT", [NFEAT, 2, 4 * TP])
        fl = sb("fl", [TP, 2, 16])
        fe = sb("fe", [TP, 2, 16])
        fm = sb("fm", [TP, 2, 4])
        fs = sb("fs", [TP, 2, 4])
        fr = sb("fr", [TP, 2, 4])
        ho = sb("ho", [TP, 2, 256])
        names3 = """ff_loaded w_made w_read ln3_stat ln3_agg ln3_var ln3_rstd ln3_done f_turned f_xT f_sx f_diag
            f_tok f_va f_q f_qc f_resid s_scored s_maxed s_shifted s_exped p_turned p_copied p_mixed c_inv c_normed
            c_guarded r0_turned r0_copied r0_gated g_added g_maxed g_shifted g_exped g_summed g_inv g_gs g_mul g_f1 g_f2
            y_made y_sum y_cent y_sq y_var y_eps y_rstd y_mul y_gam fx_made r1_fxt r1_fxc r1_fc1 r1_hx h_masked r1_fc2 t_made z_made
            z_sum z_cent z_sq z_var z_eps z_rstd z_mul z_gam fo_made r1_fot r1_foc r1_fl fl_maxed fl_shifted fl_exped
            fl_summed fl_inv fl_w fo_mul ho_made causal_set"""
        S = {n: sem(n) for n in names3.split()}
        (ff_loaded, w_made, w_read, ln3_stat, ln3_agg, ln3_var, ln3_rstd, ln3_done, f_turned, f_xT, f_sx, f_diag,
         f_tok, f_va, f_q, f_qc, f_resid, s_scored, s_maxed, s_shifted, s_exped, p_turned, p_copied, p_mixed, c_inv, c_normed,
         c_guarded, r0_turned, r0_copied, r0_gated, g_added, g_maxed, g_shifted, g_exped, g_summed, g_inv, g_gs, g_mul, g_f1, g_f2,
         y_made, y_sum, y_cent, y_sq, y_var, y_eps, y_rstd, y_mul, y_gam, fx_made, r1_fxt, r1_fxc, r1_fc1, r1_hx, h_masked, r1_fc2, t_made, z_made,
         z_sum, z_cent, z_sq, z_var, z_eps, z_rstd, z_mul, z_gam, fo_made, r1_fot, r1_foc, r1_fl, fl_maxed, fl_shifted, fl_exped,
         fl_summed, fl_inv, fl_w, fo_mul, ho_made, causal_set) = S.values()
        out_done = [sem("out_done0"), sem("out_done1")]

        F_ = psum[:, 0, :]
        SJ = [psum[:, 2, NH * WIDTH[1]:NH * (WIDTH[1] + WIDTH[0])].rearrange("p (n u) -> p n u", n=NH),
              psum[:, 2, 0:NH * WIDTH[1]].rearrange("p (n u) -> p n u", n=NH),
              psum[:, 1, 0:NH * WIDTH[2]].rearrange("p (n u) -> p n u", n=NH)]
        C3 = psum[0:TP, 5, 0:NH * NE * (HD + 1)].rearrange("p (a c) -> p a c", c=HD + 1)
        R0, R1 = psum[:, 6, :], psum[:, 7, :]

        def P3(n):
            return psum[0:NTOK, 3 + n % 2, 0:NJ * 128]
        out_stored = sem("out_stored")
        block = ctx.enter_context(nc.Block())

        @block.sync
        def _(sp):
            def load(q, pairs):
                for v in range(V1):
                    if positive(V1 * (q - 1) + v + 1):
                        sp.wait_ge(x_turned, V1 * (q - 1) + v + 1)
                    sp.dma_start(xs[:, v, 0:NTIME], pairs(v)).then_inc(x_loaded[v], 16)

            load(0, lambda v: x_pairs[v])
            sp.dma_start(q_w[:, :, :], attn_q.rearrange("h r d -> r h d")).then_inc(attn_loaded, 16)
            sp.dma_start(k_w[:, :, :], attn_k.rearrange("h r d -> r h d")).then_inc(attn_loaded, 16)
            for par in range(2):
                sp.dma_start(vo_w[64 * par:64 * par + 64, :, :],
                               attn_vo.rearrange("(hp par) d e -> par d hp e", par=2)[par]).then_inc(attn_loaded, 16)
            with sp.Fori(1, NPAIR // V1) as q:
                load(q, lambda v: x_pairs[bass.ds(q * V1 + v, 1)].rearrange("o q t -> (o q) t"))

            sp.wait_ge(zeroed3, 5)
            for n in range(NH):
                rows = slice(HD * n, HD * n + HD)
                sp.dma_start(fc1[rows, rows], fc1_w.rearrange("o i -> i o"), allow_slow_non_contiguous=True).then_inc(ff_loaded, 16)
                sp.dma_start(fc2[rows, rows], fc2_w.rearrange("o i -> i o"), allow_slow_non_contiguous=True).then_inc(ff_loaded, 16)
                sp.dma_start(fc2[NFEAT:NFEAT + 1, rows], fc2_b.rearrange("(o i) -> o i", o=1), allow_slow_non_contiguous=True).then_inc(ff_loaded, 16)
                sp.dma_start(b1[rows, :], fc1_b.rearrange("(i o) -> i o", o=1), allow_slow_non_contiguous=True).then_inc(ff_loaded, 16)
                sp.dma_start(gT[64 * (n % 2):64 * (n % 2) + 64, n // 2, NE * n:NE * n + NE],
                               gate_w[n].rearrange("e f -> f e"), allow_slow_non_contiguous=True).then_inc(ff_loaded, 16)
            sp.dma_start(whl[:, :, 0:NFEAT], hl_w.rearrange("n d h -> d n h"), allow_slow_non_contiguous=True).then_inc(ff_loaded, 16)
            sp.dma_start(whl[:, :, NFEAT], hl_b.rearrange("n d -> d n"), allow_slow_non_contiguous=True).then_inc(ff_loaded, 16)
            sp.dma_start(wq_s[:, :, :, :], wq.rearrange("n e o d -> o n e d"), allow_slow_non_contiguous=True).then_inc(ff_loaded, 16)
            sp.dma_start(wk_s[:, :, :], wk.rearrange("n o d -> o n d"), allow_slow_non_contiguous=True).then_inc(ff_loaded, 16)
            for n in range(NH):
                sp.dma_start(wvT[:, n, :], wv[n].rearrange("o d -> d o"), allow_slow_non_contiguous=True).then_inc(ff_loaded, 16)
            sp.dma_start(gbb[:, :], gate_b.rearrange("n e -> (n e)").partition_broadcast(TP), allow_slow_non_contiguous=True).then_inc(ff_loaded, 16)
            sp.dma_start(gam[:, 0, :], ln_g.partition_broadcast(TP)).then_inc(ff_loaded, 16)
            sp.dma_start(bet[:, 0, :], ln_b.partition_broadcast(TP)).then_inc(ff_loaded, 16)
            sp.dma_start(gam[:, 1, :], fnorm_g.partition_broadcast(TP)).then_inc(ff_loaded, 16)
            sp.dma_start(bet[:, 1, :], fnorm_b.partition_broadcast(TP)).then_inc(ff_loaded, 16)
            sp.dma_start(fgT[:, :], fgate_w.rearrange("n f -> f n"), allow_slow_non_contiguous=True).then_inc(ff_loaded, 16)
            def store(g, g2, quad):
                sp.wait_ge(ho_made, g + 1)
                sp.dma_start(quad.rearrange("b t f -> t b f"),
                             ho[0:NTOK, g2, :].rearrange("t (b f) -> t b f", b=4)).then_inc(out_done[g2], 16)

            with sp.Fori(0, NQUAD // 2) as q:
                for g2 in range(2):
                    store(2 * q + g2, g2, out[bass.ds(8 * q + 4 * g2, 4)])
            for g2 in range(2):
                sp.wait_ge(out_done[g2], 16 * NQUAD // 2)

        @block.gpsimd
        def _(pool):
            pool.memset(ident_w[:, :], 0.0).then_inc(zeroed, 1)
            pool.memset(neg_half[:, :], -0.5).then_inc(zeroed, 1)
            pool.memset(xs[:, :, NTIME:NTOK * KW], 0.0).then_inc(zeroed, 1)
            pool.wait_ge(zeroed, 3)
            pool.dma_start(ident_w[0:NFEAT, 128:129], tok_w.rearrange("o f -> f o")).then_inc(tok_loaded, 16)
            pool.dma_start(ident_w[NFEAT:128, 129:130], tok_w.rearrange("o f -> f o")).then_inc(tok_loaded, 16)
            pool.dma_start(tokb[:, :], tok_b.partition_broadcast(TP)).then_inc(tok_loaded, 16)
            pool.affine_select(out=ident, in_=ident, compare_op=ALU.not_equal, fill=1.0,
                               base=0, pattern=[[-1, 128]], channel_multiplier=1).then_inc(pool_own, 1)
            pool.wait_ge(pool_own, 1)
            pool.memset(h[64:TP, :, :], 0.0).then_inc(zeroed2, 1)
            pool.wait_ge(zeroed2, 4)

            def fold(q, v):
                p, w = V1 * q + v, xw[0:NTOK, v % 2, :, :]
                pool.wait_ge(x_weighted, p + 1)
                pool.tensor_tensor(w[:, 0:4, :], w[:, 0:4, :], w[:, 4:8, :], ALU.add).then_inc(x_fold, 1)

            def tokens(q):
                for v in range(V1):
                    fold(q, v)

            tokens(0)
            with pool.Fori(1, NPAIR // V1) as q:
                tokens(q)

            pool.memset(causA[:, :], 0.0).then_inc(causal_set, 1)
            pool.memset(causB[:, :, :], 0.0).then_inc(causal_set, 1)
            pool.wait_ge(causal_set, 2)
            cA = causA[:, :].rearrange("p (e t) -> p e t", e=NE)
            pool.affine_select(out=cA, in_=cA, compare_op=ALU.not_equal, fill=1.0, base=0,
                               pattern=[[0, NE], [-1, QB]], channel_multiplier=1).then_inc(causal_set, 1)
            pool.affine_select(out=causB[:, :, :], in_=causB[:, :, :], compare_op=ALU.is_ge, fill=MASKED, base=0,
                               pattern=[[0, NH], [-1, QB]], channel_multiplier=1).then_inc(causal_set, 1)
            pool.wait_ge(causal_set, 4)

            def ln_power(g):
                pool.wait_ge(ln_var, g + 1)
                if positive(g):
                    pool.wait_ge(ln_done, g)
                pool.tensor_tensor(ln_rs[:, 0:4], ln_ve[:, 0:4], neg_half[:, 0:4], ALU.pow).then_inc(ln_rstd, 1)

            def norm_p(m, v):
                pool.wait_ge(at_inverted, m + 1)
                p = pu[:, v % 4, :, :, :].rearrange("p a b u -> p (a b) u")
                pool.tensor_tensor(p, p, bcast(pr[:, v % 2, :, :].rearrange("p a b -> p (a b)"), 2, NTOK),
                                   ALU.mult).then_inc(at_normed, 1)

            def attention(q):
                for v in range(V2):
                    m, g = V2 * q + v, 2 * q + v // 4
                    if exists(m - 1, NBATCH):
                        norm_p(m - 1, (v - 1) % V2)
                    if v % 4 == 0 and exists(g + 1, NQUAD):
                        ln_power(g + 1)

            ln_power(0)
            attention(0)
            with pool.Fori(1, NBATCH // V2 - 1) as q:
                attention(q)
            attention(NBATCH // V2 - 1)
            attention(NBATCH // V2)

            def power3(g):
                pool.wait_ge(ln3_var, g + 1)
                pool.tensor_tensor(ln_rs[:, 0:4], ln_ve[:, 0:4], neg_half[:, 0:4], ALU.pow).then_inc(ln3_rstd, 1)

            def guard(m, v, g):
                pool.wait_ge(c_normed, m + 1)
                pool.wait_ge(f_va, g + 1)
                o = o3[:, v // 4, v % 4, :, :, :]
                pool.tensor_tensor(o, o, bcast(nz[:, v // 4, v % 4, :, :], 2, NE), ALU.mult).then_inc(c_guarded, 1)

            def gates(g, g2):
                pool.wait_ge(g_inv, g + 1)
                e = ge[:, g2, :].rearrange("p (a e) -> p a e", e=NE)
                pool.tensor_tensor(e, e, bcast(gr[:, g2, :], 2, NE), ALU.mult).then_inc(g_gs, 1)
                pool.wait_ge(g_gs, g + 1)
                o = o3[:, g2, :, :, :, :].rearrange("p b n e d -> p (b n e) d")
                pool.tensor_tensor(o, o, bcast(ge[:, g2, :], 2, HD), ALU.mult).then_inc(g_mul, 1)
                pool.wait_ge(g_mul, g + 1)
                o = o3[:, g2, :, :, :, :].rearrange("p b n e d -> p (b n) e d")
                pool.tensor_tensor(o[:, :, 0:2, :], o[:, :, 0:2, :], o[:, :, 2:4, :], ALU.add).then_inc(g_f1, 1)
                pool.wait_ge(g_f1, g + 1)
                y = yy[:, g2, :].rearrange("p (a d) -> p a d", d=HD)
                pool.tensor_tensor(y, o[:, :, 0, :], o[:, :, 1, :], ALU.add).then_inc(g_f2, 1)
                pool.wait_ge(g_f2, g + 1)
                y = yy[:, g2, :].rearrange("p (b c) -> p b c", b=4)
                pool.tensor_tensor(y, y, bcast(resid[:, :, :].rearrange("p n d -> p (n d)"), 1, 4), ALU.add).then_inc(y_made, 1)

            def norm_square(g, g2, k, cent, sq):
                pool.wait_ge(cent, g + 1)
                pool.tensor_tensor(ysq[:, g2, k, :], yc[:, g2, k, :], yc[:, g2, k, :], ALU.mult).then_inc(sq, 1)

            def norm_power(g, g2, k, eps, rstd):
                pool.wait_ge(eps, g + 1)
                pool.tensor_tensor(st[:, g2, k, 3, :], st[:, g2, k, 2, :], neg_half[:, :], ALU.pow).then_inc(rstd, 1)

            def norm_affine(g, g2, k, mul, mid, done, dst):
                pool.wait_ge(mul, g + 1)
                y = yc[:, g2, k, :].rearrange("p (a d) -> p a d", d=HD)
                pool.tensor_tensor(y, y, bcast(gam[:, k, :], 1, 16), ALU.mult).then_inc(mid, 1)
                pool.wait_ge(mid, g + 1)
                pool.tensor_tensor(dst[:, g2, :].rearrange("p (a d) -> p a d", d=HD), y, bcast(bet[:, k, :], 1, 16),
                                   ALU.add).then_inc(done, 1)

            def residual(g, g2):
                pool.wait_ge(t_made, g + 1)
                pool.tensor_tensor(ft[:, g2, :], ft[:, g2, :], fx[:, g2, :], ALU.add).then_inc(z_made, 1)

            def finish(g, g2, half):
                pool.wait_ge(fl_inv, g + 1)
                e = fe[:, g2, :].rearrange("p (b n) -> p b n", b=4)
                pool.tensor_tensor(e, e, bcast(fr[:, g2, :], 2, NH), ALU.mult).then_inc(fl_w, 1)
                pool.wait_ge(fl_w, g + 1)
                o = fo[:, g2, :].rearrange("p (a d) -> p a d", d=HD)
                pool.tensor_tensor(o, o, bcast(fe[:, g2, :], 2, HD), ALU.mult).then_inc(fo_mul, 1)
                pool.wait_ge(fo_mul, g + 1)
                if positive(half):
                    pool.wait_ge(out_done[g2], 16 * half)
                pool.tensor_tensor(ho[:, g2, :].rearrange("p (b f) -> p b f", b=4), fo[:, g2, :].rearrange("p (b f) -> p b f", b=4),
                                   h[:, bass.ds(4 * g, 4), :], ALU.add).then_inc(ho_made, 1)

            def experts(q):
                for v in range(V2):
                    m, g = V2 * q + v, 2 * q + v // 4
                    if v % 4 == 3 and exists(g + 2, NQUAD):
                        power3(g + 2)
                    if exists(m - 2, NBATCH):
                        guard(m - 2, (v - 2) % V2, 2 * q + (v - 2) // 4)
                    for s in (21, 18, 17, 16, 15, 12, 11, 10, 8):
                        G, g2 = 2 * q + (v - s) // 4, (v - s) // 4 % 2
                        if (v - s) % 4 or not exists(G, NQUAD):
                            continue
                        if s == 8:
                            gates(G, g2)
                        if s == 10:
                            norm_square(G, g2, 0, y_cent, y_sq)
                        if s == 11:
                            norm_power(G, g2, 0, y_eps, y_rstd)
                        if s == 12:
                            norm_affine(G, g2, 0, y_mul, y_gam, fx_made, fx)
                        if s == 15:
                            residual(G, g2)
                        if s == 16:
                            norm_square(G, g2, 1, z_cent, z_sq)
                        if s == 17:
                            norm_power(G, g2, 1, z_eps, z_rstd)
                        if s == 18:
                            norm_affine(G, g2, 1, z_mul, z_gam, fo_made, fo)
                        if s == 21:
                            finish(G, g2, q + ((v - s) // 4 - g2) // 2)

            power3(0)
            power3(1)
            experts(0)
            experts(1)
            experts(2)
            experts(3)
            with pool.Fori(4, NBATCH // V2 - 1) as q:
                experts(q)
            for q in range(NBATCH // V2 - 1, NBATCH // V2 + 3):
                experts(q)

        @block.tensor
        def _(pe):
            def turn(q, v):
                p = V1 * q + v
                pe.wait_ge(x_loaded[v], 16 * q + 16)
                if positive(p - 1):
                    pe.wait_ge(x_weighted, p - 1)
                for k in range(KW):
                    mm = pe.matmul(turned(v % 2)[:, k, 0:130], xs[:, v, k:NTOK * KW:KW], ident_w[:, :],
                                   start=True, stop=True)
                mm.then_inc(x_turned, 1)

            def tokens(q):
                for v in range(V1):
                    turn(q, v)

            pe.wait_ge(pool_own, 1)
            pe.wait_ge(tok_loaded, 16 * 3)
            tokens(0)
            with pe.Fori(1, NPAIR // V1) as q:
                tokens(q)

            pe.wait_ge(x_weighted, NPAIR)
            pe.wait_ge(attn_loaded, 16 * 4)
            pe.wait_ge(zeroed2, 4)
            for hd in range(HEADS):
                mm = pe.matmul(psum[0:NFEAT, 0, NFEAT * hd:NFEAT * (hd + 1)], q_w[:, hd, :], k_w[:, hd, :],
                               start=True, stop=True)
            mm.then_inc(g_made, 1)
            pe.wait_ge(g_ready, 1)

            def turn_x(g, g2):
                pe.wait_ge(ln_done, g + 1)
                if positive(4 * g):
                    pe.wait_ge(at_q, 4 * g)
                for b in range(4):
                    mm = pe.transpose(at_Q[:, b, :], xn[:, g2, b, :, :].rearrange("p a f -> p (a f)"), ident[0:TP, 0:TP])
                mm.then_inc(at_turned, 1)

            def project(g, g2, hp):
                if hp == 0:
                    pe.wait_ge(at_xT, g + 1)
                else:
                    pe.wait_ge(at_q, 4 * g + hp)
                pe.matmul(at_Q[:, :, 0:NTOK], g_w[:, 128 * hp:128 * (hp + 1)], xT[:, g2, :, 0, :],
                          start=True, stop=True).then_inc(at_projected, 1)

            def score(m, g, v):
                b, g2 = v % 4, v // 4
                if b == 0:
                    pe.wait_ge(at_q, 4 * g + 4)
                if positive(m - 1):
                    pe.wait_ge(at_shifted, m - 1)
                q = qs[:, g2, b, :, :].rearrange("p a t -> p (a t)")
                for t in range(NT):
                    mm = pe.matmul(at_S(v)[:, t, :], q[:, 128 * t:128 * (t + 1)],
                                   xT[:, g2, b, :, :].rearrange("p a u -> p (a u)"), start=True, stop=True)
                mm.then_inc(at_scored, 1)

            def turn_p(m, v, par):
                pe.wait_ge(at_normed, m + 1)
                if positive(2 * m + par):
                    pe.wait_ge(at_pT, 2 * m + par)
                for t in range(NT):
                    mm = pe.transpose(at_P[:, 128 * t:128 * (t + 1)], pu[:, v % 4, t, par, :], ident)
                mm.then_inc(at_pturned, 1)

            def mix(m, v, par):
                pe.wait_ge(at_pT, 2 * m + par + 1)
                if par == 0 and positive(m):
                    pe.wait_ge(at_cT, m)
                pe.matmul(at_C[64 * par:64 * par + 64, :], xn[0:NTOK, v // 4, v % 4, 0, :], pT[:, par, :],
                          start=True, stop=True).then_inc(at_mixed, 1)

            def give_out(m, v):
                pe.wait_ge(at_cT, m + 1)
                if positive(m):
                    pe.wait_ge(at_added, m)
                for hp in range(HP):
                    mm = pe.matmul(at_O, cT[:, v % 2, hp, :], vo_w[:, hp, :], start=(hp == 0), stop=(hp == HP - 1))
                mm.then_inc(at_out, 1)

            def attention(q):
                for v in range(V2):
                    m, g, g2 = V2 * q + v, 2 * q + v // 4, (v // 4 + 1) % 2
                    more = exists(g + 1, NQUAD)
                    v2, v3 = (v - 2) % V2, (v - 3) % V2
                    if exists(m - 2, NBATCH):
                        turn_p(m - 2, v2, 0)
                    if v % 4 == 3 and more:
                        project(g + 1, g2, 1)
                    if exists(m, NBATCH):
                        score(m, g, v)
                    if exists(m - 2, NBATCH):
                        turn_p(m - 2, v2, 1)
                    if v % 4 == 2 and more:
                        turn_x(g + 1, g2)
                    if v % 4 == 3 and more:
                        project(g + 1, g2, 2)
                    if exists(m - 3, NBATCH):
                        give_out(m - 3, v3)
                    if exists(m - 2, NBATCH):
                        mix(m - 2, v2, 0)
                    if v % 4 == 3 and more:
                        project(g + 1, g2, 3)
                    if exists(m - 2, NBATCH):
                        mix(m - 2, v2, 1)
                    if v % 4 == 2 and more:
                        project(g + 1, g2, 0)

            turn_x(0, 0)
            for hp in range(HP):
                project(0, 0, hp)
            attention(0)
            with pe.Fori(1, NBATCH // V2 - 1) as q:
                attention(q)
            attention(NBATCH // V2 - 1)
            attention(NBATCH // V2)

            pe.wait_ge(at_added, NBATCH)
            pe.wait_ge(ff_loaded, FF_LOADS)
            pe.wait_ge(causal_set, 4)
            for n in range(NH):
                for e in range(NE):
                    c = HD * (NE * n + e)
                    mm = pe.matmul(psum[0:HD, 0, c:c + HD], wq_s[:, n, e, :], wk_s[:, n, :], start=True, stop=True)
            mm.then_inc(w_made, 1)
            pe.wait_ge(w_read, 1)
            for n in range(NH):
                pe.matmul(psum[0:NFEAT + 1, 0, 64 * n:64 * n + 64], whl[:, n, :], m_s[:, n, :, :].rearrange("p e d -> p (e d)"),
                          start=True, stop=True)
                pe.matmul(psum[0:NFEAT + 1, 1, HD * n:HD * n + HD], whl[:, n, :], wvT[:, n, :], start=True, stop=True)
                mm = pe.matmul(psum[0:NFEAT + 1, 1, 64 + HD * n:64 + HD * n + HD], whl[:, n, :], ident[0:HD, 0:HD],
                               start=True, stop=True)
            mm.then_inc(w_made, 1)
            pe.wait_ge(w_read, 4)

            def front_turn(g, g2):
                if positive(g):
                    pe.wait_ge(f_qc, 4 * g)
                pe.wait_ge(ln3_done, g + 1)
                pe.transpose(F_[:, 0:TP], xn3[:, 0:2, :].rearrange("p b f -> p (b f)"), ident[0:TP, 0:TP])
                for b in range(1, 4):
                    mm = pe.transpose(F_[0:NFEAT, TP * b:TP * b + TP], xn3[:, b, :], ident[0:TP, 0:TP])
                mm.then_inc(f_turned, 1)

            def front_sx(g, g2):
                pe.wait_ge(f_xT, g + 1)
                pe.matmul(F_[:, 0:4 * TP], wsx[:, :, :].rearrange("p n d -> p (n d)"),
                          x3T[:, :, :].rearrange("p b t -> p (b t)"), start=True, stop=True).then_inc(f_sx, 1)

            def front_tok(g, g2):
                pe.wait_ge(f_diag, g + 1)
                for b in range(4):
                    mm = pe.matmul(F_[0:TP, 128 * b:128 * b + 128], x3T[:, b, :], wtok[:, :, :, :].rearrange("p a n d -> p (a n d)"),
                                   start=True, stop=True)
                mm.then_inc(f_tok, 1)

            def front_q(g, g2, e):
                if e == 0:
                    pe.wait_ge(f_va, g + 1)
                else:
                    pe.wait_ge(f_qc, 4 * g + e)
                pe.matmul(F_[:, 0:4 * TP], aq[:, e, :, :].rearrange("p n d -> p (n d)"),
                          x3T[:, :, :].rearrange("p b t -> p (b t)"), start=True, stop=True).then_inc(f_q, 1)

            def score3(m, g, v):
                b, g2 = v % 4, v // 4
                if b == 0:
                    pe.wait_ge(f_qc, 4 * g + 4)
                if positive(m):
                    pe.wait_ge(s_shifted, m)
                for j, start in ((2, True), (1, True), (0, False)):
                    pe.matmul(SJ[j], q3[:, g2, b, j, :, :].rearrange("p e t -> p (e t)"), sxd[:, g2, b, :, 0:WIDTH[j]],
                              start=start, stop=False, skip_group_check=True)
                for j in range(NJ):
                    w = WIDTH[j] - QB * j
                    mm = pe.matmul(SJ[j][:, :, QB * j:WIDTH[j]], causA[:, :], causB[:, :, 0:w],
                                   start=False, stop=True, skip_group_check=True)
                mm.then_inc(s_scored, 1)

            def turn_p3(m, v, n):
                if n == 0:
                    pe.wait_ge(s_exped, m + 1)
                if positive(4 * m + n - 1):
                    pe.wait_ge(p_copied, 4 * m + n - 1)
                for j in range(NJ):
                    mm = pe.transpose(P3(n)[:, 128 * j:128 * j + 128], pu3[:, v % 2, n, j, :], ident)
                mm.then_inc(p_turned, 1)

            def mix3(m, v, n):
                pe.wait_ge(p_copied, 4 * m + n + 1)
                if n == 0 and positive(m):
                    pe.wait_ge(c_normed, m)
                for e in range(NE):
                    mm = pe.matmul(C3[:, NE * n + e, :], pT3[:, n, e, :, :].rearrange("p j t -> p (j t)"),
                                   va[0:NTOK, v // 4, v % 4, n, :], start=True, stop=True)
                mm.then_inc(p_mixed, 1)

            def gate_turn(g, g2, half):
                if half == 0:
                    pe.wait_ge(c_guarded, 4 * g + 4)
                    if positive(g):
                        pe.wait_ge(g_added, g)
                else:
                    pe.wait_ge(r0_copied, 2 * g + 1)
                for b in range(2):
                    o = o3[:, g2, 2 * half + b, :, :, :].rearrange("p n e d -> p (n e d)")
                    for hp in range(2):
                        mm = pe.transpose(R0[:, TP * (2 * b + hp):TP * (2 * b + hp + 1)], o[:, 128 * hp:128 * hp + 128],
                                          ident[0:TP, 0:TP])
                mm.then_inc(r0_turned, 1)

            def gate_logits(g, g2):
                pe.wait_ge(r0_copied, 2 * g + 2)
                for b in range(4):
                    for hp in range(2):
                        mm = pe.matmul(R0[0:TP, 16 * b:16 * b + 16], oT[:, b // 2, 2 * (b % 2) + hp, :], gT[:, hp, :],
                                       start=(hp == 0), stop=(hp == 1))
                mm.then_inc(r0_gated, 1)

            def turn_rest(g, g2, src, ready, done):
                pe.wait_ge(ready, g + 1)
                pe.transpose(R1[:, 0:TP], src[:, g2, 0:128], ident[0:TP, 0:TP])
                for b in range(1, 4):
                    mm = pe.transpose(R1[0:NFEAT, TP * b:TP * b + TP], src[:, g2, 64 * b:64 * b + 64], ident[0:TP, 0:TP])
                mm.then_inc(done, 1)

            def layer1(g, g2):
                pe.wait_ge(r1_fxc, g + 1)
                pe.matmul(R1[:, 0:4 * TP], fc1[:, :], fxT[:, g2, :], start=True, stop=True).then_inc(r1_fc1, 1)

            def layer2(g, g2):
                pe.wait_ge(h_masked, g + 1)
                for b in range(4):
                    mm = pe.matmul(R1[0:TP, 64 * b:64 * b + 64], hxm[:, g2, TP * b:TP * b + TP], fc2[:, :],
                                   start=True, stop=True)
                mm.then_inc(r1_fc2, 1)

            def head_logits(g, g2):
                pe.wait_ge(r1_foc, g + 1)
                for b in range(4):
                    mm = pe.matmul(R1[0:TP, 4 * b:4 * b + 4], foT[:, g2, TP * b:TP * b + TP], fgT[:, :],
                                   start=True, stop=True)
                mm.then_inc(r1_fl, 1)

            def experts(q):
                for v in range(V2):
                    m, g, f2 = V2 * q + v, 2 * q + v // 4, (v // 4 + 1) % 2
                    more = exists(g + 1, NQUAD)

                    def rest(s):
                        G, g2 = 2 * q + (v - s) // 4, (v - s) // 4 % 2
                        if (v - s) % 4 or not exists(G, NQUAD):
                            return
                        if s == 6:
                            gate_turn(G, g2, 0)
                            gate_turn(G, g2, 1)
                        if s == 7:
                            gate_logits(G, g2)
                        if s == 13:
                            if positive(G - 1):
                                pe.wait_ge(fl_shifted, G - 1)
                            turn_rest(G, g2, fx, fx_made, r1_fxt)
                        if s == 14:
                            layer2(G, g2)
                        if s == 19:
                            last = min(G + 2, NQUAD) if isinstance(G, int) else G + 2
                            pe.wait_ge(t_made, last)
                            turn_rest(G, g2, fo, fo_made, r1_fot)
                        if s == 20:
                            head_logits(G, g2)

                    if exists(m, NBATCH):
                        score3(m, g, v)
                    rest(20)
                    rest(13)
                    rest(14)
                    rest(7)
                    if exists(m - 1, NBATCH):
                        turn_p3(m - 1, (v - 1) % V2, 0)
                        turn_p3(m - 1, (v - 1) % V2, 1)
                    if v % 4 == 1 and more:
                        front_sx(g + 1, f2)
                    rest(6)
                    if exists(m - 1, NBATCH):
                        mix3(m - 1, (v - 1) % V2, 0)
                        turn_p3(m - 1, (v - 1) % V2, 2)
                    if v % 4 == 2 and more:
                        front_q(g + 1, f2, 0)
                    if v % 4 == 3 and more:
                        front_q(g + 1, f2, 2)
                    G13 = 2 * q + (v - 13) // 4
                    if v % 4 == 1 and exists(G13, NQUAD):
                        layer1(G13, (v - 13) // 4 % 2)
                    if exists(m - 1, NBATCH):
                        mix3(m - 1, (v - 1) % V2, 1)
                        turn_p3(m - 1, (v - 1) % V2, 3)
                    if v % 4 == 1 and more:
                        front_tok(g + 1, f2)
                    if exists(m - 1, NBATCH):
                        mix3(m - 1, (v - 1) % V2, 2)
                    if v % 4 == 0 and more:
                        front_turn(g + 1, f2)
                    if v % 4 == 2 and more:
                        front_q(g + 1, f2, 1)
                    if v % 4 == 3 and more:
                        front_q(g + 1, f2, 3)
                    rest(19)
                    if exists(m - 1, NBATCH):
                        mix3(m - 1, (v - 1) % V2, 3)

            front_turn(0, 0)
            front_sx(0, 0)
            front_tok(0, 0)
            for e in range(NE):
                front_q(0, 0, e)
            experts(0)
            experts(1)
            experts(2)
            experts(3)
            with pe.Fori(4, NBATCH // V2 - 1) as q:
                experts(q)
            for q in range(NBATCH // V2 - 1, NBATCH // V2 + 3):
                experts(q)

        @block.scalar
        def _(act):
            def exp_tok(q, v):
                p = V1 * q + v
                act.wait_ge(tok_shifted, p + 1)
                act.activation(tok_e[0:NTOK, v % 2, :], tok_d[0:NTOK, v % 2, :], ACT.Exp).then_inc(tok_exped, 1)

            def store_h(q, v):
                p = V1 * q + v
                act.wait_ge(x_summed, p + 1)
                act.wait_ge(tok_inverted, p + 1)
                for b in range(2):
                    ins = act.activation(h[0:NTOK, bass.ds(2 * V1 * q + (2 * v + b), 1), :].rearrange("p o f -> p (o f)"),
                                         x_sum[0:NTOK, v % 2, NFEAT * b:NFEAT * (b + 1)], ACT.Copy,
                                         scale=tok_r[0:NTOK, v % 2, b:b + 1])
                ins.then_inc(h_pooled, 1)

            def tokens(q):
                for v in range(V1):
                    exp_tok(q, v)
                    if exists(V1 * q + v - 2, NPAIR):
                        store_h(q if v > 1 else q - 1, (v - 2) % V1)

            tokens(0)
            with act.Fori(1, NPAIR // V1) as q:
                tokens(q)
            store_h(NPAIR // V1 - 1, V1 - 2)
            store_h(NPAIR // V1 - 1, V1 - 1)

            act.wait_ge(g_made, 1)
            act.activation(g_w[0:NFEAT, :], psum[0:NFEAT, 0, :], ACT.Copy, scale=float(NFEAT) ** -0.5).then_inc(g_ready, 1)

            def copy_xT(g, g2):
                act.wait_ge(at_turned, g + 1)
                for par in range(2):
                    rows = slice(64 * par, 64 * par + 64)
                    ins = act.activation(xT[rows, g2, :, par, :], at_Q[rows, :, 0:NTOK], ACT.Copy)
                ins.then_inc(at_xT, 1)

            def copy_q(g, g2, hp):
                act.wait_ge(at_projected, 4 * g + hp + 1)
                act.activation(qs[:, g2, :, hp, 0:NTOK], at_Q[:, :, 0:NTOK], ACT.Copy).then_inc(at_q, 1)

            def exp_s(m, v):
                act.wait_ge(at_shifted, m + 1)
                p = pu[:, v % 4, :, :, :].rearrange("p a b u -> p (a b u)")
                act.activation(p, p, ACT.Exp).then_inc(at_exped, 1)

            def copy_pT(m, par):
                act.wait_ge(at_pturned, 2 * m + par + 1)
                if positive(2 * m + par - 1):
                    act.wait_ge(at_mixed, 2 * m + par - 1)
                act.activation(pT[:, par, :], at_P, ACT.Copy).then_inc(at_pT, 1)

            def copy_cT(m, v):
                act.wait_ge(at_mixed, 2 * m + 2)
                if positive(m - 1):
                    act.wait_ge(at_out, m - 1)
                act.activation(cT[:, v % 2, :, :].rearrange("p a t -> p (a t)"), at_C, ACT.Copy).then_inc(at_cT, 1)

            def attention(q):
                for v in range(V2):
                    m, g, g2 = V2 * q + v, 2 * q + v // 4, (v // 4 + 1) % 2
                    more = exists(g + 1, NQUAD)
                    if exists(m - 2, NBATCH):
                        copy_pT(m - 2, 0)
                    if exists(m - 3, NBATCH):
                        copy_cT(m - 3, (v - 3) % V2)
                    if v % 4 == 3 and more:
                        copy_q(g + 1, g2, 1)
                    if exists(m - 2, NBATCH):
                        copy_pT(m - 2, 1)
                    if v % 4 == 2 and more:
                        copy_xT(g + 1, g2)
                    if v % 4 == 3 and more:
                        copy_q(g + 1, g2, 2)
                    if exists(m, NBATCH):
                        exp_s(m, v)
                    if v % 4 == 3 and more:
                        copy_q(g + 1, g2, 3)
                    if v % 4 == 2 and more:
                        copy_q(g + 1, g2, 0)

            copy_xT(0, 0)
            for hp in range(HP):
                copy_q(0, 0, hp)
            attention(0)
            with act.Fori(1, NBATCH // V2 - 1) as q:
                attention(q)
            attention(NBATCH // V2 - 1)
            attention(NBATCH // V2)

            act.wait_ge(w_made, 1)
            act.activation(m_s[:, :, :, :].rearrange("p n e d -> p (n e d)"), psum[0:HD, 0, 0:256], ACT.Copy,
                           scale=float(HD) ** 0.5).then_inc(w_read, 1)
            act.wait_ge(w_made, 2)
            act.activation(aq[:, :, :, 0:HD].rearrange("p e n d -> p n e d"),
                           psum[0:NFEAT + 1, 0, 0:256].rearrange("p (n e d) -> p n e d", n=NH, e=NE), ACT.Copy).then_inc(w_read, 1)
            act.activation(wtok[:, :, :, :].rearrange("p a n d -> p (a n d)"), psum[0:NFEAT + 1, 1, 0:128], ACT.Copy).then_inc(w_read, 1)
            act.activation(wsx[:, :, 0:HD], psum[0:NFEAT + 1, 1, 64:128].rearrange("p (n d) -> p n d", n=NH), ACT.Copy).then_inc(w_read, 1)

            def front_xT(g):
                act.wait_ge(f_turned, g + 1)
                act.activation(x3T[0:NFEAT, :, :].rearrange("p b t -> p (b t)"), F_[0:NFEAT, 0:4 * TP], ACT.Copy).then_inc(f_xT, 1)

            def front_diag(g, g2):
                act.wait_ge(f_sx, g + 1)
                for n in range(NH):
                    rows = slice(32 * n, 32 * n + 32)
                    ins = act.activation(sxd[rows, g2, :, n, :], F_[rows, 0:4 * TP].rearrange("p (b t) -> p b t", b=4)[:, :, 0:NTOK],
                                         ACT.Copy)
                ins.then_inc(f_diag, 1)

            def front_q(g, g2, e):
                act.wait_ge(f_q, 4 * g + e + 1)
                act.activation(q3[:, g2, :, :, e, :], F_[:, 0:4 * TP].rearrange("p (b j t) -> p b j t", b=4, j=NJ),
                               ACT.Copy).then_inc(f_qc, 1)

            def exp3(m, v):
                act.wait_ge(s_shifted, m + 1)
                for j in range(NJ):
                    p = pu3[:, v % 2, :, j, 0:WIDTH[j]]
                    ins = act.activation(p, p, ACT.Exp)
                ins.then_inc(s_exped, 1)

            def copy_p3(m, n):
                act.wait_ge(p_turned, 4 * m + n + 1)
                if positive(4 * m + n - 3):
                    act.wait_ge(p_mixed, 4 * m + n - 3)
                act.activation(pT3[:, n, :, :, :].rearrange("p e j t -> p j e t"), P3(n).rearrange("p (j e t) -> p j e t", j=NJ, e=NE),
                               ACT.Copy).then_inc(p_copied, 1)

            def experts(q):
                for v in range(V2):
                    m, g, f2 = V2 * q + v, 2 * q + v // 4, (v // 4 + 1) % 2
                    more = exists(g + 1, NQUAD)

                    def rest(s):
                        G, g2 = 2 * q + (v - s) // 4, (v - s) // 4 % 2
                        if (v - s) % 4 or not exists(G, NQUAD):
                            return
                        if s == 6:
                            for half in range(2):
                                act.wait_ge(r0_turned, 2 * G + half + 1)
                                act.activation(oT[:, half, :, :].rearrange("p a t -> p (a t)"), R0[:, 0:4 * TP],
                                               ACT.Copy).then_inc(r0_copied, 1)
                        if s == 7:
                            act.wait_ge(g_shifted, G + 1)
                            act.activation(ge[:, g2, :], gl[:, g2, :], ACT.Exp).then_inc(g_exped, 1)
                        if s == 13:
                            act.wait_ge(r1_fxt, G + 1)
                            act.activation(fxT[:, g2, :], R1[0:NFEAT, 0:4 * TP], ACT.Copy).then_inc(r1_fxc, 1)
                        if s == 19:
                            act.wait_ge(r1_fot, G + 1)
                            act.activation(foT[:, g2, :], R1[0:NFEAT, 0:4 * TP], ACT.Copy).then_inc(r1_foc, 1)
                        if s == 20:
                            act.wait_ge(fl_shifted, G + 1)
                            act.activation(fe[:, g2, :], fl[:, g2, :], ACT.Exp).then_inc(fl_exped, 1)

                    rest(13)
                    if exists(m - 1, NBATCH):
                        copy_p3(m - 1, 0)
                        copy_p3(m - 1, 1)
                    if v % 4 == 1 and more:
                        front_diag(g + 1, f2)
                    rest(6)
                    if exists(m - 1, NBATCH):
                        copy_p3(m - 1, 2)
                    if v % 4 == 2 and more:
                        front_q(g + 1, f2, 0)
                    if v % 4 == 3 and more:
                        front_q(g + 1, f2, 2)
                    G13 = 2 * q + (v - 13) // 4
                    if v % 4 == 1 and exists(G13, NQUAD):
                        g2 = (v - 13) // 4 % 2
                        act.wait_ge(r1_fc1, G13 + 1)
                        act.activation(hx[:, g2, :], R1[0:NFEAT, 0:4 * TP], ACT.Relu, bias=b1[:, :]).then_inc(r1_hx, 1)
                    if exists(m - 1, NBATCH):
                        copy_p3(m - 1, 3)
                    if exists(m, NBATCH):
                        exp3(m, v)
                    if v % 4 == 0 and more:
                        front_xT(g + 1)
                    if v % 4 == 2 and more:
                        front_q(g + 1, f2, 1)
                    if v % 4 == 3 and more:
                        front_q(g + 1, f2, 3)
                    rest(19)
                    rest(7)
                    rest(20)

            front_xT(0)
            front_diag(0, 0)
            for e in range(NE):
                front_q(0, 0, e)
            experts(0)
            experts(1)
            experts(2)
            experts(3)
            with act.Fori(4, NBATCH // V2 - 1) as q:
                experts(q)
            for q in range(NBATCH // V2 - 1, NBATCH // V2 + 3):
                experts(q)

        @block.vector
        def _(dve):
            def shift_tok(q, v):
                p, v2 = V1 * q + v, v % 2
                dve.wait_ge(x_turned, p + 1)
                s = tok_s[0:NTOK, v2, :].rearrange("p (k b) -> p k b", b=2)
                dve.tensor_scalar(s, turned(v2)[:, :, 128:130], tokb[0:NTOK, :], None, ALU.add).then_inc(tok_scored, 1)
                dve.wait_ge(tok_scored, p + 1)
                dve.tensor_reduce(tok_m[0:NTOK, v2, :], s.rearrange("p k b -> p b k"), AX.X, ALU.max).then_inc(tok_maxed, 1)
                dve.wait_ge(tok_maxed, p + 1)
                dve.tensor_tensor(tok_d[0:NTOK, v2, :].rearrange("p (k b) -> p k b", b=2), s,
                                  bcast(tok_m[0:NTOK, v2, :], 1, KW), ALU.subtract).then_inc(tok_shifted, 1)

            def weigh(q, v):
                p, v2 = V1 * q + v, v % 2
                dve.wait_ge(tok_exped, p + 1)
                e = tok_e[0:NTOK, v2, :]
                dve.tensor_reduce(tok_l[0:NTOK, v2, :], e.rearrange("p (k b) -> p b k", b=2), AX.X,
                                  ALU.add).then_inc(tok_summed, 1)
                dve.tensor_tensor(xw[0:NTOK, v2, :, :].rearrange("p k (b f) -> p k b f", b=2),
                                  turned(v2)[:, :, 0:128].rearrange("p k (b f) -> p k b f", b=2),
                                  bcast(e.rearrange("p (k b) -> p k b", b=2), 3, NFEAT), ALU.mult).then_inc(x_weighted, 1)
                dve.wait_ge(tok_summed, p + 1)
                if positive(p - 1):
                    dve.wait_ge(h_pooled, p - 1)
                dve.reciprocal(tok_r[0:NTOK, v2, :], tok_l[0:NTOK, v2, :]).then_inc(tok_inverted, 1)

            def sum_tok(q, v):
                p, v2 = V1 * q + v, v % 2
                dve.wait_ge(x_fold, p + 1)
                dve.tensor_reduce(x_sum[0:NTOK, v2, :], xw[0:NTOK, v2, 0:4, :].rearrange("p k c -> p c k"), AX.X,
                                  ALU.add).then_inc(x_summed, 1)

            def tokens(q):
                for v in range(V1):
                    shift_tok(q, v)
                    if exists(V1 * q + v - 1, NPAIR):
                        sum_tok(q if v else q - 1, (v - 1) % V1)
                    weigh(q, v)

            dve.memset(xT[:, :, :, :, :], 0.0).then_inc(zeroed2, 1)
            dve.memset(qs[:, :, :, :, NTOK:TP], 0.0).then_inc(zeroed2, 1)
            dve.memset(g_w[64:128, :], 0.0).then_inc(zeroed2, 1)
            dve.memset(gT[:, :, :], 0.0).then_inc(zeroed3, 1)
            dve.memset(fc1[:, :], 0.0).then_inc(zeroed3, 1)
            dve.memset(fc2[:, :], 0.0).then_inc(zeroed3, 1)
            dve.memset(aq[:, :, :, :], 0.0).then_inc(zeroed3, 1)
            dve.memset(wsx[:, :, :], 0.0).then_inc(zeroed3, 1)
            dve.memset(sxd[:, :, :, :, :], 0.0).then_inc(zeroed4, 1)
            dve.memset(pu3[:, :, :, :, :], 0.0).then_inc(zeroed4, 1)
            dve.memset(va[:, :, :, :, HD:HD + 1], 1.0).then_inc(zeroed4, 1)
            dve.memset(x3T[NFEAT:NFEAT + 1, :, :], 1.0).then_inc(zeroed4, 1)
            dve.memset(hxm[NFEAT:NFEAT + 1, :, :], 1.0).then_inc(zeroed4, 1)
            dve.wait_ge(tok_loaded, 16 * 3)
            tokens(0)
            with dve.Fori(1, NPAIR // V1) as q:
                tokens(q)
            sum_tok(NPAIR // V1 - 1, V1 - 1)

            dve.wait_ge(h_pooled, NPAIR)
            dve.wait_ge(zeroed2, 4)

            def ln_stats(g, part):
                if part == 0:
                    for b in range(4):
                        ins = dve.bn_stats(ln_bn[:, b, :], h[:, bass.ds(4 * g + b, 1), :].rearrange("p o f -> p (o f)"))
                    ins.then_inc(ln_stat, 1)
                else:
                    dve.wait_ge(ln_stat, g + 1)
                    dve.memset(spot[:, :], 0.0)
                    for b in range(4):
                        ins = dve.bn_aggr(ln_mv[:, b, :], ln_bn[:, b, :])
                    ins.then_inc(ln_agg, 1)
                    dve.wait_ge(ln_agg, g + 1)
                    dve.tensor_scalar(ln_ve[:, 0:4], ln_mv[:, 0:4, 1], EPS_LN, None, ALU.add).then_inc(ln_var, 1)

            def ln_apply(g, g2):
                dve.wait_ge(ln_rstd, g + 1)
                if positive(8 * (g - 1)):
                    dve.wait_ge(at_mixed, 8 * (g - 1))
                for b in range(4):
                    ins = dve.tensor_scalar(xn[:, g2, b, :, :], h[:, bass.ds(4 * g + b, 1), :].broadcast_to([TP, 2, NFEAT]),
                                            ln_mv[:, b, 0:1], ln_rs[:, b:b + 1], ALU.subtract, ALU.mult)
                ins.then_inc(ln_done, 1)

            def shift(m, v):
                s = at_S(v).rearrange("p a (b u) -> p a b u", b=2)
                dve.wait_ge(at_scored, m + 1)
                dve.tensor_reduce(mx[:, v % 2, :, :], s, AX.X, ALU.max).then_inc(at_maxed, 1)
                dve.wait_ge(at_maxed, m + 1)
                if positive(2 * (m - 4) + 2):
                    dve.wait_ge(at_pturned, 2 * (m - 4) + 2)
                dve.tensor_tensor(pu[:, v % 4, :, :, :], s, bcast(mx[:, v % 2, :, :], 3, NTOK), ALU.subtract)\
                   .then_inc(at_shifted, 1)

            def sums(m, v):
                dve.wait_ge(at_exped, m + 1)
                dve.tensor_reduce(pl[:, v % 2, :, :], pu[:, v % 4, :, :, :], AX.X, ALU.add).then_inc(at_summed, 1)
                dve.wait_ge(at_summed, m + 1)
                if positive(m - 1):
                    dve.wait_ge(at_normed, m - 1)
                dve.reciprocal(pr[:, v % 2, :, :], pl[:, v % 2, :, :]).then_inc(at_inverted, 1)

            def add_out(m):
                dve.wait_ge(at_out, m + 1)
                hm = h[:, bass.ds(m, 1), :].rearrange("p o f -> p (o f)")
                dve.tensor_tensor(hm, at_O, hm, ALU.add).then_inc(at_added, 1)

            def attention(q):
                for v in range(V2):
                    m, g, g2 = V2 * q + v, 2 * q + v // 4, (v // 4 + 1) % 2
                    more = exists(g + 1, NQUAD)
                    if v % 4 == 2 and more:
                        ln_apply(g + 1, g2)
                    if exists(m - 1, NBATCH):
                        sums(m - 1, (v - 1) % V2)
                    if exists(m, NBATCH):
                        shift(m, v)
                    if v % 4 == 0 and more:
                        ln_stats(g + 1, 0)
                        ln_stats(g + 1, 1)
                    if exists(m - 3, NBATCH):
                        add_out(m - 3)

            ln_stats(0, 0)
            ln_stats(0, 1)
            ln_apply(0, 0)
            attention(0)
            with dve.Fori(1, NBATCH // V2 - 1) as q:
                attention(q)
            attention(NBATCH // V2 - 1)
            attention(NBATCH // V2)

            dve.wait_ge(ff_loaded, FF_LOADS)

            def stats3(g):
                for b in range(4):
                    ins = dve.bn_stats(ln_bn[:, b, :], h[:, bass.ds(4 * g + b, 1), :].rearrange("p o f -> p (o f)"))
                ins.then_inc(ln3_stat, 1)
                dve.wait_ge(ln3_stat, g + 1)
                dve.memset(spot[:, :], 0.0)
                for b in range(4):
                    ins = dve.bn_aggr(ln_mv[:, b, :], ln_bn[:, b, :])
                ins.then_inc(ln3_agg, 1)
                dve.wait_ge(ln3_agg, g + 1)
                dve.tensor_scalar(ln_ve[:, 0:4], ln_mv[:, 0:4, 1], EPS_LN, None, ALU.add).then_inc(ln3_var, 1)

            def apply3(g):
                dve.wait_ge(ln3_rstd, g + 1)
                if positive(g):
                    dve.wait_ge(f_turned, g)
                for b in range(4):
                    ins = dve.tensor_scalar(xn3[:, b, :], h[:, bass.ds(4 * g + b, 1), :].rearrange("p o f -> p (o f)"),
                                            ln_mv[:, b, 0:1], ln_rs[:, b:b + 1], ALU.subtract, ALU.mult)
                ins.then_inc(ln3_done, 1)

            def front_va(g, g2):
                dve.wait_ge(f_tok, g + 1)
                if positive(16 * (g - 1)):
                    dve.wait_ge(p_mixed, 16 * (g - 1))
                    dve.wait_ge(c_guarded, 4 * (g - 1))
                f = F_[0:TP, :].rearrange("p (b a n d) -> p b a n d", b=4, a=2, n=NH)
                for b in range(4):
                    dve.tensor_copy(va[:, g2, b, :, 0:HD], f[:, b, 0, :, :])
                if isinstance(g, int) and g == 0:
                    for n in range(NH):
                        ins = dve.tensor_copy(resid[:, n, :], f[:, n, 1, n, :])
                    ins.then_inc(f_resid, 1)
                dve.tensor_scalar(nz[:, g2, :, :, :].rearrange("p b n d -> p b (n d)"),
                                  F_[0:TP, :].rearrange("p (b c) -> p b c", b=4)[:, :, 64:128], 0.0, None,
                                  ALU.not_equal).then_inc(f_va, 1)

            def shift3(m, v):
                dve.wait_ge(s_scored, m + 1)
                for j in range(NJ):
                    ins = dve.tensor_reduce(mx3[:, v % 2, j, :], SJ[j], AX.X, ALU.max)
                ins.then_inc(s_maxed, 1)
                dve.wait_ge(s_maxed, m + 1)
                if positive(4 * (m - 1)):
                    dve.wait_ge(p_turned, 4 * (m - 1))
                for j in range(NJ):
                    ins = dve.tensor_tensor(pu3[:, v % 2, :, j, 0:WIDTH[j]], SJ[j], bcast(mx3[:, v % 2, j, :], 2, WIDTH[j]),
                                            ALU.subtract)
                ins.then_inc(s_shifted, 1)

            def norm3(m, v, g):
                dve.wait_ge(p_mixed, 4 * m + 4)
                dve.reciprocal(r3[:, v % 2, :], C3[:, :, HD]).then_inc(c_inv, 1)
                dve.wait_ge(c_inv, m + 1)
                if positive(g - 1):
                    dve.wait_ge(y_made, g - 1)
                dve.tensor_tensor(o3[:, v // 4, v % 4, :, :, :].rearrange("p n e d -> p (n e) d"), C3[:, :, 0:HD],
                                  bcast(r3[:, v % 2, :], 2, HD), ALU.mult).then_inc(c_normed, 1)

            def centre(g, g2, k, src, made, summed, cent):
                dve.wait_ge(made, g + 1)
                y = src[:, g2, :].rearrange("p (a d) -> p a d", d=HD)
                dve.tensor_reduce(st[:, g2, k, 0, :], y, AX.X, ALU.add).then_inc(summed, 1)
                dve.wait_ge(summed, g + 1)
                dve.scalar_tensor_tensor(out=yc[:, g2, k, :].rearrange("p (a d) -> p a d", d=HD), in0=bcast(st[:, g2, k, 0, :], 2, HD),
                                         scalar=-1.0 / HD, in1=y, op0=ALU.mult, op1=ALU.add).then_inc(cent, 1)

            def variance(g, g2, k, sq, var, eps):
                dve.wait_ge(sq, g + 1)
                dve.tensor_reduce(st[:, g2, k, 1, :], ysq[:, g2, k, :].rearrange("p (a d) -> p a d", d=HD), AX.X, ALU.add).then_inc(var, 1)
                dve.wait_ge(var, g + 1)
                dve.tensor_scalar(st[:, g2, k, 2, :], st[:, g2, k, 1, :], 1.0 / HD, EPS_FF, ALU.mult, ALU.add).then_inc(eps, 1)

            def scale(g, g2, k, rstd, mul):
                dve.wait_ge(rstd, g + 1)
                y = yc[:, g2, k, :].rearrange("p (a d) -> p a d", d=HD)
                dve.tensor_tensor(y, y, bcast(st[:, g2, k, 3, :], 2, HD), ALU.mult).then_inc(mul, 1)

            def gate_shift(g, g2):
                dve.wait_ge(r0_gated, g + 1)
                l = gl[:, g2, :].rearrange("p (b c) -> p b c", b=4)
                dve.tensor_tensor(l, R0[0:TP, 0:64].rearrange("p (b c) -> p b c", b=4), bcast(gbb[:, :], 1, 4), ALU.add).then_inc(g_added, 1)
                dve.wait_ge(g_added, g + 1)
                l = gl[:, g2, :].rearrange("p (a e) -> p a e", e=NE)
                dve.tensor_reduce(gm[:, g2, :], l, AX.X, ALU.max).then_inc(g_maxed, 1)
                dve.wait_ge(g_maxed, g + 1)
                dve.tensor_tensor(l, l, bcast(gm[:, g2, :], 2, NE), ALU.subtract).then_inc(g_shifted, 1)

            def gate_sum(g, g2):
                dve.wait_ge(g_exped, g + 1)
                dve.tensor_reduce(gs[:, g2, :], ge[:, g2, :].rearrange("p (a e) -> p a e", e=NE), AX.X, ALU.add).then_inc(g_summed, 1)
                dve.wait_ge(g_summed, g + 1)
                dve.reciprocal(gr[:, g2, :], gs[:, g2, :]).then_inc(g_inv, 1)

            def mask_hidden(g, g2):
                dve.wait_ge(r1_hx, g + 1)
                dve.scalar_tensor_tensor(out=hxm[0:NFEAT, g2, :], in0=fxT[:, g2, :], scalar=0.0, in1=hx[:, g2, :],
                                         op0=ALU.not_equal, op1=ALU.mult).then_inc(h_masked, 1)

            def mask_second(g, g2):
                dve.wait_ge(r1_fc2, g + 1)
                dve.scalar_tensor_tensor(out=ft[:, g2, :], in0=fx[:, g2, :], scalar=0.0, in1=R1[0:TP, 0:256],
                                         op0=ALU.not_equal, op1=ALU.mult).then_inc(t_made, 1)

            def head_shift(g, g2):
                dve.wait_ge(r1_fl, g + 1)
                l = R1[0:TP, 0:16].rearrange("p (b n) -> p b n", b=4)
                dve.tensor_reduce(fm[:, g2, :], l, AX.X, ALU.max).then_inc(fl_maxed, 1)
                dve.wait_ge(fl_maxed, g + 1)
                dve.tensor_tensor(fl[:, g2, :].rearrange("p (b n) -> p b n", b=4), l, bcast(fm[:, g2, :], 2, NH),
                                  ALU.subtract).then_inc(fl_shifted, 1)

            def head_sum(g, g2):
                dve.wait_ge(fl_exped, g + 1)
                dve.tensor_reduce(fs[:, g2, :], fe[:, g2, :].rearrange("p (b n) -> p b n", b=4), AX.X, ALU.add).then_inc(fl_summed, 1)
                dve.wait_ge(fl_summed, g + 1)
                dve.reciprocal(fr[:, g2, :], fs[:, g2, :]).then_inc(fl_inv, 1)

            def experts(q):
                for v in range(V2):
                    m, g, f2 = V2 * q + v, 2 * q + v // 4, (v // 4 + 1) % 2
                    more = exists(g + 1, NQUAD)

                    def rest(s):
                        G, g2 = 2 * q + (v - s) // 4, (v - s) // 4 % 2
                        if (v - s) % 4 or not exists(G, NQUAD):
                            return
                        if s == 7:
                            gate_shift(G, g2)
                        if s == 8:
                            gate_sum(G, g2)
                        if s == 9:
                            centre(G, g2, 0, yy, y_made, y_sum, y_cent)
                        if s == 10:
                            variance(G, g2, 0, y_sq, y_var, y_eps)
                        if s == 12:
                            scale(G, g2, 0, y_rstd, y_mul)
                        if s == 13:
                            mask_hidden(G, g2)
                        if s == 14:
                            mask_second(G, g2)
                        if s == 15:
                            centre(G, g2, 1, ft, z_made, z_sum, z_cent)
                        if s == 16:
                            variance(G, g2, 1, z_sq, z_var, z_eps)
                        if s == 18:
                            scale(G, g2, 1, z_rstd, z_mul)
                        if s == 20:
                            head_shift(G, g2)
                        if s == 21:
                            head_sum(G, g2)

                    if v % 4 == 3 and exists(g + 2, NQUAD):
                        stats3(g + 2)
                    if v % 4 == 0 and more:
                        apply3(g + 1)
                    for s in (21, 18, 12, 8):
                        rest(s)
                    if v % 4 == 2 and more:
                        front_va(g + 1, f2)
                    if exists(m - 2, NBATCH):
                        norm3(m - 2, (v - 2) % V2, 2 * q + (v - 2) // 4)
                    if exists(m, NBATCH):
                        shift3(m, v)
                    for s in (20, 16, 15, 14, 13, 10, 9, 7):
                        rest(s)

            dve.wait_ge(at_added, NBATCH)
            stats3(0)
            apply3(0)
            stats3(1)
            front_va(0, 0)
            experts(0)
            experts(1)
            experts(2)
            experts(3)
            with dve.Fori(4, NBATCH // V2 - 1) as q:
                experts(q)
            for q in range(NBATCH // V2 - 1, NBATCH // V2 + 3):
                experts(q)


_INS = ["x", "L0_tok_w", "L0_tok_b", "L0_attn_Q", "L0_attn_K", "L0_attn_VO", "L0_ffn_hl_w", "L0_ffn_hl_b",
        "L0_ffn_wq", "L0_ffn_wk", "L0_ffn_wv", "L0_ffn_gate_w", "L0_ffn_gate_b", "L0_ffn_ln_g", "L0_ffn_ln_b",
        "L0_ffn_fc1_w", "L0_ffn_fc1_b", "L0_ffn_fc2_w", "L0_ffn_fc2_b", "L0_ffn_fnorm_g", "L0_ffn_fnorm_b",
        "L0_ffn_fgate_w"]


def kernel(**inputs):
    import numpy as np
    import concourse.bacc as bacc
    from concourse.bass_utils import run_bass_kernel_spmd

    nc = bacc.Bacc("TRN2", target_bir_lowering=False, num_devices=1)
    arrays, args = {}, []
    for name in _INS:
        a = np.ascontiguousarray(inputs[name])
        arrays[f"in_{name}"] = a
        args.append(nc.dram_tensor(f"in_{name}", a.shape, mybir.dt.from_np(a.dtype), kind="ExternalInput").ap())
    args.append(nc.dram_tensor("out_h", (NBATCH, NTOK, NFEAT), F32, kind="ExternalOutput").ap())
    audio_tower(nc, *args)
    result = run_bass_kernel_spmd(nc, [arrays], core_ids=[0])
    return result.results[0]["out_h"]
```

```python
from contextlib import ExitStack

import concourse.bass as bass
from concourse import mybir

F32 = mybir.dt.float32
BF16 = mybir.dt.bfloat16
ALU = mybir.AluOpType
ACT = mybir.ActivationFunctionType
AX = mybir.AxisListType

NBATCH, NFEAT, NTIME = 128, 64, 750
KW = 8
NTOK = -(-NTIME // KW)
TP = 96
HEADS, RANK = 8, 32
NH, NE, HD = 4, 4, 16
QB = 32
WIDTH = [QB, 2 * QB, NTOK]
START = [0, QB, 3 * QB]
SROW = START[2] + NTOK
EPS_LN, EPS_FF = 1e-5, 1e-8
MASKED = -1.0e30
FF_LOADS = 16 * (5 * NH + 4 + NH + 6)


def positive(v):
    return not isinstance(v, int) or v > 0


def exists(m, total):
    return not isinstance(m, int) or 0 <= m < total


def bcast(ap, axis, n):
    ap = ap.unsqueeze(axis)
    shape = list(ap.shape)
    shape[axis] = n
    return ap.broadcast_to(shape)


def audio_tower(nc, x, tok_w, tok_b, attn_q, attn_k, attn_vo, hl_w, hl_b, wq, wk, wv, gate_w, gate_b,
                ln_g, ln_b, fc1_w, fc1_b, fc2_w, fc2_b, fnorm_g, fnorm_b, fgate_w, out):
    with ExitStack() as ctx:
        def sb(name, shape, dt=F32):
            return ctx.enter_context(nc.sbuf_tensor(name, shape, dt))

        def sem(name):
            return ctx.enter_context(nc.semaphore(name))

        psum = ctx.enter_context(nc.psum_tensor("psum", [128, 8, 512], F32))

        ident_w = sb("ident_w", [128, 130])
        ident = ident_w[:, 0:128]
        neg_half = sb("neg_half", [TP, 16])
        tokb = sb("tokb", [TP, 1])
        q_w = sb("q_w", [RANK, HEADS, NFEAT])
        k_w = sb("k_w", [RANK, HEADS, NFEAT])
        g_w = sb("g_w", [128, HEADS * NFEAT])
        vo_w = sb("vo_w", [128, HEADS // 2, NFEAT])

        h = sb("h", [TP, NBATCH, NFEAT])

        zeroed = sem("zeroed")
        zeroed2 = sem("zeroed2")
        zeroed3 = sem("zeroed3")
        zeroed4 = sem("zeroed4")
        pool_own = sem("pool_own")
        tok_loaded = sem("tok_loaded")
        attn_loaded = sem("attn_loaded")

        NPAIR = NBATCH // 2
        V1 = 4
        xs = sb("xs", [128, V1, NTOK * KW])
        tok_s = sb("tok_s", [TP, 2, 2 * KW])
        tok_m = sb("tok_m", [TP, 2, 2])
        tok_d = sb("tok_d", [TP, 2, 2 * KW])
        tok_e = sb("tok_e", [TP, 2, 2 * KW])
        tok_l = sb("tok_l", [TP, 2, 2])
        tok_r = sb("tok_r", [TP, V1, 2])
        xw = sb("xw", [TP, 2, KW, 128])
        x_sum = sb("x_sum", [TP, V1, 128])
        x_loaded = [sem(f"x_loaded{i}") for i in range(V1)]
        x_turned = sem("x_turned")
        tok_scored = sem("tok_scored")
        tok_maxed = sem("tok_maxed")
        tok_shifted = sem("tok_shifted")
        tok_exped = sem("tok_exped")
        tok_summed = sem("tok_summed")
        tok_inverted = sem("tok_inverted")
        KD = 6
        x_weighted = sem("x_weighted")
        x_weighted_a = sem("x_weighted_a")
        x_fold = sem("x_fold")
        x_summed = sem("x_summed")
        h_pooled = sem("h_pooled")

        x_pairs = x.rearrange("(p two) f t -> p (two f) t", two=2)

        def turned(v2):
            return psum[0:NTOK, 4 * v2:4 * v2 + 4, :].rearrange("p a (two c) -> p (a two) c", two=2)

        V2 = 8
        NQUAD = NBATCH // 4
        HP = HEADS // 2
        NT = 3
        ln_bn = sb("ln_bn", [TP, 4, 6])
        ln_mv = sb("ln_mv", [TP, 4, 2])
        ln_ve = sb("ln_ve", [TP, 4])
        ln_rs = sb("ln_rs", [TP, 4])
        spot = sb("spot", [1, 1])
        xn = sb("xn", [TP, 2, 4, 2, NFEAT])
        xT = sb("xT", [128, 2, 4, 2, NTOK])
        qs = sb("qs", [128, 2, 4, HP, TP])
        mx = sb("mx", [128, 2, NT, 2])
        pl = sb("pl", [128, 2, NT, 2])
        pr = sb("pr", [128, 4, NT, 2])
        pu = sb("pu", [128, 4, NT, 2, NTOK])
        pT = sb("pT", [NTOK, 2, HP * TP])
        cT = sb("cT", [128, 2, HP, TP])
        ln_stat = sem("ln_stat")
        ln_agg = sem("ln_agg")
        ln_var = sem("ln_var")
        ln_rstd = sem("ln_rstd")
        ln_done = sem("ln_done")
        at_turned = sem("at_turned")
        at_xT = sem("at_xT")
        at_projected = sem("at_projected")
        at_q = sem("at_q")
        at_scored = sem("at_scored")
        at_maxed = sem("at_maxed")
        at_shifted = sem("at_shifted")
        at_exped = sem("at_exped")
        at_summed = sem("at_summed")
        at_inverted = sem("at_inverted")
        at_normed = sem("at_normed")
        at_pturned = sem("at_pturned")
        at_pT = sem("at_pT")
        at_mixed = sem("at_mixed")
        at_cT = sem("at_cT")
        at_out = sem("at_out")
        at_added = sem("at_added")
        g_made = sem("g_made")
        g_ready = sem("g_ready")

        at_Q = psum[:, 0, 0:4 * TP].rearrange("p (b t) -> p b t", b=4)

        def at_S(v):
            s = psum[:, 1 + 2 * (v % 2):3 + 2 * (v % 2), :].rearrange("p a (two c) -> p (a two) c", two=2)
            return s[:, 0:NT, 0:2 * NTOK]

        def at_proj(g, hp):
            bank = hp if isinstance(g, int) and g == 0 else 0
            return psum[:, bank, 0:4 * TP].rearrange("p (b t) -> p b t", b=4)[:, :, 0:NTOK]

        at_P = psum[0:NTOK, 5, 0:NT * 128]
        at_C = psum[:, 6, 0:HP * TP]
        at_O = psum[0:TP, 7, 0:NFEAT]

        NJ = 3
        whl = sb("whl", [HD, NH, NFEAT + 1])
        wq_s = sb("wq_s", [HD, NH, NE, HD])
        wk_s = sb("wk_s", [HD, NH, HD])
        wvT = sb("wvT", [HD, NH, HD])
        m_s = sb("m_s", [HD, NH, NE, HD])
        aq = sb("aq", [NFEAT + 1, NE, NH, 32])
        wsx = sb("wsx", [NFEAT + 1, NH, 32])
        wtok = sb("wtok", [NFEAT + 1, 2, NH, HD])
        gT = sb("gT", [128, 2, NH * NE])
        gbb = sb("gbb", [TP, NH * NE])
        gam = sb("gam", [TP, 2, HD])
        bet = sb("bet", [TP, 2, HD])
        fc1 = sb("fc1", [NFEAT, 128])
        b1 = sb("b1", [NFEAT, 1])
        fc2 = sb("fc2", [NFEAT + 1, NFEAT])
        fgT = sb("fgT", [NFEAT, NH])
        causA = sb("causA", [QB, NE * QB], BF16)
        causB = sb("causB", [QB, NH, QB], BF16)
        l3_bn = sb("l3_bn", [TP, 4, 6])
        l3_mv = sb("l3_mv", [TP, 4, 2])
        l3_ve = sb("l3_ve", [TP, 4])
        l3_rs = sb("l3_rs", [TP, 4])
        xn3 = sb("xn3", [TP, 4, NFEAT])
        x3T = sb("x3T", [NFEAT + 1, 4, TP])
        sxd = sb("sxd", [128, 2, 4, NH, NTOK])
        q3 = sb("q3", [128, 2, 4, NJ, NE, QB])
        va = sb("va", [TP, 2, 4, NH, 32])
        nz = sb("nz", [TP, 2, 4, NH, HD])
        resid = sb("resid", [TP, NH, HD])
        mx3 = sb("mx3", [128, 2, NJ, NH])
        pu3 = sb("pu3", [128, 2, NH, NJ, NTOK])
        ct3 = sb("ct3", [128, NE, TP])
        pT3 = sb("pT3", [NTOK, NH, NE, NJ, QB])
        r3 = sb("r3", [TP, 2, NH * NE])
        o3 = sb("o3", [TP, 2, 4, NH, NE, HD])
        oT = sb("oT", [128, 2, 4, TP])
        gl = sb("gl", [TP, 2, 64])
        ge = sb("ge", [TP, 2, 64])
        gm = sb("gm", [TP, 2, 16])
        gs = sb("gs", [TP, 2, 16])
        gr = sb("gr", [TP, 2, 16])
        yy = sb("yy", [TP, 2, 256])
        st = sb("st", [TP, 2, 2, 4, 16])
        yc = sb("yc", [TP, 2, 2, 256])
        ysq = sb("ysq", [TP, 2, 2, 256])
        fx = sb("fx", [TP, 2, 256])
        fxT = sb("fxT", [NFEAT, 2, 4 * TP])
        hx = sb("hx", [NFEAT, 2, 4 * TP])
        hxm = sb("hxm", [NFEAT + 1, 2, 4 * TP])
        ft = sb("ft", [TP, 2, 256])
        fo = sb("fo", [TP, 2, 256])
        foT = sb("foT", [NFEAT, 2, 4 * TP])
        fl = sb("fl", [TP, 2, 16])
        fe = sb("fe", [TP, 2, 16])
        fm = sb("fm", [TP, 2, 4])
        fs = sb("fs", [TP, 2, 4])
        fr = sb("fr", [TP, 2, 4])
        ho = sb("ho", [TP, 2, 256])
        names3 = """ff_loaded w_made w_read ln3_stat ln3_agg ln3_var ln3_rstd ln3_done f_turned f_xT f_sx f_diag
            f_tok f_va f_q f_qc f_resid s_scored s_maxed s_shifted s_exped p_turned p_copied p_mixed c_copied c_turned c_inv c_normed
            c_guarded r0_turned r0_copied r0_gated g_added g_maxed g_shifted g_exped g_summed g_inv g_gs g_mul g_sum
            y_made y_sum y_cent y_sq y_var y_eps y_rstd y_mul y_gam fx_made r1_fxt r1_fxc r1_fc1 r1_hx h_masked r1_fc2 t_made z_made
            z_sum z_cent z_sq z_var z_eps z_rstd z_mul z_gam fo_made r1_fot r1_foc r1_fl fl_maxed fl_shifted fl_exped
            fl_summed fl_inv fl_w fo_mul ho_made causal_set"""
        S = {n: sem(n) for n in names3.split()}
        (ff_loaded, w_made, w_read, ln3_stat, ln3_agg, ln3_var, ln3_rstd, ln3_done, f_turned, f_xT, f_sx, f_diag,
         f_tok, f_va, f_q, f_qc, f_resid, s_scored, s_maxed, s_shifted, s_exped, p_turned, p_copied, p_mixed, c_copied, c_turned, c_inv, c_normed,
         c_guarded, r0_turned, r0_copied, r0_gated, g_added, g_maxed, g_shifted, g_exped, g_summed, g_inv, g_gs, g_mul, g_sum,
         y_made, y_sum, y_cent, y_sq, y_var, y_eps, y_rstd, y_mul, y_gam, fx_made, r1_fxt, r1_fxc, r1_fc1, r1_hx, h_masked, r1_fc2, t_made, z_made,
         z_sum, z_cent, z_sq, z_var, z_eps, z_rstd, z_mul, z_gam, fo_made, r1_fot, r1_foc, r1_fl, fl_maxed, fl_shifted, fl_exped,
         fl_summed, fl_inv, fl_w, fo_mul, ho_made, causal_set) = S.values()
        out_done = [sem("out_done0"), sem("out_done1")]

        F_ = psum[:, 0, :]

        def front_bank(g, e):
            return psum[:, (e + 1) % 4 if isinstance(g, int) and g == 0 else 0, 0:4 * TP]

        SJ = [psum[:, 2, NH * WIDTH[1]:NH * (WIDTH[1] + WIDTH[0])].rearrange("p (n u) -> p n u", n=NH),
              psum[:, 2, 0:NH * WIDTH[1]].rearrange("p (n u) -> p n u", n=NH),
              psum[:, 1, 0:NH * WIDTH[2]].rearrange("p (n u) -> p n u", n=NH)]
        CT = psum[:, 5, 0:NE * TP]
        C3 = psum[0:TP, 5, :].rearrange("p (e n c) -> p e n c", n=NH, c=32)
        R0, R1 = psum[:, 6, :], psum[:, 7, :]

        def P3(n):
            return psum[0:NTOK, 3 + n % 2, 0:NJ * 128]
        block = ctx.enter_context(nc.Block())

        @block.sync
        def _(sp):
            def load(q, pairs):
                for v in range(V1):
                    if positive(V1 * (q - 1) + v + 1):
                        sp.wait_ge(x_turned, V1 * (q - 1) + v + 1)
                    sp.dma_start(xs[:, v, 0:NTIME], pairs(v)).then_inc(x_loaded[v], 16)

            load(0, lambda v: x_pairs[v])
            sp.dma_start(q_w[:, :, :], attn_q.rearrange("h r d -> r h d")).then_inc(attn_loaded, 16)
            sp.dma_start(k_w[:, :, :], attn_k.rearrange("h r d -> r h d")).then_inc(attn_loaded, 16)
            for par in range(2):
                sp.dma_start(vo_w[64 * par:64 * par + 64, :, :],
                               attn_vo.rearrange("(hp par) d e -> par d hp e", par=2)[par]).then_inc(attn_loaded, 16)
            def slow(dst, src):
                sp.dma_start(dst, src, allow_slow_non_contiguous=True).then_inc(ff_loaded, 16)

            sp.wait_ge(zeroed3, 5)
            for n in range(NH):
                load(1 + n, lambda v: x_pairs[V1 * (1 + n) + v])
                rows = slice(HD * n, HD * n + HD)
                slow(fc1[rows, rows], fc1_w.rearrange("o i -> i o"))
                slow(fc2[rows, rows], fc2_w.rearrange("o i -> i o"))
                slow(fc2[NFEAT:NFEAT + 1, rows], fc2_b.rearrange("(o i) -> o i", o=1))
                slow(b1[rows, :], fc1_b.rearrange("(i o) -> i o", o=1))
                slow(gT[64 * (n % 2):64 * (n % 2) + 64, n // 2, NE * n:NE * n + NE], gate_w[n].rearrange("e f -> f e"))
                slow(wvT[:, n, :], wv[n].rearrange("o d -> d o"))
            load(1 + NH, lambda v: x_pairs[V1 * (1 + NH) + v])
            slow(whl[:, :, 0:NFEAT], hl_w.rearrange("n d h -> d n h"))
            slow(whl[:, :, NFEAT], hl_b.rearrange("n d -> d n"))
            slow(wq_s[:, :, :, :], wq.rearrange("n e o d -> o n e d"))
            slow(wk_s[:, :, :], wk.rearrange("n o d -> o n d"))
            slow(fgT[:, :], fgate_w.rearrange("n f -> f n"))
            load(2 + NH, lambda v: x_pairs[V1 * (2 + NH) + v])
            slow(gbb[:, :], gate_b.rearrange("n e -> (n e)").partition_broadcast(TP))
            slow(gam[:, 0, :], ln_g.partition_broadcast(TP))
            slow(bet[:, 0, :], ln_b.partition_broadcast(TP))
            slow(gam[:, 1, :], fnorm_g.partition_broadcast(TP))
            slow(bet[:, 1, :], fnorm_b.partition_broadcast(TP))
            with sp.Fori(3 + NH, NPAIR // V1) as q:
                load(q, lambda v: x_pairs[bass.ds(q * V1 + v, 1)].rearrange("o q t -> (o q) t"))

            def store(g, g2, quad):
                sp.wait_ge(ho_made, g + 1)
                sp.dma_start(quad.rearrange("b t f -> t b f"),
                             ho[0:NTOK, g2, :].rearrange("t (b f) -> t b f", b=4)).then_inc(out_done[g2], 16)

            with sp.Fori(0, NQUAD // 2) as q:
                for g2 in range(2):
                    store(2 * q + g2, g2, out[bass.ds(8 * q + 4 * g2, 4)])
            for g2 in range(2):
                sp.wait_ge(out_done[g2], 16 * NQUAD // 2)

        @block.gpsimd
        def _(pool):
            pool.memset(ident_w[:, :], 0.0).then_inc(zeroed, 1)
            pool.memset(neg_half[:, :], -0.5).then_inc(zeroed, 1)
            pool.memset(xs[:, :, NTIME:NTOK * KW], 0.0).then_inc(zeroed, 1)
            pool.wait_ge(zeroed, 3)
            pool.dma_start(ident_w[0:NFEAT, 128:129], tok_w.rearrange("o f -> f o")).then_inc(tok_loaded, 16)
            pool.dma_start(ident_w[NFEAT:128, 129:130], tok_w.rearrange("o f -> f o")).then_inc(tok_loaded, 16)
            pool.dma_start(tokb[:, :], tok_b.partition_broadcast(TP)).then_inc(tok_loaded, 16)
            pool.affine_select(out=ident, in_=ident, compare_op=ALU.not_equal, fill=1.0,
                               base=0, pattern=[[-1, 128]], channel_multiplier=1).then_inc(pool_own, 1)
            pool.wait_ge(pool_own, 1)
            pool.memset(h[64:TP, :, :], 0.0).then_inc(zeroed2, 1)
            pool.wait_ge(zeroed2, 4)

            def fold(q, v):
                p, w = V1 * q + v, xw[0:NTOK, v % 2, :, :]
                pool.wait_ge(x_weighted, p + 1)
                pool.wait_ge(x_weighted_a, p + 1)
                pool.tensor_tensor(w[:, 0:4, :], w[:, 0:4, :], w[:, 4:8, :], ALU.add).then_inc(x_fold, 1)

            def tokens(q):
                for v in range(V1):
                    fold(q, v)

            tokens(0)
            with pool.Fori(1, NPAIR // V1) as q:
                tokens(q)

            def ln_power(g):
                pool.wait_ge(ln_var, g + 1)
                if positive(g):
                    pool.wait_ge(ln_done, g)
                pool.tensor_tensor(ln_rs[:, 0:4], ln_ve[:, 0:4], neg_half[:, 0:4], ALU.pow).then_inc(ln_rstd, 1)

            def norm_p(m, v):
                pool.wait_ge(at_inverted, m + 1)
                p = pu[:, v % 4, :, :, :].rearrange("p a b u -> p (a b) u")
                pool.tensor_tensor(p, p, bcast(pr[:, v % 4, :, :].rearrange("p a b -> p (a b)"), 2, NTOK),
                                   ALU.mult).then_inc(at_normed, 1)

            def attention(q):
                for v in range(V2):
                    m, g = V2 * q + v, 2 * q + v // 4
                    if exists(m - 1, NBATCH):
                        norm_p(m - 1, (v - 1) % V2)
                    if v % 4 == 0 and exists(g + 1, NQUAD):
                        ln_power(g + 1)

            ln_power(0)
            pool.memset(causA[:, :], 0.0).then_inc(causal_set, 1)
            pool.memset(causB[:, :, :], 0.0).then_inc(causal_set, 1)
            pool.wait_ge(causal_set, 2)
            cA = causA[:, :].rearrange("p (e t) -> p e t", e=NE)
            pool.affine_select(out=cA, in_=cA, compare_op=ALU.not_equal, fill=1.0, base=0,
                               pattern=[[0, NE], [-1, QB]], channel_multiplier=1).then_inc(causal_set, 1)
            pool.affine_select(out=causB[:, :, :], in_=causB[:, :, :], compare_op=ALU.is_ge, fill=MASKED, base=0,
                               pattern=[[0, NH], [-1, QB]], channel_multiplier=1).then_inc(causal_set, 1)
            pool.wait_ge(causal_set, 4)
            attention(0)
            with pool.Fori(1, NBATCH // V2 - 1) as q:
                attention(q)

            def power3(g):
                pool.wait_ge(ln3_var, g + 1)
                pool.tensor_tensor(l3_rs[:, 0:4], l3_ve[:, 0:4], neg_half[:, 0:4], ALU.pow).then_inc(ln3_rstd, 1)

            def guard(m, v, g):
                pool.wait_ge(c_normed, m + 1)
                pool.wait_ge(f_va, g + 1)
                o = o3[:, v // 4, v % 4, :, :, :]
                pool.tensor_tensor(o, o, bcast(nz[:, v // 4, v % 4, :, :], 2, NE), ALU.mult).then_inc(c_guarded, 1)

            def gates(g, g2):
                pool.wait_ge(g_inv, g + 1)
                e = ge[:, g2, :].rearrange("p (a e) -> p a e", e=NE)
                pool.tensor_tensor(e, e, bcast(gr[:, g2, :], 2, NE), ALU.mult).then_inc(g_gs, 1)
                pool.wait_ge(g_gs, g + 1)
                o = o3[:, g2, :, :, :, :].rearrange("p b n e d -> p (b n e) d")
                pool.tensor_tensor(o, o, bcast(ge[:, g2, :], 2, HD), ALU.mult).then_inc(g_mul, 1)

            def norm_square(g, g2, k, cent, sq):
                pool.wait_ge(cent, g + 1)
                pool.tensor_tensor(ysq[:, g2, k, :], yc[:, g2, k, :], yc[:, g2, k, :], ALU.mult).then_inc(sq, 1)

            def norm_power(g, g2, k, eps, rstd):
                pool.wait_ge(eps, g + 1)
                pool.tensor_tensor(st[:, g2, k, 3, :], st[:, g2, k, 2, :], neg_half[:, :], ALU.pow).then_inc(rstd, 1)

            def norm_affine(g, g2, k, mul, mid, done, dst):
                pool.wait_ge(mul, g + 1)
                y = yc[:, g2, k, :].rearrange("p (a d) -> p a d", d=HD)
                pool.tensor_tensor(y, y, bcast(gam[:, k, :], 1, 16), ALU.mult).then_inc(mid, 1)
                pool.wait_ge(mid, g + 1)
                pool.tensor_tensor(dst[:, g2, :].rearrange("p (a d) -> p a d", d=HD), y, bcast(bet[:, k, :], 1, 16),
                                   ALU.add).then_inc(done, 1)

            def residual(g, g2):
                pool.wait_ge(t_made, g + 1)
                pool.tensor_tensor(ft[:, g2, :], ft[:, g2, :], fx[:, g2, :], ALU.add).then_inc(z_made, 1)

            def finish(g, g2, half):
                pool.wait_ge(fl_inv, g + 1)
                e = fe[:, g2, :].rearrange("p (b n) -> p b n", b=4)
                pool.tensor_tensor(e, e, bcast(fr[:, g2, :], 2, NH), ALU.mult).then_inc(fl_w, 1)
                pool.wait_ge(fl_w, g + 1)
                o = fo[:, g2, :].rearrange("p (a d) -> p a d", d=HD)
                pool.tensor_tensor(o, o, bcast(fe[:, g2, :], 2, HD), ALU.mult).then_inc(fo_mul, 1)
                pool.wait_ge(fo_mul, g + 1)
                if positive(half):
                    pool.wait_ge(out_done[g2], 16 * half)
                pool.tensor_tensor(ho[:, g2, :].rearrange("p (b f) -> p b f", b=4), fo[:, g2, :].rearrange("p (b f) -> p b f", b=4),
                                   h[:, bass.ds(4 * g, 4), :], ALU.add).then_inc(ho_made, 1)

            def experts(q):
                for v in range(V2):
                    m, g = V2 * q + v, 2 * q + v // 4
                    def rest(s):
                        G, g2 = 2 * q + (v - s) // 4, (v - s) // 4 % 2
                        if (v - s) % 4 or not exists(G, NQUAD):
                            return
                        if s == 8:
                            gates(G, g2)
                        if s == 10:
                            norm_square(G, g2, 0, y_cent, y_sq)
                        if s == 11:
                            norm_power(G, g2, 0, y_eps, y_rstd)
                        if s == 12:
                            norm_affine(G, g2, 0, y_mul, y_gam, fx_made, fx)
                        if s == 15:
                            residual(G, g2)
                        if s == 16:
                            norm_square(G, g2, 1, z_cent, z_sq)
                        if s == 17:
                            norm_power(G, g2, 1, z_eps, z_rstd)
                        if s == 18:
                            norm_affine(G, g2, 1, z_mul, z_gam, fo_made, fo)
                        if s == 21:
                            finish(G, g2, q + ((v - s) // 4 - g2) // 2)

                    for s in (15, 10, 16):
                        rest(s)
                    if exists(m - 2, NBATCH):
                        guard(m - 2, (v - 2) % V2, 2 * q + (v - 2) // 4)
                    if v % 4 == 3 and exists(g + 2, NQUAD):
                        power3(g + 2)
                    for s in (12, 18, 21, 8, 11, 17):
                        rest(s)

            power3(0)
            power3(1)
            attention(NBATCH // V2 - 1)
            attention(NBATCH // V2)
            experts(0)
            experts(1)
            experts(2)
            experts(3)
            with pool.Fori(4, NBATCH // V2 - 1) as q:
                experts(q)
            for q in range(NBATCH // V2 - 1, NBATCH // V2 + 3):
                experts(q)

        @block.tensor
        def _(pe):
            def turn(q, v):
                p = V1 * q + v
                pe.wait_ge(x_loaded[v], 16 * q + 16)
                if positive(p - 1):
                    pe.wait_ge(x_weighted, p - 1)
                    pe.wait_ge(x_weighted_a, p - 1)
                for k in range(KW):
                    mm = pe.matmul(turned(v % 2)[:, k, 0:130], xs[:, v, k:NTOK * KW:KW], ident_w[:, :],
                                   start=True, stop=True)
                mm.then_inc(x_turned, 1)

            def tokens(q):
                for v in range(V1):
                    turn(q, v)

            pe.wait_ge(pool_own, 1)
            pe.wait_ge(tok_loaded, 16 * 3)
            tokens(0)
            with pe.Fori(1, NPAIR // V1) as q:
                tokens(q)

            pe.wait_ge(x_weighted, NPAIR - 1)
            pe.wait_ge(x_weighted_a, NPAIR - 1)
            pe.wait_ge(attn_loaded, 16 * 4)
            pe.wait_ge(zeroed2, 4)
            for hd in range(HEADS):
                mm = pe.matmul(psum[0:NFEAT, 0, NFEAT * hd:NFEAT * (hd + 1)], q_w[:, hd, :], k_w[:, hd, :],
                               start=True, stop=True)
            mm.then_inc(g_made, 1)
            pe.wait_ge(ff_loaded, FF_LOADS)
            for n in range(NH):
                for e in range(NE):
                    c = HD * (NE * n + e)
                    mm = pe.matmul(psum[0:HD, 1, c:c + HD], wq_s[:, n, e, :], wk_s[:, n, :], start=True, stop=True)
            mm.then_inc(w_made, 1)
            pe.wait_ge(w_read, 1)
            for n in range(NH):
                pe.matmul(psum[0:NFEAT + 1, 1, 64 * n:64 * n + 64], whl[:, n, :], m_s[:, n, :, :].rearrange("p e d -> p (e d)"),
                          start=True, stop=True)
                pe.matmul(psum[0:NFEAT + 1, 2, HD * n:HD * n + HD], whl[:, n, :], wvT[:, n, :], start=True, stop=True)
                mm = pe.matmul(psum[0:NFEAT + 1, 2, 64 + HD * n:64 + HD * n + HD], whl[:, n, :], ident[0:HD, 0:HD],
                               start=True, stop=True)
            mm.then_inc(w_made, 1)
            pe.wait_ge(w_read, 4)
            pe.wait_ge(g_ready, 1)

            def turn_x(g, g2):
                pe.wait_ge(ln_done, g + 1)
                if positive(4 * g):
                    pe.wait_ge(at_q, 4 * g)
                for b in range(4):
                    mm = pe.transpose(at_Q[:, b, :], xn[:, g2, b, :, :].rearrange("p a f -> p (a f)"), ident[0:TP, 0:TP])
                mm.then_inc(at_turned, 1)

            def project(g, g2, hp):
                if hp == 0:
                    pe.wait_ge(at_xT, g + 1)
                elif positive(g):
                    pe.wait_ge(at_q, 4 * g + hp)
                pe.matmul(at_proj(g, hp), g_w[:, 128 * hp:128 * (hp + 1)], xT[:, g2, :, 0, :],
                          start=True, stop=True).then_inc(at_projected, 1)

            def score(m, g, v):
                b, g2 = v % 4, v // 4
                if b == 0:
                    pe.wait_ge(at_q, 4 * g + 4)
                if positive(m - 1):
                    pe.wait_ge(at_shifted, m - 1)
                q = qs[:, g2, b, :, :].rearrange("p a t -> p (a t)")
                for t in range(NT):
                    mm = pe.matmul(at_S(v)[:, t, :], q[:, 128 * t:128 * (t + 1)],
                                   xT[:, g2, b, :, :].rearrange("p a u -> p (a u)"), start=True, stop=True)
                mm.then_inc(at_scored, 1)

            def turn_p(m, v, par):
                pe.wait_ge(at_normed, m + 1)
                if positive(2 * m + par):
                    pe.wait_ge(at_pT, 2 * m + par)
                for t in range(NT):
                    mm = pe.transpose(at_P[:, 128 * t:128 * (t + 1)], pu[:, v % 4, t, par, :], ident)
                mm.then_inc(at_pturned, 1)

            def mix(m, v, par):
                pe.wait_ge(at_pT, 2 * m + par + 1)
                if par == 0 and positive(m):
                    pe.wait_ge(at_cT, m)
                pe.matmul(at_C[64 * par:64 * par + 64, :], xn[0:NTOK, v // 4, v % 4, 0, :], pT[:, par, :],
                          start=True, stop=True).then_inc(at_mixed, 1)

            def give_out(m, v):
                pe.wait_ge(at_cT, m + 1)
                if positive(m):
                    pe.wait_ge(at_added, m)
                for hp in range(HP):
                    mm = pe.matmul(at_O, cT[:, v % 2, hp, :], vo_w[:, hp, :], start=(hp == 0), stop=(hp == HP - 1))
                mm.then_inc(at_out, 1)

            def attention(q):
                for v in range(V2):
                    m, g, g2 = V2 * q + v, 2 * q + v // 4, (v // 4 + 1) % 2
                    more = exists(g + 1, NQUAD)
                    v2, v3 = (v - 2) % V2, (v - 3) % V2
                    if exists(m - 2, NBATCH):
                        turn_p(m - 2, v2, 0)
                    if v % 4 == 3 and more:
                        project(g + 1, g2, 1)
                    if exists(m, NBATCH):
                        score(m, g, v)
                    if exists(m - 2, NBATCH):
                        turn_p(m - 2, v2, 1)
                    if v % 4 == 2 and more:
                        turn_x(g + 1, g2)
                    if v % 4 == 3 and more:
                        project(g + 1, g2, 2)
                    if exists(m - 3, NBATCH):
                        give_out(m - 3, v3)
                    if v % 4 == 2 and more:
                        project(g + 1, g2, 0)
                    if v % 4 == 3 and more:
                        project(g + 1, g2, 3)
                    if exists(m - 2, NBATCH):
                        mix(m - 2, v2, 0)
                        mix(m - 2, v2, 1)

            turn_x(0, 0)
            for hp in range(HP):
                project(0, 0, hp)
            pe.wait_ge(x_weighted, NPAIR)
            pe.wait_ge(x_weighted_a, NPAIR)
            attention(0)
            with pe.Fori(1, NBATCH // V2 - 1) as q:
                attention(q)

            pe.wait_ge(causal_set, 4)
            def front_turn(g, g2):
                if positive(g):
                    pe.wait_ge(f_qc, 4 * g)
                pe.wait_ge(ln3_done, g + 1)
                pe.transpose(F_[:, 0:TP], xn3[:, 0:2, :].rearrange("p b f -> p (b f)"), ident[0:TP, 0:TP])
                for b in range(1, 4):
                    mm = pe.transpose(F_[0:NFEAT, TP * b:TP * b + TP], xn3[:, b, :], ident[0:TP, 0:TP])
                mm.then_inc(f_turned, 1)

            def front_sx(g, g2):
                pe.wait_ge(f_xT, g + 1)
                pe.matmul(F_[:, 0:4 * TP], wsx[:, :, :].rearrange("p n d -> p (n d)"),
                          x3T[:, :, :].rearrange("p b t -> p (b t)"), start=True, stop=True).then_inc(f_sx, 1)

            def front_tok(g, g2):
                pe.wait_ge(f_diag, g + 1)
                for b in range(4):
                    mm = pe.matmul(F_[0:TP, 128 * b:128 * b + 128], x3T[:, b, :], wtok[:, :, :, :].rearrange("p a n d -> p (a n d)"),
                                   start=True, stop=True)
                mm.then_inc(f_tok, 1)

            def front_q(g, g2, e):
                if isinstance(g, int) and g == 0:
                    if e == 3:
                        pe.wait_ge(f_va, 1)
                elif e == 0:
                    pe.wait_ge(f_va, g + 1)
                else:
                    pe.wait_ge(f_qc, 4 * g + e)
                pe.matmul(front_bank(g, e), aq[:, e, :, :].rearrange("p n d -> p (n d)"),
                          x3T[:, :, :].rearrange("p b t -> p (b t)"), start=True, stop=True).then_inc(f_q, 1)

            def score3(m, g, v):
                b, g2 = v % 4, v // 4
                if b == 0:
                    pe.wait_ge(f_qc, 4 * g + 4)
                if positive(m):
                    pe.wait_ge(s_shifted, m)
                for j, start in ((2, True), (1, True), (0, False)):
                    pe.matmul(SJ[j], q3[:, g2, b, j, :, :].rearrange("p e t -> p (e t)"), sxd[:, g2, b, :, 0:WIDTH[j]],
                              start=start, stop=False, skip_group_check=True)
                for j in range(NJ):
                    w = WIDTH[j] - QB * j
                    mm = pe.matmul(SJ[j][:, :, QB * j:WIDTH[j]], causA[:, :], causB[:, :, 0:w],
                                   start=False, stop=True, skip_group_check=True)
                mm.then_inc(s_scored, 1)

            def turn_p3(m, v, n):
                if n == 0:
                    pe.wait_ge(s_exped, m + 1)
                if positive(4 * m + n - 1):
                    pe.wait_ge(p_copied, 4 * m + n - 1)
                for j in range(NJ):
                    mm = pe.transpose(P3(n)[:, 128 * j:128 * j + 128], pu3[:, v % 2, n, j, :], ident)
                mm.then_inc(p_turned, 1)

            def mix3(m, v):
                pe.wait_ge(p_copied, 4 * m + 4)
                if positive(m):
                    pe.wait_ge(c_normed, m)
                for n in range(NH):
                    mm = pe.matmul(CT[32 * n:32 * n + 32, :], va[0:NTOK, v // 4, v % 4, n, :],
                                   pT3[:, n, :, :, :].rearrange("p e j t -> p (e j t)"), start=True, stop=True)
                mm.then_inc(p_mixed, 1)

            def turn_c(m):
                pe.wait_ge(c_copied, m + 1)
                for e in range(NE):
                    mm = pe.transpose(C3[:, e, :, :].rearrange("p n c -> p (n c)"), ct3[:, e, :], ident)
                mm.then_inc(c_turned, 1)

            def gate_turn(g, g2, half):
                if half == 0:
                    pe.wait_ge(c_guarded, 4 * g + 4)
                    if positive(g):
                        pe.wait_ge(g_added, g)
                else:
                    pe.wait_ge(r0_copied, 2 * g + 1)
                for b in range(2):
                    o = o3[:, g2, 2 * half + b, :, :, :].rearrange("p n e d -> p (n e d)")
                    for hp in range(2):
                        mm = pe.transpose(R0[:, TP * (2 * b + hp):TP * (2 * b + hp + 1)], o[:, 128 * hp:128 * hp + 128],
                                          ident[0:TP, 0:TP])
                mm.then_inc(r0_turned, 1)

            def gate_logits(g, g2):
                pe.wait_ge(r0_copied, 2 * g + 2)
                for b in range(4):
                    for hp in range(2):
                        mm = pe.matmul(R0[0:TP, 16 * b:16 * b + 16], oT[:, b // 2, 2 * (b % 2) + hp, :], gT[:, hp, :],
                                       start=(hp == 0), stop=(hp == 1))
                mm.then_inc(r0_gated, 1)

            def turn_rest(g, g2, src, ready, done):
                pe.wait_ge(ready, g + 1)
                pe.transpose(R1[:, 0:TP], src[:, g2, 0:128], ident[0:TP, 0:TP])
                for b in range(1, 4):
                    mm = pe.transpose(R1[0:NFEAT, TP * b:TP * b + TP], src[:, g2, 64 * b:64 * b + 64], ident[0:TP, 0:TP])
                mm.then_inc(done, 1)

            def layer1(g, g2):
                pe.wait_ge(r1_fxc, g + 1)
                pe.matmul(R1[:, 0:4 * TP], fc1[:, :], fxT[:, g2, :], start=True, stop=True).then_inc(r1_fc1, 1)

            def layer2(g, g2):
                pe.wait_ge(h_masked, g + 1)
                for b in range(4):
                    mm = pe.matmul(R1[0:TP, 64 * b:64 * b + 64], hxm[:, g2, TP * b:TP * b + TP], fc2[:, :],
                                   start=True, stop=True)
                mm.then_inc(r1_fc2, 1)

            def head_logits(g, g2):
                pe.wait_ge(r1_foc, g + 1)
                for b in range(4):
                    mm = pe.matmul(R1[0:TP, 4 * b:4 * b + 4], foT[:, g2, TP * b:TP * b + TP], fgT[:, :],
                                   start=True, stop=True)
                mm.then_inc(r1_fl, 1)

            def experts(q):
                for v in range(V2):
                    m, g, f2 = V2 * q + v, 2 * q + v // 4, (v // 4 + 1) % 2
                    more = exists(g + 1, NQUAD)

                    def rest(s, half=0):
                        G, g2 = 2 * q + (v - s) // 4, (v - s) // 4 % 2
                        if (v - s) % 4 or not exists(G, NQUAD):
                            return
                        if s == 6:
                            gate_turn(G, g2, half)
                        if s == 7:
                            gate_logits(G, g2)
                        if s == 13:
                            if positive(G - 1):
                                pe.wait_ge(fl_shifted, G - 1)
                            turn_rest(G, g2, fx, fx_made, r1_fxt)
                        if s == 14:
                            layer2(G, g2)
                        if s == 19:
                            last = min(G + 2, NQUAD) if isinstance(G, int) else G + 2
                            pe.wait_ge(t_made, last)
                            turn_rest(G, g2, fo, fo_made, r1_fot)
                        if s == 20:
                            head_logits(G, g2)

                    if exists(m - 1, NBATCH):
                        turn_p3(m - 1, (v - 1) % V2, 0)
                        turn_p3(m - 1, (v - 1) % V2, 1)
                    if v % 4 == 1 and more:
                        front_sx(g + 1, f2)
                    if exists(m, NBATCH):
                        score3(m, g, v)
                    if exists(m - 2, NBATCH):
                        turn_c(m - 2)
                    rest(20)
                    rest(13)
                    rest(14)
                    rest(7)
                    rest(6)
                    if exists(m - 1, NBATCH):
                        turn_p3(m - 1, (v - 1) % V2, 2)
                    if v % 4 == 2 and more:
                        front_q(g + 1, f2, 0)
                    if v % 4 == 3 and more:
                        front_q(g + 1, f2, 2)
                    rest(6, 1)
                    G13 = 2 * q + (v - 13) // 4
                    if v % 4 == 1 and exists(G13, NQUAD):
                        layer1(G13, (v - 13) // 4 % 2)
                    if exists(m - 1, NBATCH):
                        turn_p3(m - 1, (v - 1) % V2, 3)
                    if v % 4 == 0 and more:
                        front_turn(g + 1, f2)
                    if v % 4 == 1 and more:
                        front_tok(g + 1, f2)
                    rest(19)
                    if v % 4 == 2 and more:
                        front_q(g + 1, f2, 1)
                    if v % 4 == 3 and more:
                        front_q(g + 1, f2, 3)
                    if exists(m - 1, NBATCH):
                        mix3(m - 1, (v - 1) % V2)

            attention(NBATCH // V2 - 1)
            pe.wait_ge(at_q, HP * NQUAD)
            front_turn(0, 0)
            attention(NBATCH // V2)
            front_sx(0, 0)
            front_tok(0, 0)
            pe.wait_ge(at_shifted, NBATCH)
            for e in range(NE):
                front_q(0, 0, e)
            pe.wait_ge(at_added, NBATCH)
            experts(0)
            experts(1)
            experts(2)
            experts(3)
            with pe.Fori(4, NBATCH // V2 - 1) as q:
                experts(q)
            for q in range(NBATCH // V2 - 1, NBATCH // V2 + 3):
                experts(q)

        @block.scalar
        def _(act):
            def exp_tok(q, v):
                p = V1 * q + v
                act.wait_ge(tok_shifted, p + 1)
                act.activation(tok_e[0:NTOK, v % 2, :], tok_d[0:NTOK, v % 2, :], ACT.Exp).then_inc(tok_exped, 1)

            def weigh(q, v):
                p = V1 * q + v
                act.wait_ge(tok_exped, p + 1)
                if positive(p - 1):
                    act.wait_ge(x_summed, p - 1)
                for k in range(KD, KW):
                    for b in range(2):
                        c = slice(NFEAT * b, NFEAT * b + NFEAT)
                        ins = act.activation(xw[0:NTOK, v % 2, k, c], turned(v % 2)[:, k, c], ACT.Copy,
                                             scale=tok_e[0:NTOK, v % 2, 2 * k + b:2 * k + b + 1])
                ins.then_inc(x_weighted_a, 1)

            def store_h(q, v):
                p = V1 * q + v
                act.wait_ge(x_summed, p + 1)
                act.wait_ge(tok_inverted, p + 1)
                for b in range(2):
                    ins = act.activation(h[0:NTOK, bass.ds(2 * V1 * q + (2 * v + b), 1), :].rearrange("p o f -> p (o f)"),
                                         x_sum[0:NTOK, v, NFEAT * b:NFEAT * (b + 1)], ACT.Copy,
                                         scale=tok_r[0:NTOK, v, b:b + 1])
                ins.then_inc(h_pooled, 1)

            def tokens(q):
                for v in range(V1):
                    exp_tok(q, v)
                    weigh(q, v)
                    if exists(V1 * q + v - 2, NPAIR):
                        store_h(q if v > 1 else q - 1, (v - 2) % V1)

            tokens(0)
            with act.Fori(1, NPAIR // V1) as q:
                tokens(q)

            act.wait_ge(g_made, 1)
            act.activation(g_w[0:NFEAT, :], psum[0:NFEAT, 0, :], ACT.Copy, scale=float(NFEAT) ** -0.5).then_inc(g_ready, 1)
            act.wait_ge(w_made, 1)
            act.activation(m_s[:, :, :, :].rearrange("p n e d -> p (n e d)"), psum[0:HD, 1, 0:256], ACT.Copy,
                           scale=float(HD) ** 0.5).then_inc(w_read, 1)
            act.wait_ge(w_made, 2)
            act.activation(aq[:, :, :, 0:HD].rearrange("p e n d -> p n e d"),
                           psum[0:NFEAT + 1, 1, 0:256].rearrange("p (n e d) -> p n e d", n=NH, e=NE), ACT.Copy).then_inc(w_read, 1)
            act.activation(wtok[:, :, :, :].rearrange("p a n d -> p (a n d)"), psum[0:NFEAT + 1, 2, 0:128], ACT.Copy).then_inc(w_read, 1)
            act.activation(wsx[:, :, 0:HD], psum[0:NFEAT + 1, 2, 64:128].rearrange("p (n d) -> p n d", n=NH), ACT.Copy).then_inc(w_read, 1)

            store_h(NPAIR // V1 - 1, V1 - 2)
            store_h(NPAIR // V1 - 1, V1 - 1)

            def copy_xT(g, g2):
                act.wait_ge(at_turned, g + 1)
                for par in range(2):
                    rows = slice(64 * par, 64 * par + 64)
                    ins = act.activation(xT[rows, g2, :, par, :], at_Q[rows, :, 0:NTOK], ACT.Copy)
                ins.then_inc(at_xT, 1)

            def copy_q(g, g2, hp):
                act.wait_ge(at_projected, 4 * g + hp + 1)
                act.activation(qs[:, g2, :, hp, 0:NTOK], at_proj(g, hp), ACT.Copy).then_inc(at_q, 1)

            def exp_s(m, v):
                act.wait_ge(at_shifted, m + 1)
                p = pu[:, v % 4, :, :, :].rearrange("p a b u -> p (a b u)")
                act.activation(p, p, ACT.Exp).then_inc(at_exped, 1)

            def copy_pT(m, par):
                act.wait_ge(at_pturned, 2 * m + par + 1)
                if positive(2 * m + par - 1):
                    act.wait_ge(at_mixed, 2 * m + par - 1)
                act.activation(pT[:, par, :], at_P, ACT.Copy).then_inc(at_pT, 1)

            def copy_cT(m, v):
                act.wait_ge(at_mixed, 2 * m + 2)
                if positive(m - 1):
                    act.wait_ge(at_out, m - 1)
                act.activation(cT[:, v % 2, :, :].rearrange("p a t -> p (a t)"), at_C, ACT.Copy).then_inc(at_cT, 1)

            def attention(q):
                for v in range(V2):
                    m, g, g2 = V2 * q + v, 2 * q + v // 4, (v // 4 + 1) % 2
                    more = exists(g + 1, NQUAD)
                    if exists(m - 2, NBATCH):
                        copy_pT(m - 2, 0)
                    if exists(m - 3, NBATCH):
                        copy_cT(m - 3, (v - 3) % V2)
                    if v % 4 == 3 and more:
                        copy_q(g + 1, g2, 1)
                    if exists(m - 2, NBATCH):
                        copy_pT(m - 2, 1)
                    if v % 4 == 2 and more:
                        copy_xT(g + 1, g2)
                    if v % 4 == 3 and more:
                        copy_q(g + 1, g2, 2)
                    if v % 4 == 3 and more:
                        copy_q(g + 1, g2, 3)
                    if v % 4 == 2 and more:
                        copy_q(g + 1, g2, 0)
                    if exists(m, NBATCH):
                        exp_s(m, v)

            copy_xT(0, 0)
            for hp in range(HP):
                copy_q(0, 0, hp)
            attention(0)
            with act.Fori(1, NBATCH // V2 - 1) as q:
                attention(q)

            def front_xT(g):
                act.wait_ge(f_turned, g + 1)
                act.activation(x3T[0:NFEAT, :, :].rearrange("p b t -> p (b t)"), F_[0:NFEAT, 0:4 * TP], ACT.Copy).then_inc(f_xT, 1)

            def front_diag(g, g2):
                act.wait_ge(f_sx, g + 1)
                for n in range(NH):
                    rows = slice(32 * n, 32 * n + 32)
                    ins = act.activation(sxd[rows, g2, :, n, :], F_[rows, 0:4 * TP].rearrange("p (b t) -> p b t", b=4)[:, :, 0:NTOK],
                                         ACT.Copy)
                ins.then_inc(f_diag, 1)

            def front_q(g, g2, e):
                act.wait_ge(f_q, 4 * g + e + 1)
                act.activation(q3[:, g2, :, :, e, :], front_bank(g, e).rearrange("p (b j t) -> p b j t", b=4, j=NJ),
                               ACT.Copy).then_inc(f_qc, 1)

            def exp3(m, v):
                act.wait_ge(s_shifted, m + 1)
                for j in range(NJ):
                    p = pu3[:, v % 2, :, j, 0:WIDTH[j]]
                    ins = act.activation(p, p, ACT.Exp)
                ins.then_inc(s_exped, 1)

            def copy_p3(m, n):
                act.wait_ge(p_turned, 4 * m + n + 1)
                if n == 0 and positive(m):
                    act.wait_ge(p_mixed, m)
                act.activation(pT3[:, n, :, :, :].rearrange("p e j t -> p j e t"), P3(n).rearrange("p (j e t) -> p j e t", j=NJ, e=NE),
                               ACT.Copy).then_inc(p_copied, 1)

            def copy_ct(m):
                act.wait_ge(p_mixed, m + 1)
                act.activation(ct3[:, :, :].rearrange("p e t -> p (e t)"), CT, ACT.Copy).then_inc(c_copied, 1)

            def experts(q):
                for v in range(V2):
                    m, g, f2 = V2 * q + v, 2 * q + v // 4, (v // 4 + 1) % 2
                    more = exists(g + 1, NQUAD)

                    def rest(s, half=0):
                        G, g2 = 2 * q + (v - s) // 4, (v - s) // 4 % 2
                        if (v - s) % 4 or not exists(G, NQUAD):
                            return
                        if s == 6:
                            act.wait_ge(r0_turned, 2 * G + half + 1)
                            act.activation(oT[:, half, :, :].rearrange("p a t -> p (a t)"), R0[:, 0:4 * TP],
                                           ACT.Copy).then_inc(r0_copied, 1)
                        if s == 7:
                            act.wait_ge(g_shifted, G + 1)
                            act.activation(ge[:, g2, :], gl[:, g2, :], ACT.Exp).then_inc(g_exped, 1)
                        if s == 13:
                            act.wait_ge(r1_fxt, G + 1)
                            act.activation(fxT[:, g2, :], R1[0:NFEAT, 0:4 * TP], ACT.Copy).then_inc(r1_fxc, 1)
                        if s == 19:
                            act.wait_ge(r1_fot, G + 1)
                            act.activation(foT[:, g2, :], R1[0:NFEAT, 0:4 * TP], ACT.Copy).then_inc(r1_foc, 1)
                        if s == 20:
                            act.wait_ge(fl_shifted, G + 1)
                            act.activation(fe[:, g2, :], fl[:, g2, :], ACT.Exp).then_inc(fl_exped, 1)

                    if exists(m - 2, NBATCH):
                        copy_ct(m - 2)
                    if exists(m - 1, NBATCH):
                        copy_p3(m - 1, 0)
                        copy_p3(m - 1, 1)
                    if v % 4 == 1 and more:
                        front_diag(g + 1, f2)
                    rest(13)
                    rest(6)
                    if exists(m - 1, NBATCH):
                        copy_p3(m - 1, 2)
                    if v % 4 == 2 and more:
                        front_q(g + 1, f2, 0)
                    if v % 4 == 3 and more:
                        front_q(g + 1, f2, 2)
                    rest(6, 1)
                    G13 = 2 * q + (v - 13) // 4
                    if v % 4 == 1 and exists(G13, NQUAD):
                        g2 = (v - 13) // 4 % 2
                        act.wait_ge(r1_fc1, G13 + 1)
                        act.activation(hx[:, g2, :], R1[0:NFEAT, 0:4 * TP], ACT.Relu, bias=b1[:, :]).then_inc(r1_hx, 1)
                    if exists(m - 1, NBATCH):
                        copy_p3(m - 1, 3)
                    if exists(m, NBATCH):
                        exp3(m, v)
                    if v % 4 == 0 and more:
                        front_xT(g + 1)
                    if v % 4 == 2 and more:
                        front_q(g + 1, f2, 1)
                    if v % 4 == 3 and more:
                        front_q(g + 1, f2, 3)
                    rest(19)
                    rest(7)
                    rest(20)

            attention(NBATCH // V2 - 1)
            front_xT(0)
            attention(NBATCH // V2)
            front_diag(0, 0)
            for e in range(NE):
                front_q(0, 0, e)
            experts(0)
            experts(1)
            experts(2)
            experts(3)
            with act.Fori(4, NBATCH // V2 - 1) as q:
                experts(q)
            for q in range(NBATCH // V2 - 1, NBATCH // V2 + 3):
                experts(q)

        @block.vector
        def _(dve):
            def shift_tok(q, v):
                p, v2 = V1 * q + v, v % 2
                dve.wait_ge(x_turned, p + 1)
                s = tok_s[0:NTOK, v2, :].rearrange("p (k b) -> p k b", b=2)
                dve.tensor_scalar(s, turned(v2)[:, :, 128:130], tokb[0:NTOK, :], None, ALU.add).then_inc(tok_scored, 1)
                dve.wait_ge(tok_scored, p + 1)
                dve.tensor_reduce(tok_m[0:NTOK, v2, :], s.rearrange("p k b -> p b k"), AX.X, ALU.max).then_inc(tok_maxed, 1)
                dve.wait_ge(tok_maxed, p + 1)
                dve.tensor_tensor(tok_d[0:NTOK, v2, :].rearrange("p (k b) -> p k b", b=2), s,
                                  bcast(tok_m[0:NTOK, v2, :], 1, KW), ALU.subtract).then_inc(tok_shifted, 1)

            def weigh(q, v):
                p, v2 = V1 * q + v, v % 2
                dve.wait_ge(tok_exped, p + 1)
                e = tok_e[0:NTOK, v2, :]
                dve.tensor_reduce(tok_l[0:NTOK, v2, :], e.rearrange("p (k b) -> p b k", b=2), AX.X,
                                  ALU.add).then_inc(tok_summed, 1)
                if positive(p - 1):
                    dve.wait_ge(x_summed, p - 1)
                dve.tensor_tensor(xw[0:NTOK, v2, 0:KD, :].rearrange("p k (b f) -> p k b f", b=2),
                                  turned(v2)[:, 0:KD, 0:128].rearrange("p k (b f) -> p k b f", b=2),
                                  bcast(e.rearrange("p (k b) -> p k b", b=2)[:, 0:KD, :], 3, NFEAT), ALU.mult).then_inc(x_weighted, 1)
                dve.wait_ge(tok_summed, p + 1)
                if positive(p - 3):
                    dve.wait_ge(h_pooled, p - 3)
                dve.reciprocal(tok_r[0:NTOK, v, :], tok_l[0:NTOK, v2, :]).then_inc(tok_inverted, 1)

            def sum_tok(q, v):
                p, v2 = V1 * q + v, v % 2
                dve.wait_ge(x_fold, p + 1)
                dve.tensor_reduce(x_sum[0:NTOK, v, :], xw[0:NTOK, v2, 0:4, :].rearrange("p k c -> p c k"), AX.X,
                                  ALU.add).then_inc(x_summed, 1)

            def tokens(q):
                for v in range(V1):
                    shift_tok(q, v)
                    if exists(V1 * q + v - 2, NPAIR):
                        sum_tok(q if v > 1 else q - 1, (v - 2) % V1)
                    weigh(q, v)

            dve.memset(xT[:, :, :, :, :], 0.0).then_inc(zeroed2, 1)
            dve.memset(qs[:, :, :, :, NTOK:TP], 0.0).then_inc(zeroed2, 1)
            dve.memset(g_w[64:128, :], 0.0).then_inc(zeroed2, 1)
            dve.memset(gT[:, :, :], 0.0).then_inc(zeroed3, 1)
            dve.memset(fc1[:, :], 0.0).then_inc(zeroed3, 1)
            dve.memset(fc2[:, :], 0.0).then_inc(zeroed3, 1)
            dve.memset(aq[:, :, :, :], 0.0).then_inc(zeroed3, 1)
            dve.memset(wsx[:, :, :], 0.0).then_inc(zeroed3, 1)
            dve.memset(sxd[:, :, :, :, :], 0.0).then_inc(zeroed4, 1)
            dve.memset(pu3[:, :, :, :, :], 0.0).then_inc(zeroed4, 1)
            dve.memset(va[:, :, :, :, HD:32], 1.0).then_inc(zeroed4, 1)
            dve.memset(x3T[NFEAT:NFEAT + 1, :, :], 1.0).then_inc(zeroed4, 1)
            dve.memset(hxm[NFEAT:NFEAT + 1, :, :], 1.0).then_inc(zeroed4, 1)
            dve.wait_ge(tok_loaded, 16 * 3)
            tokens(0)
            with dve.Fori(1, NPAIR // V1) as q:
                tokens(q)

            dve.wait_ge(h_pooled, 2)
            dve.wait_ge(zeroed2, 4)

            def ln_stats(g, part):
                if part == 0:
                    for b in range(4):
                        ins = dve.bn_stats(ln_bn[:, b, :], h[:, bass.ds(4 * g + b, 1), :].rearrange("p o f -> p (o f)"))
                    ins.then_inc(ln_stat, 1)
                else:
                    dve.wait_ge(ln_stat, g + 1)
                    dve.memset(spot[:, :], 0.0)
                    for b in range(4):
                        ins = dve.bn_aggr(ln_mv[:, b, :], ln_bn[:, b, :])
                    ins.then_inc(ln_agg, 1)
                    dve.wait_ge(ln_agg, g + 1)
                    dve.tensor_scalar(ln_ve[:, 0:4], ln_mv[:, 0:4, 1], EPS_LN, None, ALU.add).then_inc(ln_var, 1)

            def ln_apply(g, g2):
                dve.wait_ge(ln_rstd, g + 1)
                if positive(8 * (g - 1)):
                    dve.wait_ge(at_mixed, 8 * (g - 1))
                for b in range(4):
                    ins = dve.tensor_scalar(xn[:, g2, b, :, :], h[:, bass.ds(4 * g + b, 1), :].broadcast_to([TP, 2, NFEAT]),
                                            ln_mv[:, b, 0:1], ln_rs[:, b:b + 1], ALU.subtract, ALU.mult)
                ins.then_inc(ln_done, 1)

            def shift(m, v):
                s = at_S(v).rearrange("p a (b u) -> p a b u", b=2)
                dve.wait_ge(at_scored, m + 1)
                dve.tensor_reduce(mx[:, v % 2, :, :], s, AX.X, ALU.max).then_inc(at_maxed, 1)
                dve.wait_ge(at_maxed, m + 1)
                if positive(2 * (m - 4) + 2):
                    dve.wait_ge(at_pturned, 2 * (m - 4) + 2)
                dve.tensor_tensor(pu[:, v % 4, :, :, :], s, bcast(mx[:, v % 2, :, :], 3, NTOK), ALU.subtract)\
                   .then_inc(at_shifted, 1)

            def sums(m, v):
                dve.wait_ge(at_exped, m + 1)
                dve.tensor_reduce(pl[:, v % 2, :, :], pu[:, v % 4, :, :, :], AX.X, ALU.add).then_inc(at_summed, 1)
                dve.wait_ge(at_summed, m + 1)
                if positive(m - 3):
                    dve.wait_ge(at_normed, m - 3)
                dve.reciprocal(pr[:, v % 4, :, :], pl[:, v % 2, :, :]).then_inc(at_inverted, 1)

            def add_out(m):
                dve.wait_ge(at_out, m + 1)
                hm = h[:, bass.ds(m, 1), :].rearrange("p o f -> p (o f)")
                dve.tensor_tensor(hm, at_O, hm, ALU.add).then_inc(at_added, 1)

            def attention(q):
                for v in range(V2):
                    m, g, g2 = V2 * q + v, 2 * q + v // 4, (v // 4 + 1) % 2
                    more = exists(g + 1, NQUAD)
                    if v % 4 == 2 and more:
                        ln_apply(g + 1, g2)
                    if exists(m - 1, NBATCH):
                        sums(m - 1, (v - 1) % V2)
                    if exists(m, NBATCH):
                        shift(m, v)
                    if v % 4 == 3 and exists(g + 2, NQUAD):
                        ln_stats(g + 2, 0)
                    if v % 4 == 0 and more:
                        ln_stats(g + 1, 1)
                    if exists(m - 3, NBATCH):
                        add_out(m - 3)

            ln_stats(0, 0)
            ln_stats(0, 1)
            sum_tok(NPAIR // V1 - 1, V1 - 2)
            sum_tok(NPAIR // V1 - 1, V1 - 1)
            ln_apply(0, 0)
            dve.wait_ge(h_pooled, NPAIR)
            ln_stats(1, 0)
            attention(0)
            with dve.Fori(1, NBATCH // V2 - 1) as q:
                attention(q)

            dve.wait_ge(ff_loaded, FF_LOADS)

            def stats3(g):
                for b in range(4):
                    ins = dve.bn_stats(l3_bn[:, b, :], h[:, bass.ds(4 * g + b, 1), :].rearrange("p o f -> p (o f)"))
                ins.then_inc(ln3_stat, 1)
                dve.wait_ge(ln3_stat, g + 1)
                dve.memset(spot[:, :], 0.0)
                for b in range(4):
                    ins = dve.bn_aggr(l3_mv[:, b, :], l3_bn[:, b, :])
                ins.then_inc(ln3_agg, 1)
                dve.wait_ge(ln3_agg, g + 1)
                dve.tensor_scalar(l3_ve[:, 0:4], l3_mv[:, 0:4, 1], EPS_LN, None, ALU.add).then_inc(ln3_var, 1)

            def apply3(g):
                dve.wait_ge(ln3_rstd, g + 1)
                if positive(g):
                    dve.wait_ge(f_turned, g)
                for b in range(4):
                    ins = dve.tensor_scalar(xn3[:, b, :], h[:, bass.ds(4 * g + b, 1), :].rearrange("p o f -> p (o f)"),
                                            l3_mv[:, b, 0:1], l3_rs[:, b:b + 1], ALU.subtract, ALU.mult)
                ins.then_inc(ln3_done, 1)

            def front_va(g, g2):
                dve.wait_ge(f_tok, g + 1)
                if positive(4 * (g - 1)):
                    dve.wait_ge(p_mixed, 4 * (g - 1))
                    dve.wait_ge(c_guarded, 4 * (g - 1))
                f = F_[0:TP, :].rearrange("p (b a n d) -> p b a n d", b=4, a=2, n=NH)
                for b in range(4):
                    dve.tensor_copy(va[:, g2, b, :, 0:HD], f[:, b, 0, :, :])
                if isinstance(g, int) and g == 0:
                    for n in range(NH):
                        ins = dve.tensor_copy(resid[:, n, :], f[:, n, 1, n, :])
                    ins.then_inc(f_resid, 1)
                dve.tensor_scalar(nz[:, g2, :, :, :].rearrange("p b n d -> p b (n d)"),
                                  F_[0:TP, :].rearrange("p (b c) -> p b c", b=4)[:, :, 64:128], 0.0, None,
                                  ALU.not_equal).then_inc(f_va, 1)

            def mix_experts(g, g2):
                dve.wait_ge(g_mul, g + 1)
                dve.tensor_reduce(yy[:, g2, :].rearrange("p (a d) -> p a d", d=HD),
                                  o3[:, g2, :, :, :, :].rearrange("p b n e d -> p (b n) d e"), AX.X, ALU.add).then_inc(g_sum, 1)
                dve.wait_ge(g_sum, g + 1)
                y = yy[:, g2, :].rearrange("p (b c) -> p b c", b=4)
                dve.tensor_tensor(y, y, bcast(resid[:, :, :].rearrange("p n d -> p (n d)"), 1, 4), ALU.add).then_inc(y_made, 1)

            def maximum3(m, v):
                dve.wait_ge(s_scored, m + 1)
                for j in range(NJ):
                    ins = dve.tensor_reduce(mx3[:, v % 2, j, :], SJ[j], AX.X, ALU.max)
                ins.then_inc(s_maxed, 1)

            def shift3(m, v):
                dve.wait_ge(s_maxed, m + 1)
                if positive(4 * (m - 1)):
                    dve.wait_ge(p_turned, 4 * (m - 1))
                for j in range(NJ):
                    ins = dve.tensor_tensor(pu3[:, v % 2, :, j, 0:WIDTH[j]], SJ[j], bcast(mx3[:, v % 2, j, :], 2, WIDTH[j]),
                                            ALU.subtract)
                ins.then_inc(s_shifted, 1)

            def invert3(m, v):
                dve.wait_ge(c_turned, m + 1)
                dve.reciprocal(r3[:, v % 2, :].rearrange("p (e n) -> p e n", e=NE), C3[:, :, :, HD]).then_inc(c_inv, 1)

            def norm3(m, v, g):
                dve.wait_ge(c_inv, m + 1)
                if positive(g - 1):
                    dve.wait_ge(y_made, g - 1)
                dve.tensor_tensor(o3[:, v // 4, v % 4, :, :, :].rearrange("p n e d -> p e n d"), C3[:, :, :, 0:HD],
                                  bcast(r3[:, v % 2, :].rearrange("p (e n) -> p e n", e=NE), 3, HD), ALU.mult).then_inc(c_normed, 1)

            def centre(g, g2, k, src, made, summed, cent):
                dve.wait_ge(made, g + 1)
                y = src[:, g2, :].rearrange("p (a d) -> p a d", d=HD)
                dve.tensor_reduce(st[:, g2, k, 0, :], y, AX.X, ALU.add).then_inc(summed, 1)
                dve.wait_ge(summed, g + 1)
                dve.scalar_tensor_tensor(out=yc[:, g2, k, :].rearrange("p (a d) -> p a d", d=HD), in0=bcast(st[:, g2, k, 0, :], 2, HD),
                                         scalar=-1.0 / HD, in1=y, op0=ALU.mult, op1=ALU.add).then_inc(cent, 1)

            def variance(g, g2, k, sq, var, eps):
                dve.wait_ge(sq, g + 1)
                dve.tensor_reduce(st[:, g2, k, 1, :], ysq[:, g2, k, :].rearrange("p (a d) -> p a d", d=HD), AX.X, ALU.add).then_inc(var, 1)
                dve.wait_ge(var, g + 1)
                dve.tensor_scalar(st[:, g2, k, 2, :], st[:, g2, k, 1, :], 1.0 / HD, EPS_FF, ALU.mult, ALU.add).then_inc(eps, 1)

            def scale(g, g2, k, rstd, mul):
                dve.wait_ge(rstd, g + 1)
                y = yc[:, g2, k, :].rearrange("p (a d) -> p a d", d=HD)
                dve.tensor_tensor(y, y, bcast(st[:, g2, k, 3, :], 2, HD), ALU.mult).then_inc(mul, 1)

            def gate_shift(g, g2):
                dve.wait_ge(r0_gated, g + 1)
                l = gl[:, g2, :].rearrange("p (b c) -> p b c", b=4)
                dve.tensor_tensor(l, R0[0:TP, 0:64].rearrange("p (b c) -> p b c", b=4), bcast(gbb[:, :], 1, 4), ALU.add).then_inc(g_added, 1)
                dve.wait_ge(g_added, g + 1)
                l = gl[:, g2, :].rearrange("p (a e) -> p a e", e=NE)
                dve.tensor_reduce(gm[:, g2, :], l, AX.X, ALU.max).then_inc(g_maxed, 1)
                dve.wait_ge(g_maxed, g + 1)
                dve.tensor_tensor(l, l, bcast(gm[:, g2, :], 2, NE), ALU.subtract).then_inc(g_shifted, 1)

            def gate_sum(g, g2):
                dve.wait_ge(g_exped, g + 1)
                dve.tensor_reduce(gs[:, g2, :], ge[:, g2, :].rearrange("p (a e) -> p a e", e=NE), AX.X, ALU.add).then_inc(g_summed, 1)
                dve.wait_ge(g_summed, g + 1)
                dve.reciprocal(gr[:, g2, :], gs[:, g2, :]).then_inc(g_inv, 1)

            def mask_hidden(g, g2):
                dve.wait_ge(r1_hx, g + 1)
                dve.scalar_tensor_tensor(out=hxm[0:NFEAT, g2, :], in0=fxT[:, g2, :], scalar=0.0, in1=hx[:, g2, :],
                                         op0=ALU.not_equal, op1=ALU.mult).then_inc(h_masked, 1)

            def mask_second(g, g2):
                dve.wait_ge(r1_fc2, g + 1)
                dve.scalar_tensor_tensor(out=ft[:, g2, :], in0=fx[:, g2, :], scalar=0.0, in1=R1[0:TP, 0:256],
                                         op0=ALU.not_equal, op1=ALU.mult).then_inc(t_made, 1)

            def head_shift(g, g2):
                dve.wait_ge(r1_fl, g + 1)
                l = R1[0:TP, 0:16].rearrange("p (b n) -> p b n", b=4)
                dve.tensor_reduce(fm[:, g2, :], l, AX.X, ALU.max).then_inc(fl_maxed, 1)
                dve.wait_ge(fl_maxed, g + 1)
                dve.tensor_tensor(fl[:, g2, :].rearrange("p (b n) -> p b n", b=4), l, bcast(fm[:, g2, :], 2, NH),
                                  ALU.subtract).then_inc(fl_shifted, 1)

            def head_sum(g, g2):
                dve.wait_ge(fl_exped, g + 1)
                dve.tensor_reduce(fs[:, g2, :], fe[:, g2, :].rearrange("p (b n) -> p b n", b=4), AX.X, ALU.add).then_inc(fl_summed, 1)
                dve.wait_ge(fl_summed, g + 1)
                dve.reciprocal(fr[:, g2, :], fs[:, g2, :]).then_inc(fl_inv, 1)

            def experts(q):
                for v in range(V2):
                    m, g, f2 = V2 * q + v, 2 * q + v // 4, (v // 4 + 1) % 2
                    more = exists(g + 1, NQUAD)

                    def rest(s):
                        G, g2 = 2 * q + (v - s) // 4, (v - s) // 4 % 2
                        if (v - s) % 4 or not exists(G, NQUAD):
                            return
                        if s == 7:
                            gate_shift(G, g2)
                        if s == 8:
                            gate_sum(G, g2)
                        if s == 9:
                            mix_experts(G, g2)
                            centre(G, g2, 0, yy, y_made, y_sum, y_cent)
                        if s == 10:
                            variance(G, g2, 0, y_sq, y_var, y_eps)
                        if s == 12:
                            scale(G, g2, 0, y_rstd, y_mul)
                        if s == 13:
                            mask_hidden(G, g2)
                        if s == 14:
                            mask_second(G, g2)
                        if s == 15:
                            centre(G, g2, 1, ft, z_made, z_sum, z_cent)
                        if s == 16:
                            variance(G, g2, 1, z_sq, z_var, z_eps)
                        if s == 18:
                            scale(G, g2, 1, z_rstd, z_mul)
                        if s == 20:
                            head_shift(G, g2)
                        if s == 21:
                            head_sum(G, g2)

                    if v % 4 == 0 and more:
                        apply3(g + 1)
                    if v % 4 == 2 and more:
                        front_va(g + 1, f2)
                    if exists(m, NBATCH):
                        maximum3(m, v)
                    if exists(m - 2, NBATCH):
                        invert3(m - 2, (v - 2) % V2)
                    if exists(m, NBATCH):
                        shift3(m, v)
                    if exists(m - 2, NBATCH):
                        norm3(m - 2, (v - 2) % V2, 2 * q + (v - 2) // 4)
                    if v % 4 == 3 and exists(g + 2, NQUAD):
                        stats3(g + 2)
                    for s in (8, 21, 20, 14, 13, 7, 18, 12, 16, 15, 10, 9):
                        rest(s)

            dve.wait_ge(at_added, 8)
            stats3(0)
            apply3(0)
            stats3(1)
            attention(NBATCH // V2 - 1)
            attention(NBATCH // V2)
            dve.wait_ge(at_added, NBATCH)
            front_va(0, 0)
            experts(0)
            experts(1)
            experts(2)
            experts(3)
            with dve.Fori(4, NBATCH // V2 - 1) as q:
                experts(q)
            for q in range(NBATCH // V2 - 1, NBATCH // V2 + 3):
                experts(q)


_INS = ["x", "L0_tok_w", "L0_tok_b", "L0_attn_Q", "L0_attn_K", "L0_attn_VO", "L0_ffn_hl_w", "L0_ffn_hl_b",
        "L0_ffn_wq", "L0_ffn_wk", "L0_ffn_wv", "L0_ffn_gate_w", "L0_ffn_gate_b", "L0_ffn_ln_g", "L0_ffn_ln_b",
        "L0_ffn_fc1_w", "L0_ffn_fc1_b", "L0_ffn_fc2_w", "L0_ffn_fc2_b", "L0_ffn_fnorm_g", "L0_ffn_fnorm_b",
        "L0_ffn_fgate_w"]


def kernel(**inputs):
    import numpy as np
    import concourse.bacc as bacc
    from concourse.bass_utils import run_bass_kernel_spmd

    nc = bacc.Bacc("TRN2", target_bir_lowering=False, num_devices=1)
    arrays, args = {}, []
    for name in _INS:
        a = np.ascontiguousarray(inputs[name])
        arrays[f"in_{name}"] = a
        args.append(nc.dram_tensor(f"in_{name}", a.shape, mybir.dt.from_np(a.dtype), kind="ExternalInput").ap())
    args.append(nc.dram_tensor("out_h", (NBATCH, NTOK, NFEAT), F32, kind="ExternalOutput").ap())
    audio_tower(nc, *args)
    result = run_bass_kernel_spmd(nc, [arrays], core_ids=[0])
    return result.results[0]["out_h"]
```
